# Optimizing a Trainium2 kernel written in Bass

```python
import numpy as np
import jax
import jax.numpy as jnp

def _softmax(x, axis=-1):
    return jax.nn.softmax(x, axis=axis)

def _gelu(x):
    return jax.nn.gelu(x, approximate=True)

def _silu(x):
    return jax.nn.silu(x)

def _sigmoid(x):
    return jax.nn.sigmoid(x)

def _layernorm(x, axis=-1, eps=1e-05):
    m = jnp.mean(x, axis=axis, keepdims=True)
    v = jnp.var(x, axis=axis, keepdims=True)
    return (x - m) / jnp.sqrt(v + eps)

def _scatter_add(tgt, idx, src, axis=0):
    return tgt.at[idx].add(src)

def _segment_sum(src, seg, n):
    return jax.ops.segment_sum(src, seg, n)
kernel_name = 'mk_gnn_ffn_d1_gnn_r8_c30e21'

def setup_inputs(seed: int=0):
    np.random.seed(seed)
    _w = jnp.asarray

    def _rec_inputs():
        import jax
        import jax.numpy as jnp
        _gk = jax.random.key(seed)
        x = -0.0002117 + 1 * jax.random.normal(jax.random.fold_in(_gk, 1), (6250, 256), jnp.float32)
        src = jax.random.randint(jax.random.fold_in(_gk, 2), (200000,), 0, 6250, jnp.int32)
        dst = jax.random.randint(jax.random.fold_in(_gk, 3), (200000,), 0, 6250, jnp.int32)
        _o = jnp.argsort(dst, stable=True)
        src = src[_o]
        dst = dst[_o]
        return (x, src, dst)
    x, src, dst = _rec_inputs()

    def _L0_gnn_setup():
        import jax, jax.numpy as jnp
        import numpy as np
        N_NODES = 12500
        N_EDGES = 200000
        IN_DIM = 256
        OUT_DIM = 256
        key = jax.random.key(seed)
        k1, k2, k3 = jax.random.split(key, 3)
        x = jax.random.normal(k1, (N_NODES, IN_DIM), dtype=jnp.float32)
        limit = 0.1 * np.sqrt(6.0 / (IN_DIM + OUT_DIM))
        W = jax.random.uniform(k2, (OUT_DIM, IN_DIM), dtype=jnp.float32, minval=-limit, maxval=limit)
        b = jnp.zeros((OUT_DIM,), dtype=jnp.float32)
        edge_index = jax.random.randint(k3, (2, N_EDGES), 0, N_NODES, dtype=jnp.int64)
        return {'x': x, 'W': W, 'b': b, 'edge_index': edge_index}
    _L0_gnn_all = _L0_gnn_setup()
    _L0_gnn_in = {k: v for k, v in _L0_gnn_all.items() if k in ('W', 'b')}
    del _L0_gnn_all

    def _L0_ffn_setup():
        import jax, jax.numpy as jnp
        import numpy as np
        B, N, D = (16, 512, 256)
        NUM_EXPERTS, TOP_K, HEADS = (4, 2, 4)
        N_EDGES = 131072
        LN_EPS = 1e-05

        def _layernorm(x, g, b):
            mu = x.mean(-1, keepdims=True)
            var = ((x - mu) ** 2).mean(-1, keepdims=True)
            return (x - mu) * jax.lax.rsqrt(var + LN_EPS) * g + b

        def _forward(x, edge_index, W_gat, att_src, att_dst, b_gat, ln_gamma, ln_beta, W1, b1, W2, b2):
            Bc, Nc, Dc = x.shape
            M = Bc * Nc
            x_flat = x.reshape(M, Dc)
            h = (x_flat @ W_gat).reshape(M, HEADS, NUM_EXPERTS)
            loops = jnp.arange(M, dtype=edge_index.dtype)
            src = jnp.concatenate([edge_index[0], loops])
            dst = jnp.concatenate([edge_index[1], loops])
            a_src = (h * att_src).sum(-1)
            a_dst = (h * att_dst).sum(-1)
            e = jax.nn.leaky_relu(a_src[src] + a_dst[dst], negative_slope=0.2)
            e_max = jax.ops.segment_max(e, dst, num_segments=M)
            ee = jnp.exp(e - e_max[dst])
            denom = jax.ops.segment_sum(ee, dst, num_segments=M)
            alpha = ee / (denom[dst] + 1e-16)
            msg = h[src] * alpha[:, :, None]
            agg = jax.ops.segment_sum(msg, dst, num_segments=M).reshape(M, HEADS * NUM_EXPERTS) + b_gat
            scores = _layernorm(agg, ln_gamma, ln_beta).reshape(M, HEADS, NUM_EXPERTS).mean(1)
            scores = scores.reshape(Bc, Nc, NUM_EXPERTS)
            topk_s, topk_i = jax.lax.top_k(scores, TOP_K)
            w = jax.nn.softmax(topk_s, axis=-1)
            out = jnp.zeros_like(x)
            for ei in range(NUM_EXPERTS):
                g = jnp.where(topk_i == ei, w, 0.0).sum(-1)
                hh = jax.nn.gelu(x @ W1[ei] + b1[ei], approximate=False)
                out = out + g[..., None] * (hh @ W2[ei] + b2[ei])
            return out
        key = jax.random.key(seed)
        ks = jax.random.split(key, 8)
        s = 0.05
        return {'x': jax.random.normal(ks[0], (B, N, D), jnp.float32), 'W_gat': jax.random.normal(ks[1], (D, HEADS * NUM_EXPERTS), jnp.float32) * s, 'att_src': jax.random.normal(ks[2], (HEADS, NUM_EXPERTS), jnp.float32) * s, 'att_dst': jax.random.normal(ks[3], (HEADS, NUM_EXPERTS), jnp.float32) * s, 'b_gat': jnp.zeros((HEADS * NUM_EXPERTS,), jnp.float32), 'ln_gamma': jnp.ones((HEADS * NUM_EXPERTS,), jnp.float32), 'ln_beta': jnp.zeros((HEADS * NUM_EXPERTS,), jnp.float32), 'W1': jax.random.normal(ks[4], (NUM_EXPERTS, D, 2 * D), jnp.float32) * s, 'b1': jnp.zeros((NUM_EXPERTS, 2 * D), jnp.float32), 'W2': jax.random.normal(ks[5], (NUM_EXPERTS, 2 * D, D), jnp.float32) * s, 'b2': jnp.zeros((NUM_EXPERTS, D), jnp.float32), 'edge_index': jax.random.randint(ks[6], (2, N_EDGES), 0, B * N, jnp.int32)}
    _L0_ffn_all = _L0_ffn_setup()
    _L0_ffn_in = {k: v for k, v in _L0_ffn_all.items() if k in ('W_gat', 'att_src', 'att_dst', 'b_gat', 'ln_gamma', 'ln_beta', 'W1', 'b1', 'W2', 'b2', 'edge_index')}
    del _L0_ffn_all
    return {'x': x, 'src': src, 'dst': dst, 'L0_gnn_W': _L0_gnn_in['W'], 'L0_gnn_b': _L0_gnn_in['b'], 'L0_ffn_W_gat': _L0_ffn_in['W_gat'], 'L0_ffn_att_src': _L0_ffn_in['att_src'], 'L0_ffn_att_dst': _L0_ffn_in['att_dst'], 'L0_ffn_b_gat': _L0_ffn_in['b_gat'], 'L0_ffn_ln_gamma': _L0_ffn_in['ln_gamma'], 'L0_ffn_ln_beta': _L0_ffn_in['ln_beta'], 'L0_ffn_W1': _L0_ffn_in['W1'], 'L0_ffn_b1': _L0_ffn_in['b1'], 'L0_ffn_W2': _L0_ffn_in['W2'], 'L0_ffn_b2': _L0_ffn_in['b2'], 'L0_ffn_edge_index': _L0_ffn_in['edge_index']}

def reference(x, src, dst, L0_gnn_W, L0_gnn_b, L0_ffn_W_gat, L0_ffn_att_src, L0_ffn_att_dst, L0_ffn_b_gat, L0_ffn_ln_gamma, L0_ffn_ln_beta, L0_ffn_W1, L0_ffn_b1, L0_ffn_W2, L0_ffn_b2, L0_ffn_edge_index):
    import jax
    import jax.numpy as jnp

    def _L0_gnn_ref(x, W, b, edge_index):
        import jax, jax.numpy as jnp
        import numpy as np
        N_NODES = 12500
        N_EDGES = 200000
        IN_DIM = 256
        OUT_DIM = 256
        num_nodes = x.shape[0]
        src, tgt = (edge_index[0], edge_index[1])
        xt = jnp.einsum('ni,oi->no', x, W) + b
        out = jax.ops.segment_sum(xt[src], tgt, num_segments=num_nodes)
        deg = jax.ops.segment_sum(jnp.ones_like(tgt, dtype=x.dtype), tgt, num_segments=num_nodes)
        out = out / (deg + 1.0)[:, None]
        return out

    def _L0_ffn_ref(x, W_gat, att_src, att_dst, b_gat, ln_gamma, ln_beta, W1, b1, W2, b2, edge_index):
        import jax, jax.numpy as jnp
        import numpy as np
        B, N, D = (16, 512, 256)
        NUM_EXPERTS, TOP_K, HEADS = (4, 2, 4)
        N_EDGES = 131072
        LN_EPS = 1e-05

        def _layernorm(x, g, b):
            mu = x.mean(-1, keepdims=True)
            var = ((x - mu) ** 2).mean(-1, keepdims=True)
            return (x - mu) * jax.lax.rsqrt(var + LN_EPS) * g + b

        def _forward(x, edge_index, W_gat, att_src, att_dst, b_gat, ln_gamma, ln_beta, W1, b1, W2, b2):
            Bc, Nc, Dc = x.shape
            M = Bc * Nc
            x_flat = x.reshape(M, Dc)
            h = (x_flat @ W_gat).reshape(M, HEADS, NUM_EXPERTS)
            loops = jnp.arange(M, dtype=edge_index.dtype)
            src = jnp.concatenate([edge_index[0], loops])
            dst = jnp.concatenate([edge_index[1], loops])
            a_src = (h * att_src).sum(-1)
            a_dst = (h * att_dst).sum(-1)
            e = jax.nn.leaky_relu(a_src[src] + a_dst[dst], negative_slope=0.2)
            e_max = jax.ops.segment_max(e, dst, num_segments=M)
            ee = jnp.exp(e - e_max[dst])
            denom = jax.ops.segment_sum(ee, dst, num_segments=M)
            alpha = ee / (denom[dst] + 1e-16)
            msg = h[src] * alpha[:, :, None]
            agg = jax.ops.segment_sum(msg, dst, num_segments=M).reshape(M, HEADS * NUM_EXPERTS) + b_gat
            scores = _layernorm(agg, ln_gamma, ln_beta).reshape(M, HEADS, NUM_EXPERTS).mean(1)
            scores = scores.reshape(Bc, Nc, NUM_EXPERTS)
            topk_s, topk_i = jax.lax.top_k(scores, TOP_K)
            w = jax.nn.softmax(topk_s, axis=-1)
            out = jnp.zeros_like(x)
            for ei in range(NUM_EXPERTS):
                g = jnp.where(topk_i == ei, w, 0.0).sum(-1)
                hh = jax.nn.gelu(x @ W1[ei] + b1[ei], approximate=False)
                out = out + g[..., None] * (hh @ W2[ei] + b2[ei])
            return out
        return _forward(x, edge_index, W_gat, att_src, att_dst, b_gat, ln_gamma, ln_beta, W1, b1, W2, b2)
    edge_index = jnp.stack([src, dst])
    x = x + _L0_gnn_ref(_layernorm(x, axis=-1), L0_gnn_W, L0_gnn_b, edge_index)
    x = x + _L0_ffn_ref(_layernorm(x, axis=-1)[None], L0_ffn_W_gat, L0_ffn_att_src, L0_ffn_att_dst, L0_ffn_b_gat, L0_ffn_ln_gamma, L0_ffn_ln_beta, L0_ffn_W1, L0_ffn_b1, L0_ffn_W2, L0_ffn_b2, L0_ffn_edge_index)[0]
    return x

_drawn_inputs = setup_inputs


def setup_inputs(seed=0):
    import zlib

    import numpy as np

    out = dict(_drawn_inputs(seed))
    spreads = {'L0_gnn_b': (0.0, 0.1),
     'L0_ffn_b_gat': (0.0, 0.1),
     'L0_ffn_ln_gamma': (1.0, 0.2),
     'L0_ffn_ln_beta': (0.0, 0.1),
     'L0_ffn_b1': (0.0, 0.1),
     'L0_ffn_b2': (0.0, 0.1)}
    factors = {}
    for name, (base, spread) in spreads.items():
        noise = np.random.default_rng([zlib.crc32(name.encode()), seed]).standard_normal(out[name].shape)
        drawn = base * np.exp(spread * noise) if base else spread * noise
        out[name] = jnp.asarray(drawn.astype(out[name].dtype))
    for name, factor in factors.items():
        out[name] = (out[name] * factor).astype(out[name].dtype)
    return out
```

```python
from contextlib import ExitStack, contextmanager

import numpy as np

import concourse.bass as bass
from concourse import mybir

F32 = mybir.dt.float32
F16 = mybir.dt.float16
I32 = mybir.dt.int32
ALU = mybir.AluOpType
ACT = mybir.ActivationFunctionType
AX = mybir.AxisListType
RED = bass.bass_isa.ReduceOp
ds = bass.ds

P = 128
D = 256
EPS = 1e-5

CH = 16
GROUP = CH * P
AGW = D + 1
TAB_SCALE = 1024.0

HEADS, NX = 4, 4
HX = HEADS * NX
LO = 512
NJ = LO // P
BC = 8
ROWW = HEADS + HEADS * (1 + NX)
VAL = HEADS * (1 + NX)
LEVEL = 8.0
DEN_SCALE = 4096.0
FULL = 16384.0
BIG = 1e30
HID = 512


class Chain:

    def __init__(self, eng, sem):
        self.eng, self.sem, self.base, self.n = eng, sem, 0, 0

    def link(self, *instructions):
        instructions[-1].then_inc(self.sem, 1)
        self.n += 1
        self.eng.wait_ge(self.sem, self.base + self.n)

    @contextmanager
    def loop(self, count, steps):
        base, n = self.base, self.n
        with self.eng.Fori(0, count) as i:
            self.base, self.n = i * steps + (base + n), 0
            yield i
            assert self.n == steps, (self.n, steps)
        self.base, self.n = base, n + count * steps


def gnn_moe(nc, x, src, dst, W, b, W_gat, att_src, att_dst, b_gat, ln_g, ln_b, W1, b1, W2, b2, edges, out):
    N = x.shape[0]
    NT = -(-N // P)
    LAST = N - (NT - 1) * P
    NE = src.shape[0]
    NG = -(-NE // GROUP)
    TAIL = NE - (NG - 1) * GROUP
    NA = edges.shape[1]
    NB = NA // (BC * P)
    NHI = -(-N // LO)
    NTP = NHI * NJ
    HIV = NHI * VAL
    NE_X = W1.shape[0]
    PADN = NT * P - 1
    LOB_LEVEL = 16 * (NB // 2 + 1)
    ROWS_LEVEL = 16 * BC * NB // 2
    BT = 7
    assert NT % BT == 0 and NG % 2 == 0 and NB % 2 == 0 and NA % (BC * P) == 0
    BATCHES = ((0, 4), (4, 3))

    table = nc.dram_tensor("ln_table", (NT * P, 2 * D), F16, kind="Internal").ap()
    lo_rows = nc.dram_tensor("lo_rows", (NB + 2, BC * P), F16, kind="Internal").ap()
    atable = nc.dram_tensor("att_table", (NTP * P, ROWW), F32, kind="Internal").ap()

    with ExitStack() as ctx:
        def sb(name, shape, dt, where=ctx):
            return where.enter_context(nc.sbuf_tensor(name, shape, dt))

        def sem(name):
            return ctx.enter_context(nc.semaphore(name))

        X = sb("X", [P, NT * D], F32)
        AG = sb("AG", [P, (NT + 1) * AGW], F32)
        identf = sb("identf", [P, P], F32)
        identh = sb("identh", [P, P], F16)
        H = sb("H", [P, NTP, HX], F32)
        acc = sb("acc", [P, NTP, VAL], F32)
        sc = sb("sc", [P, 16], F32)
        lohi = sb("lohi", [P, NB + 1, 2, BC], F32)
        asrc_idx = sb("asrc_idx", [P, NB + 2, BC], I32)
        iota_lo = sb("iota_lo", [P, LO], F16)
        minus_node = sb("minus_node", [P, NJ], F32)
        consts = sb("consts", [P, 8], F32)
        W_sb = sb("W_sb", [P, 2, D], F32)
        WT = sb("WT", [P, 2, D], F32)
        Wg = sb("Wg", [P, 2, HX], F32)
        b_bc = sb("b_bc", [P, D], F32)
        small = sb("small", [P, 5, HX], F32)
        stats = sb("stats", [P, BT, 6], F32)
        mv = sb("mv", [P, BT, 2], F32)
        std = sb("std", [P, BT], F32)
        rstd = sb("rstd", [P, BT], F32)
        shift = sb("shift", [P, BT], F32)
        scratch = nc.sbuf_base

        g1 = ExitStack()
        ring = sb("ring", [P, 2 * CH, 2 * D + 2], F16, g1)
        OH = sb("OH", [P, CH, 2 * P], F16, g1)
        drel_all = sb("drel_all", [P, NG * CH], F32, g1)
        sidx_all = sb("sidx_all", [P, NG * CH], I32, g1)
        drelw = sb("drelw", [P, CH], F32, g1)
        sstage = sb("sstage", [P, 2 * CH], I32, g1)
        info = sb("info", [1, 4 * NG], I32, g1)
        cols = sb("cols", [P, 16], I32, g1)
        colf = sb("colf", [P, 16], F32, g1)
        tri = sb("tri", [P, NG + 1], F32, g1)
        nat = ring[:, :, :].rearrange("p a b -> p (a b)").bitcast(F32)
        srcf = nat[0:NG, 0:GROUP]
        dstf = nat[0:NG, GROUP:2 * GROUP]
        srcn = nat[:, 2 * GROUP:3 * GROUP].bitcast(I32)
        dstn = nat[:, 3 * GROUP:4 * GROUP].bitcast(I32)
        tstage = sb("tstage", [P, BT, 2 * D], F16, g1)
        xs = sb("xs", [P, BT, D], F32, g1)
        g1.close()

        g2 = ExitStack()
        y = sb("y", [P, BT, D], F32, g2)
        yT = sb("yT", [P, BT, 2, P], F32, g2)
        xnb = sb("xnb", [P, BT, D], F32, g2)
        xT = sb("xT", [P, BT, 2, P], F32, g2)
        dgs = sb("dgs", [P, 4, BT], F32, g2)
        g2.close()

        g3 = ExitStack()
        S = sb("S", [P, 2, BC, LO], F16, g3)
        lob = sb("lob", [P, 2, BC * P], F16, g3)
        ST = sb("ST", [P, 2, NJ, BC * P], F16, g3)
        Hm = sb("Hm", [P, BC, HIV], F16, g3)
        M = sb("M", [P, 2, BC, 2 * HIV], F16, g3)
        iota_hi = sb("iota_hi", [P, HIV], F16, g3)
        zero_l = sb("zero_l", [P, P], F16, g3)
        rows = sb("rows", [P, 2, BC, ROWW], F32, g3)
        estage = sb("estage", [P, 2, 2 * BC], F32, g3)
        istage = sb("istage", [P, 2 * BC], I32, g3)
        sel = sb("sel", [P, BC, HEADS, NHI], F32, g3)
        adu = sb("adu", [P, BC, HEADS], F32, g3)
        ez = sb("ez", [P, BC, HEADS], F32, g3)
        ez2 = sb("ez2", [P, BC, HEADS], F32, g3)
        er = sb("er", [P, BC, HEADS], F32, g3)
        er2 = sb("er2", [P, BC, HEADS], F32, g3)
        wexp = sb("wexp", [P, BC, HEADS], F32, g3)
        val = sb("val", [P, BC, VAL], F32, g3)
        vh = sb("vh", [P, BC, 2, VAL], F16, g3)
        Tad = sb("Tad", [P, 2, NJ, NHI, HEADS], F16, g3)
        AS = sb("AS", [P, NTP, HEADS], F32, g3)
        AD = sb("AD", [P, NTP, HEADS], F32, g3)
        ADs = sb("ADs", [P, NTP, HEADS], F32, g3)
        NTB = sb("NTB", [P, NTP, ROWW], F32, g3)
        n1 = sb("n1", [P, NTP, HEADS], F32, g3)
        n2 = sb("n2", [P, NTP, HEADS], F32, g3)
        n3 = sb("n3", [P, NTP, HEADS], F32, g3)
        n4 = sb("n4", [P, NTP, HEADS], F32, g3)
        Rsh = sb("Rsh", [P, NTP, HEADS], F32, g3)
        ext = sb("ext", [P, 16], F32, g3)
        extr = sb("extr", [P, 16], F32, g3)
        Gk = sb("Gk", [P, HEADS], F32, g3)
        Gk1 = sb("Gk1", [P, HEADS], F32, g3)
        nlev = sb("nlev", [P, 1], I32, g3)
        g3.close()
        SF = S[:, :, :, :].rearrange("p a r n -> p (a r n)").bitcast(F32)
        L = SF[:, 0:NTP * VAL].rearrange("p (t f) -> p t f", f=VAL)
        tmp16 = SF[:, NTP * VAL:2 * NTP * VAL].rearrange("p (t f) -> p t f", f=VAL)

        g4 = ExitStack()
        W1_sb = sb("W1_sb", [P, 2, NE_X, HID], F32, g4)
        W2_sb = sb("W2_sb", [P, NE_X, HID // P, D], F32, g4)
        b1n = sb("b1n", [NE_X * HID // P, P], F32, g4)
        b1T = sb("b1T", [P, NE_X * HID // P], F32, g4)
        b2r = sb("b2r", [1, NE_X * D], F32, g4)
        ones1 = sb("ones1", [1, P], F32, g4)
        hh = sb("hh", [P, 2, HID // P, LO], F32, g4)
        gate = sb("gate", [P, NT * NX], F32, g4)
        A16 = sb("A16", [P, NTP, HX], F32, g4)
        B16 = sb("B16", [P, NTP, HX], F32, g4)
        m1 = sb("m1", [P, NTP], F32, g4)
        m2 = sb("m2", [P, NTP], F32, g4)
        m3 = sb("m3", [P, NTP], F32, g4)
        scr4 = sb("scr4", [P, NTP, NX], F32, g4)
        rank = sb("rank", [P, NTP, NX], F32, g4)
        cmp = sb("cmp", [P, NTP], F32, g4)
        pick = sb("pick", [P, NTP, NX], F32, g4)
        s1 = sb("s1", [P, NTP], F32, g4)
        s2 = sb("s2", [P, NTP], F32, g4)
        dexp = sb("dexp", [P, NTP], F32, g4)
        g4.close()
        PS = ctx.enter_context(nc.psum_tensor("PS", [P, 8, 512], F32))

        pads_set = sem("pads_set")
        x_loaded = sem("x_loaded")
        edges_loaded = sem("edges_loaded")
        edges2_loaded = sem("edges2_loaded")
        small_loaded = sem("small_loaded")
        tslot_free = sem("tslot_free")
        lo_ready = sem("lo_ready")
        table_stored = sem("table_stored")
        ext_reduced = sem("ext_reduced")
        nlev_ready = sem("nlev_ready")
        atable_ready = sem("atable_ready")
        atable_stored = sem("atable_stored")
        level_end = sem("level_end")
        level_go = sem("level_go")
        gates_ready = sem("gates_ready")
        exp_loaded = sem("exp_loaded")
        o_used = sem("o_used")
        stored = sem("stored")
        pool_steps = sem("pool_steps")
        iotas_ready = sem("iotas_ready")
        staged = sem("staged")
        pool_go = sem("pool_go")
        xT_ready = sem("xT_ready")
        xT_kept = sem("xT_kept")
        ext_ready = sem("ext_ready")
        iota_hi_ready = sem("iota_hi_ready")
        estaged = sem("estaged")
        att_go = sem("att_go")
        stats_ready = sem("stats_ready")
        std_ready = sem("std_ready")
        rstd_ready = sem("rstd_ready")
        hi_ready = sem("hi_ready")
        idx_ready = sem("idx_ready")
        win_done = sem("win_done")
        scales_ready = sem("scales_ready")
        y_ready = sem("y_ready")
        yT_turned = sem("yT_turned")
        yT_ready = sem("yT_ready")
        node_stats = sem("node_stats")
        node_std = sem("node_std")
        xn_turned = sem("xn_turned")
        turned = sem("turned")
        lev_ready = sem("lev_ready")
        e_ready = sem("e_ready")
        w_ready = sem("w_ready")
        self_e = sem("self_e")
        self_w = sem("self_w")
        mg_ready = sem("mg_ready")
        mg_exp = sem("mg_exp")
        level_done = sem("level_done")
        act_go = sem("act_go")
        gate_in = sem("gate_in")
        gate_std_r = sem("gate_std_r")
        gate_exp = sem("gate_exp")
        exp_ready = sem("exp_ready")
        h_mm = sem("h_mm")
        hid_ready = sem("hid_ready")
        nat_ready = sem("nat_ready")
        nat_turned = sem("nat_turned")
        nat_evacuated = sem("nat_evacuated")
        info_turned = sem("info_turned")
        ef_ready = sem("ef_ready")
        ef_turned = sem("ef_turned")
        info_ready = sem("info_ready")
        wt_turned = sem("wt_turned")
        prep_done = sem("prep_done")
        agg_done = sem("agg_done")
        oh_ready = sem("oh_ready")
        mm_done = sem("mm_done")
        xn_ready = sem("xn_ready")
        h_done = sem("h_done")
        ad_done = sem("ad_done")
        acc_done = sem("acc_done")
        sums_ready = sem("sums_ready")
        pe_go = sem("pe_go")
        b1_turned = sem("b1_turned")
        o_mm = sem("o_mm")
        prep_steps = sem("prep_steps")
        info_zeroed = sem("info_zeroed")
        win_steps = sem("win_steps")
        drel_ready = sem("drel_ready")
        node_steps = sem("node_steps")
        att_steps = sem("att_steps")
        level_steps = sem("level_steps")
        dve_go = sem("dve_go")
        gate_steps = sem("gate_steps")
        sp_go = sem("sp_go")
        away_ready = sem("away_ready")
        rows_used = sem("rows_used")
        loh_ready = sem("loh_ready")
        lo_stored = sem("lo_stored")
        lob_in = [sem(f"lob_in{h}") for h in range(2)]
        turned_kept = sem("turned_kept")
        lo_hot_ready = sem("lo_hot_ready")
        spread_ready = sem("spread_ready")
        rows_in = [sem(f"rows_in{h}") for h in range(2)]
        arows_in = [sem(f"arows_in{h}") for h in range(2)]
        LEVEL_SEMS = [away_ready, rows_used, turned_kept, lo_hot_ready, spread_ready, estaged, att_go, turned, lev_ready, e_ready, w_ready, self_e, self_w, mg_ready, mg_exp, level_done, ad_done, acc_done, sums_ready, level_steps]
        block = ctx.enter_context(nc.Block())
        x_t = x[0:(NT - 1) * P, :].rearrange("(t p) d -> p t d", p=P)
        out_t = out[0:(NT - 1) * P, :].rearrange("(t p) d -> p t d", p=P)
        X3 = X[:, :].rearrange("p (t d) -> p t d", d=D)
        AG3 = AG[:, :].rearrange("p (t n) -> p t n", n=AGW)
        PSF = PS[:, :, :].rearrange("p a b -> p (a b)")

        def tile_of(i, k):
            return X3[:, ds(i * BT + k, 1), :].rearrange("p a d -> p (a d)")

        table_t = table.rearrange("(t p) w -> p t w", p=P)
        atable_t = atable.rearrange("(t p) w -> p t w", p=P)

        AGf = AG[:, :]
        en = AGf[:, 0:2 * BC * P].bitcast(I32)
        eni = AGf[:, 2 * BC * P:4 * BC * P].bitcast(I32)
        ef = AGf[:, 4 * BC * P:7 * BC * P]
        E1 = BC * P
        loh = AGf[:, 7 * BC * P:7 * BC * P + BC * P // 2].bitcast(F16)

        def bcast(dram_row, n):
            return dram_row.to_broadcast([P, n])

        def flat(a):
            return a.rearrange("(a n) -> a n", a=1)

        @block.sync
        def _(sp):
            sp.wait_ge(pads_set, 2)
            sp.dma_start(X3[0:LAST, NT - 1, :], x[(NT - 1) * P:N, :]).then_inc(x_loaded, 16)
            for a in range(4):
                q = (NT - 1) // 4
                sp.dma_start(X3[:, a * q:(a + 1) * q, :], x_t[:, a * q:(a + 1) * q, :]).then_inc(x_loaded, 16)
            for nat_t, e in ((srcn, src), (dstn, dst)):
                sp.dma_start(nat_t[0:NG - 1, :], e[0:(NG - 1) * GROUP].rearrange("(g e) -> g e", e=GROUP)).then_inc(edges_loaded, 16)
                sp.dma_start(nat_t[NG - 1:NG, 0:TAIL], flat(e[(NG - 1) * GROUP:NE])).then_inc(edges_loaded, 16)
            for a in range(2):
                sp.dma_start(en[:, a * E1:(a + 1) * E1], edges[a:a + 1, :].rearrange("a (q e) -> (a q) e", e=E1)).then_inc(edges2_loaded, 16)
            sp.dma_start(W_sb[:, :, :], W.rearrange("(a p) i -> p a i", p=P)).then_inc(small_loaded, 16)
            sp.dma_start(Wg[:, :, :], W_gat.rearrange("(k p) c -> p k c", p=P)).then_inc(small_loaded, 16)
            sp.dma_start(b_bc[:, :], bcast(flat(b), D)).then_inc(small_loaded, 16)
            for a, row in enumerate((att_src.rearrange("h e -> (h e)"), att_dst.rearrange("h e -> (h e)"), b_gat, ln_g, ln_b)):
                sp.dma_start(small[:, a, :], bcast(flat(row), HX)).then_inc(small_loaded, 16)
            sp.sem_inc(tslot_free, 1)
            with sp.Fori(0, NT // BT) as i:
                for h, (k0, nk) in enumerate(BATCHES):
                    sp.wait_ge(lo_ready, i * 2 + (h + 1))
                    sp.dma_start(table_t[:, ds(i * BT + k0, nk), :], tstage[:, k0:k0 + nk, :]).then_inc(table_stored, 16)
                sp.wait_ge(table_stored, i * 32 + 32)
                sp.sem_inc(tslot_free, 1)
            sp.wait_ge(loh_ready, 1)
            sp.dma_start(lo_rows[0:NB, :], loh[:, :]).then_inc(lo_stored, 16)
            sp.dma_start(lo_rows[NB:NB + 2, :], loh[0:2, :]).then_inc(lo_stored, 16)
            sp.wait_ge(lo_stored, 32)
            sp.wait_ge(ext_reduced, 1)
            sp.wait_ge(nlev_ready, 1)
            levels = sp.value_load(nlev[0:1, 0:1], min_val=1, max_val=1 << 17)
            with sp.Fori(0, levels) as lv:
                sp.wait_ge(atable_ready, lv + 1)
                sp.dma_start(atable_t, NTB[:, :, :]).then_inc(atable_stored, 16)
                sp.dma_start(lob[:, 0, :], bcast(lo_rows[0:1, :], BC * P)).then_inc(lob_in[0], 16)
                sp.dma_start(lob[:, 1, :], bcast(lo_rows[1:2, :], BC * P)).then_inc(lob_in[1], 16)
                with sp.Fori(0, NB // 2) as i:
                    for h in range(2):
                        sp.wait_ge(away_ready, i * 2 + (h + 1))
                        sp.dma_start(lob[:, h, :], bcast(lo_rows[ds(i * 2 + (h + 2), 1), :], BC * P)).then_inc(lob_in[h], 16)
                for h in range(2):
                    sp.wait_ge(lob_in[h], lv * LOB_LEVEL + LOB_LEVEL)
                sp.wait_ge(level_end, lv * 4 + 4)
                sp.sem_inc(sp_go, 1)
                for q in LEVEL_SEMS:
                    sp.sem_clear(q)
                sp.sem_inc(level_go, 1)
            sp.wait_ge(gates_ready, 1)
            for k in range(2):
                sp.dma_start(W1_sb[:, k, :, :], W1[:, k * P:(k + 1) * P, :].rearrange("e p n -> p e n")).then_inc(exp_loaded, 16)
            for e in range(NE_X):
                sp.dma_start(W2_sb[:, e, :, :], W2[e, :, :].rearrange("(c p) n -> p c n", p=P)).then_inc(exp_loaded, 16)
            sp.dma_start(b1n[:, :], b1.rearrange("e (c p) -> (e c) p", p=P)).then_inc(exp_loaded, 16)
            sp.dma_start(b2r[:, :], flat(b2.rearrange("e n -> (e n)"))).then_inc(exp_loaded, 16)
            with sp.Fori(0, NT // NJ) as i:
                sp.wait_ge(o_used, i * 4 + 6)
                sp.dma_start(out_t[:, ds(i * NJ, NJ), :], X3[:, ds(i * NJ, NJ), :]).then_inc(stored, 16)
            sp.wait_ge(o_used, (NT // NJ) * 4 + 6)
            sp.dma_start(out[(NT - 1) * P:N, :], X3[0:LAST, NT - 1, :]).then_inc(stored, 16)
            sp.wait_ge(stored, 16 * (NT // NJ + 1))

        @block.gpsimd
        def _(pool):
            steps = Chain(pool, pool_steps)
            steps.link(nc.gpsimd.memset(identf[:, :], 0.0), nc.gpsimd.memset(identh[:, :], 0.0), nc.gpsimd.memset(tri[:, :], 0.0))
            nc.gpsimd.affine_select(out=identf[:, :], in_=identf[:, :], compare_op=ALU.not_equal, fill=1.0, base=0,
                                    pattern=[[-1, P]], channel_multiplier=1)
            nc.gpsimd.affine_select(out=identh[:, :], in_=identh[:, :], compare_op=ALU.not_equal, fill=1.0, base=0,
                                    pattern=[[-1, P]], channel_multiplier=1)
            nc.gpsimd.affine_select(out=tri[:, :], in_=tri[:, :], compare_op=ALU.is_ge, fill=1.0, base=0,
                                    pattern=[[-1, NG + 1]], channel_multiplier=1)
            nc.gpsimd.iota(minus_node[:, :], [[-P, NJ]], base=0, channel_multiplier=-1, allow_small_or_imprecise_dtypes=True)
            nc.gpsimd.iota(iota_lo[:, :], [[1, LO]], base=0, channel_multiplier=0,
                           allow_small_or_imprecise_dtypes=True).then_inc(iotas_ready, 1)
            with pool.Fori(0, NG // 2) as i:
                for h in range(2):
                    pool.wait_ge(staged, i * 2 + (h + 1))
                    pool.sem_inc(pool_go, 1)
                    pool.wait_ge(table_stored, 32 * (NT // BT))
                    for k in range(h * CH, (h + 1) * CH):
                        pool.indirect_dma_start(ring[:, k, 0:2 * D], None, table,
                                                bass.IndirectOffsetOnAxis(ap=sstage[:, k:k + 1], axis=0)).then_inc(rows_in[h], 16)
            pool.sem_inc(xT_kept, 2)
            with pool.Fori(0, NT // BT) as i:
                for h, (k0, nk) in enumerate(BATCHES):
                    pool.wait_ge(xT_ready, i * 2 + (h + 1))
                    for k in range(k0, k0 + nk):
                        last = nc.gpsimd.tensor_copy(AG[:, ds((i * BT + k) * AGW, D)], xT[:, k, :, :].rearrange("p a n -> p (a n)"))
                    last.then_inc(xT_kept, 1)
            pool.wait_ge(ext_ready, 1)
            nc.gpsimd.partition_all_reduce(extr[:, :], ext[:, :], P, RED.max).then_inc(ext_reduced, 1)
            nc.gpsimd.iota(iota_hi[:, :], [[1, NHI], [0, VAL]], base=0, channel_multiplier=0,
                           allow_small_or_imprecise_dtypes=True).then_inc(iota_hi_ready, 1)
            pool.wait_ge(nlev_ready, 1)
            levels = pool.value_load(nlev[0:1, 0:1], min_val=1, max_val=1 << 17)
            with pool.Fori(0, levels) as lv:
                pool.wait_ge(atable_stored, lv * 16 + 16)
                pool.sem_inc(pool_go, 1)
                with pool.Fori(0, NB // 2) as i:
                    for h in range(2):
                        pool.wait_ge(estaged, i * 2 + (h + 1))
                        pool.sem_inc(att_go, 1)
                        pool.wait_ge(iota_hi_ready, 1)
                        for k in range(BC):
                            pool.indirect_dma_start(rows[:, h, k, :], None, atable,
                                                    bass.IndirectOffsetOnAxis(ap=istage[:, h * BC + k:h * BC + k + 1], axis=0)).then_inc(arows_in[h], 16)
                for h in range(2):
                    pool.wait_ge(arows_in[h], lv * ROWS_LEVEL + ROWS_LEVEL)
                pool.sem_inc(level_end, 1)
                pool.wait_ge(level_go, lv + 1)
                pool.sem_inc(pool_go, 1)

        @block.scalar
        def _(act):
            act.wait_ge(pads_set, 2)
            with act.Fori(0, NT // BT) as i:
                for h, (k0, nk) in enumerate(BATCHES):
                    act.wait_ge(stats_ready, i * 2 + (h + 1))
                    nc.scalar.activation(std[:, k0:k0 + nk], mv[:, k0:k0 + nk, 1], ACT.Sqrt, bias=consts[:, 0:1]).then_inc(std_ready, 1)
                    act.wait_ge(rstd_ready, i * 2 + (h + 1))
                    if h == 0:
                        act.wait_ge(tslot_free, i + 1)
                    act.wait_ge(pads_set, 2)
                    for k in range(k0, k0 + nk):
                        last = nc.scalar.activation(tstage[:, k, D:2 * D], X3[:, ds(i * BT + k, 1), :].rearrange("p a d -> p (a d)"), ACT.Identity,
                                                    bias=shift[:, k:k + 1], scale=rstd[:, k:k + 1])
                    last.then_inc(hi_ready, 1)
            act.wait_ge(idx_ready, 1)
            with act.Fori(0, NG // 2) as i:
                for h in range(2):
                    before = act.value_load(info[0:1, ds(i * 2 + (NG + 2 + h), 1)], min_val=0, max_val=32 * NG)
                    act.wait_ge(win_done, before + 1)
                    act.wait_ge(idx_ready, 1)
                    nc.scalar.copy(sstage[:, h * CH:(h + 1) * CH], sidx_all[:, ds((i * 2 + h) * CH, CH)]).then_inc(staged, 1)
            with act.Fori(0, NT // BT) as i:
                for h, (k0, nk) in enumerate(BATCHES):
                    act.wait_ge(scales_ready, i * 2 + (h + 1))
                    act.wait_ge(idx_ready, 1)
                    for k in range(k0, k0 + nk):
                        last = nc.scalar.activation(y[:, k, :], AG[:, ds((i * BT + k) * AGW, D)], ACT.Copy, scale=dgs[:, 2, k:k + 1])
                    last.then_inc(y_ready, 1)
                for h, (k0, nk) in enumerate(BATCHES):
                    act.wait_ge(yT_turned, i * 2 + (h + 1))
                    nc.scalar.copy(yT[:, k0:k0 + nk, :, :].rearrange("p k a n -> p (k a n)"), PSF[:, h * 1024:h * 1024 + nk * D]).then_inc(yT_ready, 1)
                for h, (k0, nk) in enumerate(BATCHES):
                    act.wait_ge(node_stats, i * 2 + (h + 1))
                    nc.scalar.activation(std[:, k0:k0 + nk], mv[:, k0:k0 + nk, 1], ACT.Sqrt, bias=consts[:, 0:1]).then_inc(node_std, 1)
                for h, (k0, nk) in enumerate(BATCHES):
                    act.wait_ge(xn_turned, i * 2 + (h + 1))
                    act.wait_ge(xT_kept, i * 2 + (h + 1))
                    nc.scalar.copy(xT[:, k0:k0 + nk, :, :].rearrange("p k a n -> p (k a n)"), PSF[:, h * 1024:h * 1024 + nk * D]).then_inc(xT_ready, 1)
            act.wait_ge(nlev_ready, 1)
            levels = act.value_load(nlev[0:1, 0:1], min_val=1, max_val=1 << 17)
            with act.Fori(0, levels) as lv:

                def stage_rows(q, h):
                    nc.scalar.copy(istage[:, h * BC:(h + 1) * BC],
                                   asrc_idx[:, ds(q, 1), :].rearrange("p a r -> p (a r)")).then_inc(estaged, 1)

                def one_hot_columns(h):
                    for j in range(NJ):
                        last = nc.scalar.activation(ST[:, h, j, :], lob[:, h, :], ACT.Abs, bias=minus_node[:, j:j + 1])
                    last.then_inc(away_ready, 1)

                def cut(h):
                    flat_st = ST[:, h, :, :].rearrange("p j e -> p (j e)")
                    nc.scalar.activation(flat_st, flat_st, ACT.Relu, bias=1.0, scale=-1.0).then_inc(turned_kept, 1)

                act.wait_ge(lev_ready, 1)
                stage_rows(0, 0)
                stage_rows(1, 1)
                for h in range(2):
                    act.wait_ge(lob_in[h], lv * LOB_LEVEL + 16)
                    one_hot_columns(h)
                    act.wait_ge(away_ready, h + 1)
                    cut(h)
                with act.Fori(0, NB // 2) as i:
                    for h in range(2):
                        act.wait_ge(e_ready, i * 2 + (h + 1))
                        nc.scalar.activation(wexp[:, :, :], ez[:, :, :], ACT.Exp).then_inc(w_ready, 1)
                        act.wait_ge(lob_in[h], lv * LOB_LEVEL + i * 16 + 32)
                        act.wait_ge(ad_done, i * 2 + (h + 1))
                        one_hot_columns(h)
                        act.wait_ge(rows_used, i * 2 + (h + 1))
                        act.wait_ge(lev_ready, 1)
                        stage_rows(i * 2 + (h + 2), h)
                        act.wait_ge(away_ready, i * 2 + (h + 3))
                        cut(h)
                act.wait_ge(self_e, 1)
                nc.scalar.activation(n3[:, :, :], n2[:, :, :], ACT.Exp).then_inc(self_w, 1)
                act.wait_ge(mg_ready, 1)
                nc.scalar.activation(n4[:, :, :], n2[:, :, :], ACT.Exp).then_inc(mg_exp, 1)
                act.wait_ge(level_done, 1)
                act.sem_inc(level_end, 1)
                act.wait_ge(level_go, lv + 1)
                act.sem_inc(act_go, 1)
            act.wait_ge(gate_in, 1)
            nc.scalar.activation(m3[:, :], m2[:, :], ACT.Sqrt, bias=consts[:, 0:1]).then_inc(gate_std_r, 1)
            act.wait_ge(gate_in, 2)
            nc.scalar.activation(dexp[:, :], cmp[:, :], ACT.Exp).then_inc(gate_exp, 1)
            act.wait_ge(exp_ready, 1)

            def hidden(base, w):
                for e in range(NE_X):
                    for c in range(HID // P):
                        act.wait_ge(h_mm, base + (e * 4 + c + 1))
                        nc.scalar.activation(hh[:, e % 2, c, 0:w], PS[:, c, 0:w], ACT.Gelu,
                                             bias=b1T[:, e * 4 + c:e * 4 + c + 1]).then_inc(hid_ready, 1)

            with act.Fori(0, NT // NJ) as i:
                hidden(i * 16, LO)
            hidden((NT // NJ) * 16, P)

        @block.tensor
        def _(pe):
            pe.wait_ge(iotas_ready, 1)
            pe.wait_ge(nat_ready, 1)
            for r in range(8):
                for k in range(4):
                    f = (srcf, dstf)[r // 4][:, ((r % 4) * 4 + k) * P:((r % 4) * 4 + k + 1) * P]
                    last = nc.tensor.transpose(PS[:, r, k * NG:(k + 1) * NG], f, identf[0:NG, 0:NG])
                last.then_inc(nat_turned, 1)
            pe.wait_ge(nat_evacuated, 8)
            nc.tensor.matmul(PS[0:1, 0, 0:NG], colf[0:NG, 2:3], identf[0:NG, 0:NG], start=True, stop=True)
            nc.tensor.matmul(PS[0:1, 1, 0:NG + 1], colf[0:NG, 5:6], tri[0:NG, 0:NG + 1], start=True, stop=True).then_inc(info_turned, 1)
            pe.wait_ge(ef_ready, 1)
            for r in range(6):
                for k in range(4):
                    last = nc.tensor.transpose(PS[:, 2 + r, k * P:(k + 1) * P], ef[:, (r * 4 + k) * P:(r * 4 + k + 1) * P], identf[:, :])
                last.then_inc(ef_turned, 1)
            pe.wait_ge(info_ready, 1)
            pe.wait_ge(small_loaded, 16 * 8)
            for kin in range(2):
                for a in range(2):
                    last = nc.tensor.transpose(PS[:, 0, (kin * 2 + a) * P:(kin * 2 + a + 1) * P], W_sb[:, a, kin * P:(kin + 1) * P], identf[:, :])
            last.then_inc(wt_turned, 1)
            pe.wait_ge(prep_done, 1)
            pe.sem_inc(win_done, 1)
            with pe.Fori(0, NG // 2) as i:
                for h in range(2):
                    w0 = pe.value_load(info[0:1, ds(i * 2 + (NG + 3 + h), 1)], min_val=0, max_val=32 * NG)
                    w1 = pe.value_load(info[0:1, ds(i * 2 + (NG + 4 + h), 1)], min_val=1, max_val=32 * NG)
                    pe.wait_ge(rows_in[h], i * (16 * CH) + 16 * CH)
                    pe.sem_inc(pe_go, 1)
                    with pe.Fori(w0, w1) as v:
                        pe.wait_ge(agg_done, v + 1)
                        pe.wait_ge(oh_ready, v + 1)
                        for k in range(CH):
                            for t in range(2):
                                oh = OH[:, k, t * P:(t + 1) * P]
                                nc.tensor.matmul(PS[:, t, 0:AGW], oh, ring[:, h * CH + k, D:2 * D + 1], start=(k == 0), stop=False, skip_group_check=True)
                                last = nc.tensor.matmul(PS[:, t, 0:D], oh, ring[:, h * CH + k, 0:D], start=False, stop=(k == CH - 1), skip_group_check=True)
                        last.then_inc(win_done, 1)
            with pe.Fori(0, NT // BT) as i:
                for h, (k0, nk) in enumerate(BATCHES):
                    pe.wait_ge(y_ready, i * 2 + (h + 1))
                    for k in range(nk):
                        for a in range(2):
                            last = nc.tensor.transpose(PSF[:, h * 1024 + (k * 2 + a) * P:h * 1024 + (k * 2 + a + 1) * P], y[:, k0 + k, a * P:(a + 1) * P], identf[:, :])
                    last.then_inc(yT_turned, 1)
                for h, (k0, nk) in enumerate(BATCHES):
                    pe.wait_ge(yT_ready, i * 2 + (h + 1))
                    for k in range(nk):
                        o = 2048 + h * 1024 + k * D
                        for a in range(2):
                            last = nc.tensor.matmul(PSF[:, o:o + D], yT[:, k0 + k, a, :], WT[:, a, :], start=(a == 0), stop=(a == 1))
                    last.then_inc(mm_done, 1)
                for h, (k0, nk) in enumerate(BATCHES):
                    pe.wait_ge(xn_ready, i * 2 + (h + 1))
                    for k in range(nk):
                        for a in range(2):
                            last = nc.tensor.transpose(PSF[:, h * 1024 + (k * 2 + a) * P:h * 1024 + (k * 2 + a + 1) * P], xnb[:, k0 + k, a * P:(a + 1) * P], identf[:, :])
                    last.then_inc(xn_turned, 1)
                for h, (k0, nk) in enumerate(BATCHES):
                    pe.wait_ge(xT_ready, i * 2 + (h + 1))
                    for k in range(nk):
                        o = 2048 + h * 1024 + k * HX
                        for a in range(2):
                            last = nc.tensor.matmul(PSF[:, o:o + HX], xT[:, k0 + k, a, :], Wg[:, a, :], start=(a == 0), stop=(a == 1))
                    last.then_inc(h_done, 1)
            pe.wait_ge(nlev_ready, 1)
            levels = pe.value_load(nlev[0:1, 0:1], min_val=1, max_val=1 << 17)
            with pe.Fori(0, levels) as lv:

                def look_up(h):
                    for r in range(BC):
                        for j in range(NJ):
                            for part in range(2):
                                last = nc.tensor.matmul(PS[:, 4 + h, r * NHI * HEADS:(r + 1) * NHI * HEADS], ST[:, h, j, r * P:(r + 1) * P],
                                                        Tad[:, part, j, :, :].rearrange("p a b -> p (a b)"),
                                                        start=(j == 0 and part == 0), stop=(j == NJ - 1 and part == 1))
                    last.then_inc(ad_done, 1)

                def add_up(h):
                    for r in range(BC):
                        for j in range(NJ):
                            for part in range(2):
                                last = nc.tensor.matmul(PS[:, j, 0:HIV], S[:, h, r, j * P:(j + 1) * P], M[:, h, r, part * HIV:(part + 1) * HIV],
                                                        start=False, stop=False, skip_group_check=True)
                    last.then_inc(acc_done, 1)

                def clear_sums(start):
                    for j in range(NJ):
                        last = nc.tensor.matmul(PS[:, j, 0:HIV], zero_l[:, :], iota_hi[:, 0:HIV], start=start, stop=not start, skip_group_check=True)
                    return last

                pe.wait_ge(lev_ready, 1)
                clear_sums(True).then_inc(acc_done, 1)
                pe.wait_ge(turned_kept, 1)
                look_up(0)
                with pe.Fori(0, NB // 2) as i:
                    for h in range(2):
                        pe.wait_ge(turned_kept, i * 2 + (h + 2))
                        pe.wait_ge(spread_ready, i * 2 + (h + 1))
                        look_up(1 - h)
                        pe.wait_ge(lo_hot_ready, i * 2 + (h + 1))
                        pe.wait_ge(spread_ready, i * 2 + (h + 2))
                        add_up(h)
                clear_sums(False).then_inc(sums_ready, 1)
                pe.wait_ge(level_done, 1)
                pe.sem_inc(level_end, 1)
                pe.wait_ge(level_go, lv + 1)
                pe.sem_inc(pe_go, 1)
            pe.wait_ge(exp_loaded, 16 * (2 + NE_X + 2))
            nb1 = NE_X * HID // P
            nc.tensor.transpose(PS[:, 7, 0:nb1], b1n[:, :], identf[0:nb1, 0:nb1]).then_inc(b1_turned, 1)
            pe.wait_ge(exp_ready, 1)

            def hid_products(e, base, tile0, nt):
                for c in range(HID // P):
                    if e > 0:
                        pe.wait_ge(hid_ready, base * 16 + ((e - 1) * 4 + c + 1))
                    for a in range(2):
                        rhs = AG3[:, ds(tile0, nt), a * P:(a + 1) * P]
                        last = nc.tensor.matmul(PS[:, c, 0:nt * P], W1_sb[:, a, e, c * P:(c + 1) * P], rhs, start=(a == 0), stop=(a == 1))
                    last.then_inc(h_mm, 1)

            def out_products(e, base, nt):
                pe.wait_ge(o_used, base * 4 + (e + 1))
                pe.wait_ge(hid_ready, base * 16 + (e * 4 + 4))
                for t in range(nt):
                    o = PS[:, 4 + 2 * (e % 2) + t // 2, (t % 2) * D:(t % 2 + 1) * D]
                    nc.tensor.matmul(o, ones1[0:1, :], b2r[0:1, e * D:(e + 1) * D], start=True, stop=False)
                    for c in range(HID // P):
                        last = nc.tensor.matmul(o, hh[:, e % 2, c, t * P:(t + 1) * P], W2_sb[:, e, c, :], start=False, stop=(c == HID // P - 1))
                last.then_inc(o_mm, 1)

            def experts(base, tile0, nt):
                hid_products(0, base, tile0, nt)
                for e in range(1, NE_X):
                    hid_products(e, base, tile0, nt)
                    out_products(e - 1, base, nt)
                out_products(NE_X - 1, base, nt)

            with pe.Fori(0, NT // NJ) as i:
                experts(i, i * NJ, NJ)
            experts(NT // NJ, (NT // NJ) * NJ, 1)

        @block.vector
        def _(v):
            vec = nc.vector
            steps = Chain(v, prep_steps)
            link = steps.link
            vec.memset(X3[:, NT - 1, :], 0.0)
            vec.memset(consts[:, 0:1], EPS)
            vec.memset(srcn[P - 32:P, :], 0).then_inc(pads_set, 1)
            vec.memset(dstn[P - 32:P, :], PADN).then_inc(pads_set, 1)
            v.wait_ge(x_loaded, 16 * 5)
            v.wait_ge(pads_set, 2)
            with steps.loop(NT // BT, 12) as i:
                for h, (k0, nk) in enumerate(BATCHES):
                    ks = slice(k0, k0 + nk)

                    def tile(k):
                        return X3[:, ds(i * BT + k, 1), :].rearrange("p a d -> p (a d)")

                    link(*[vec.bn_stats(stats[:, k, :], tile(k)) for k in range(k0, k0 + nk)])
                    v.sem_inc(dve_go, 1)
                    link(*[vec.bn_aggr(mv[:, k, :], stats[:, k, :]) for k in range(k0, k0 + nk)])
                    v.sem_inc(stats_ready, 1)
                    v.wait_ge(std_ready, i * 2 + (h + 1))
                    link(vec.reciprocal(rstd[:, ks], std[:, ks]))
                    link(vec.tensor_scalar(rstd[:, ks], rstd[:, ks], TAB_SCALE, None, ALU.mult))
                    link(vec.scalar_tensor_tensor(shift[:, ks], mv[:, ks, 0], -1.0, rstd[:, ks], ALU.mult, ALU.mult))
                    v.sem_inc(rstd_ready, 1)
                    link(*[vec.tensor_scalar(xs[:, k, :], tile(k), mv[:, k, 0:1], rstd[:, k:k + 1], ALU.subtract, ALU.mult) for k in range(k0, k0 + nk)])
                    v.wait_ge(hi_ready, i * 2 + (h + 1))
                    vec.tensor_tensor(tstage[:, ks, 0:D], xs[:, ks, :], tstage[:, ks, D:2 * D], ALU.subtract).then_inc(lo_ready, 1)
            v.wait_ge(edges_loaded, 64)
            link(vec.tensor_scalar(dstf, dstn[0:NG, :], PADN, None, ALU.min),
                 vec.tensor_scalar(srcf, srcn[0:NG, :], N - 1, None, ALU.min))
            link(vec.tensor_reduce(colf[0:NG, 0:1], dstf, AX.X, ALU.min), vec.tensor_reduce(colf[0:NG, 1:2], dstf, AX.X, ALU.max))
            link(vec.tensor_copy(cols[0:NG, 0:2], colf[0:NG, 0:2]))
            link(vec.tensor_scalar(cols[0:NG, 2:4], cols[0:NG, 0:2], 7, None, ALU.arith_shift_right))
            link(vec.tensor_copy(colf[0:NG, 2:4], cols[0:NG, 2:4]))
            link(vec.tensor_tensor(cols[0:NG, 4:5], colf[0:NG, 3:4], colf[0:NG, 2:3], ALU.subtract),
                 vec.tensor_scalar(colf[0:NG, 6:7], colf[0:NG, 2:3], float(P), None, ALU.mult))
            link(vec.tensor_scalar(cols[0:NG, 5:6], cols[0:NG, 4:5], 1, None, ALU.arith_shift_right))
            link(vec.tensor_scalar(colf[0:NG, 5:6], cols[0:NG, 5:6], 1.0, None, ALU.add),
                 vec.tensor_scalar(dstf, dstf, colf[0:NG, 6:7], None, ALU.subtract))
            v.sem_inc(nat_ready, 1)
            for r in range(8):
                v.wait_ge(nat_turned, r + 1)
                to = (sidx_all, drel_all)[r // 4][:, :].rearrange("p (g k) -> p k g", k=CH)[:, 4 * (r % 4):4 * (r % 4) + 4, :]
                vec.tensor_copy(to, PS[:, r, 0:4 * NG].rearrange("p (k g) -> p k g", k=4)).then_inc(nat_evacuated, 1)
            vec.memset(info[0:1, :], 0).then_inc(info_zeroed, 1)
            v.wait_ge(info_turned, 1)
            v.wait_ge(info_zeroed, 1)
            link(vec.tensor_copy(info[0:1, 0:NG], PS[0:1, 0, 0:NG]), vec.tensor_copy(info[0:1, NG + 3:2 * NG + 4], PS[0:1, 1, 0:NG + 1]))
            v.wait_ge(nat_evacuated, 8)
            v.sem_inc(idx_ready, 1)
            v.sem_inc(info_ready, 1)
            v.wait_ge(edges2_loaded, 32)
            link(vec.tensor_scalar(eni[:, 0:E1], en[:, E1:2 * E1], LO - 1, None, ALU.bitwise_and),
                 vec.tensor_scalar(eni[:, E1:2 * E1], en[:, E1:2 * E1], int(np.log2(LO)), None, ALU.arith_shift_right),
                 vec.tensor_scalar(ef[:, 0:E1], en[:, 0:E1], N - 1, None, ALU.min))
            link(vec.tensor_copy(ef[:, E1:3 * E1], eni[:, :]), vec.tensor_copy(loh, eni[:, 0:E1]),
                 vec.memset(asrc_idx[:, NB:NB + 2, :], 0), vec.memset(lohi[:, NB:NB + 1, :, :], 0.0))
            v.sem_inc(ef_ready, 1)
            v.sem_inc(loh_ready, 1)
            for r in range(6):
                v.wait_ge(ef_turned, r + 1)
                turn4 = PS[:, 2 + r, :].rearrange("p (k q) -> p k q", k=4)
                ks = slice(4 * (r % 2), 4 * (r % 2) + 4)
                to = asrc_idx[:, 0:NB, ks].rearrange("p q r -> p r q") if r < 2 else lohi[:, 0:NB, r // 2 - 1, ks].rearrange("p q r -> p r q")
                last = vec.tensor_copy(to, turn4)
            link(last)
            v.wait_ge(wt_turned, 1)
            link(vec.tensor_copy(WT[:, :, :].rearrange("p a n -> p (a n)"), PS[:, 0, :]),
                 vec.memset(ring[:, :, 2 * D:2 * D + 1], 1.0))
            v.wait_ge(lo_stored, 32)
            vec.memset(AG[:, :], 0.0).then_inc(agg_done, 1)
            v.wait_ge(agg_done, 1)
            v.sem_inc(prep_done, 1)
            wsteps = Chain(v, win_steps)
            with v.Fori(0, NG // 2) as i:
                for h in range(2):
                    w0 = v.value_load(info[0:1, ds(i * 2 + (NG + 3 + h), 1)], min_val=0, max_val=32 * NG)
                    w1 = v.value_load(info[0:1, ds(i * 2 + (NG + 4 + h), 1)], min_val=1, max_val=32 * NG)
                    t0 = v.value_load(info[0:1, ds(i * 2 + h, 1)], min_val=0, max_val=NT - 1)
                    vec.tensor_copy(drelw[:, :], drel_all[:, ds((i * 2 + h) * CH, CH)]).then_inc(drel_ready, 1)
                    v.wait_ge(drel_ready, i * 2 + (h + 1))
                    v.sem_inc(dve_go, 1)
                    with v.Fori(w0, w1) as w:
                        for k in range(CH):
                            last = vec.tensor_scalar(OH[:, k, :], iota_lo[:, 0:2 * P], drelw[:, k:k + 1], None, ALU.is_equal)
                        last.then_inc(oh_ready, 1)
                        v.wait_ge(oh_ready, w + 1)
                        vec.tensor_scalar(drelw[:, :], drelw[:, :], 2.0 * P, None, ALU.subtract).then_inc(win_steps, 1)
                        v.wait_ge(win_steps, w + 1)
                        v.wait_ge(win_done, w + 2)
                        tile = nc.s_assert_within(t0 + (w - w0) * 2, 0, NT - 1,
                                                  skip_runtime_bounds_check_because="the windows of a group end with its last tile")
                        at = AG[:, ds(tile * AGW, 2 * AGW)].rearrange("p (t n) -> p t n", t=2)
                        vec.tensor_tensor(at, at, PS[:, 0:2, 0:AGW], ALU.add).then_inc(agg_done, 1)
                        v.wait_ge(agg_done, w + 2)
            steps = Chain(v, node_steps)
            link = steps.link
            v.wait_ge(small_loaded, 16 * 8)
            with steps.loop(NT // BT, 2 * 3 + 2 * 4 + 2 * 2 + 2) as i:
                for h, (k0, nk) in enumerate(BATCHES):
                    ks = slice(k0, k0 + nk)
                    deg = AG3[:, ds(i * BT + k0, nk), D:D + 1].rearrange("p t a -> p (t a)")
                    link(vec.tensor_scalar(dgs[:, 0, ks], deg, 1.0, None, ALU.add))
                    link(vec.reciprocal(dgs[:, 1, ks], dgs[:, 0, ks]))
                    link(vec.tensor_scalar(dgs[:, 2, ks], dgs[:, 1, ks], 1.0 / TAB_SCALE, None, ALU.mult),
                         vec.tensor_tensor(dgs[:, 3, ks], dgs[:, 1, ks], deg, ALU.mult))
                    v.sem_inc(scales_ready, 1)
                for h, (k0, nk) in enumerate(BATCHES):
                    v.wait_ge(mm_done, i * 2 + (h + 1))
                    Xb = X3[:, ds(i * BT + k0, nk), :]
                    link(vec.tensor_tensor(Xb, Xb, PSF[:, 2048 + h * 1024:2048 + h * 1024 + nk * D].rearrange("p (t n) -> p t n", n=D), ALU.add))
                    link(*[vec.scalar_tensor_tensor(tile_of(i, k), b_bc[:, :], dgs[:, 3, k:k + 1], tile_of(i, k), ALU.mult, ALU.add) for k in range(k0, k0 + nk)])
                    v.sem_inc(dve_go, 1)
                    link(*[vec.bn_stats(stats[:, k, :], tile_of(i, k)) for k in range(k0, k0 + nk)])
                    v.sem_inc(dve_go, 1)
                    link(*[vec.bn_aggr(mv[:, k, :], stats[:, k, :]) for k in range(k0, k0 + nk)])
                    v.sem_inc(node_stats, 1)
                for h, (k0, nk) in enumerate(BATCHES):
                    ks = slice(k0, k0 + nk)
                    v.wait_ge(node_std, i * 2 + (h + 1))
                    link(vec.reciprocal(rstd[:, ks], std[:, ks]))
                    link(*[vec.tensor_scalar(xnb[:, k, :], tile_of(i, k), mv[:, k, 0:1], rstd[:, k:k + 1], ALU.subtract, ALU.mult) for k in range(k0, k0 + nk)])
                    v.sem_inc(xn_ready, 1)
                for h, (k0, nk) in enumerate(BATCHES):
                    v.wait_ge(h_done, i * 2 + (h + 1))
                    link(vec.tensor_copy(H[:, ds(i * BT + k0, nk), :].rearrange("p t n -> p (t n)"), PSF[:, 2048 + h * 1024:2048 + h * 1024 + nk * HX]))
            v.wait_ge(xT_kept, 2 * (NT // BT) + 2)
            steps = Chain(v, att_steps)
            link = steps.link
            ops = lambda o, a, b_, op: vec.tensor_tensor(o, a, b_, op)
            link(vec.memset(H[:, NT:NTP, :], 0.0), vec.memset(acc[:, :, :], 0.0), vec.memset(Rsh[:, :, :], 0.0),
                 vec.memset(zero_l[:, :], 0.0), vec.memset(ext[:, :], 0.0))
            for a, to in ((0, AS), (1, AD)):
                link(ops(tmp16[:, :, 0:HX], H[:, :, :], small[:, a:a + 1, :].to_broadcast([P, NTP, HX]), ALU.mult))
                link(vec.tensor_reduce(to[:, :, :], tmp16[:, :, 0:HX].rearrange("p t (h e) -> p t h e", e=NX), AX.X, ALU.add))
            link(vec.tensor_reduce(ext[:, 0:4], AS[:, :, :].rearrange("p t h -> p h t"), AX.X, ALU.max),
                 vec.tensor_reduce(ext[:, 4:8], AS[:, :, :].rearrange("p t h -> p h t"), AX.X, ALU.min),
                 vec.tensor_reduce(ext[:, 8:9], AD[:, :, :].rearrange("p t h -> p (t h)"), AX.X, ALU.max, apply_absolute_value=True),
                 vec.tensor_reduce(ext[:, 9:10], H[:, :, :].rearrange("p t h -> p (t h)"), AX.X, ALU.max, apply_absolute_value=True))
            link(vec.tensor_scalar(ext[:, 4:8], ext[:, 4:8], -1.0, None, ALU.mult))
            v.sem_inc(ext_ready, 1)
            v.wait_ge(ext_reduced, 1)
            link(vec.tensor_scalar(sc[:, 0:2], extr[:, 8:10], 1e-25, None, ALU.max),
                 vec.tensor_tensor(n1[:, 0, :], extr[:, 0:4], extr[:, 4:8], ALU.add))
            link(vec.reciprocal(sc[:, 2:4], sc[:, 0:2]), vec.tensor_reduce(sc[:, 8:9], n1[:, 0, :], AX.X, ALU.max))
            link(vec.tensor_scalar(sc[:, 4:5], sc[:, 2:3], FULL, None, ALU.mult), vec.tensor_scalar(sc[:, 5:6], sc[:, 0:1], 1.0 / FULL, None, ALU.mult),
                 vec.tensor_scalar(sc[:, 6:7], sc[:, 3:4], FULL, None, ALU.mult), vec.tensor_scalar(sc[:, 7:8], sc[:, 1:2], 1.0 / FULL, None, ALU.mult),
                 vec.tensor_scalar(nlev[:, :], sc[:, 8:9], 1.0 / LEVEL, 1.0, ALU.mult, ALU.add))
            v.sem_inc(nlev_ready, 1)
            NT5 = NTB[:, :, HEADS:ROWW].rearrange("p t (h e) -> p t h e", e=1 + NX)
            link(vec.tensor_scalar(ADs[:, :, :], AD[:, :, :], sc[:, 4:5], None, ALU.mult),
                 vec.memset(NTB[:, :, :], DEN_SCALE), vec.tensor_copy(Gk[:, :], extr[:, 0:4]))
            Tp = [Tad[:, a, :, :, :].rearrange("p j t h -> p t j h") for a in range(2)]
            AD4 = ADs[:, :, :].rearrange("p (t j) h -> p t j h", j=NJ)
            link(*[vec.tensor_scalar(NT5[:, :, hd, 1:1 + NX], H[:, :, hd * NX:(hd + 1) * NX], sc[:, 6:7], None, ALU.mult) for hd in range(HEADS)])
            link(*[vec.tensor_copy(Tp[0][:, :, j, :], AD4[:, :, j, :]) for j in range(NJ)])
            link(*[ops(Tp[1][:, :, j, :], AD4[:, :, j, :], Tp[0][:, :, j, :], ALU.subtract) for j in range(NJ)])
            v.wait_ge(iota_hi_ready, 1)
            levels = v.value_load(nlev[0:1, 0:1], min_val=1, max_val=1 << 17)
            NTH = [P, NTP, HEADS]
            with v.Fori(0, levels) as lv:
                steps = Chain(v, level_steps)
                link = steps.link
                Gb = Gk[:, :].unsqueeze(1).to_broadcast(NTH)
                link(vec.tensor_scalar(Gk1[:, :], Gk[:, :], LEVEL, None, ALU.subtract), ops(n3[:, :, :], AS[:, :, :], Gb, ALU.is_le),
                     ops(n1[:, :, :], AD[:, :, :], Gb, ALU.add))
                link(ops(n2[:, :, :], AS[:, :, :], Gk1[:, :].unsqueeze(1).to_broadcast(NTH), ALU.is_gt))
                link(ops(n2[:, :, :], n2[:, :, :], n3[:, :, :], ALU.mult))
                link(ops(NTB[:, :, 0:HEADS], AS[:, :, :], n2[:, :, :], ALU.mult), vec.tensor_scalar(n3[:, :, :], n2[:, :, :], 1.0, BIG, ALU.subtract, ALU.mult))
                link(ops(NTB[:, :, 0:HEADS], NTB[:, :, 0:HEADS], n3[:, :, :], ALU.add))
                v.sem_inc(atable_ready, 1)
                v.sem_inc(lev_ready, 1)

                def copy_stage(q, h):
                    link(vec.tensor_copy(estage[:, h, :], lohi[:, ds(q, 1), :, :].rearrange("p a b r -> p (a b r)")))

                def make_S(h):
                    for r in range(BC):
                        last = vec.tensor_scalar(S[:, h, r, :], iota_lo[:, :], estage[:, h, r:r + 1], None, ALU.is_equal)
                    last.then_inc(lo_hot_ready, 1)

                copy_stage(0, 0)
                make_S(0)
                v.sem_inc(spread_ready, 1)
                with steps.loop(NB // 2, 2 * 9) as i:
                    for h in range(2):
                        v.wait_ge(spread_ready, i * 2 + (h + 1))
                        link(*[vec.tensor_scalar(Hm[:, r, :], iota_hi[:, :], estage[:, h, BC + r:BC + r + 1], None, ALU.is_equal) for r in range(BC)])
                        v.wait_ge(ad_done, i * 2 + (h + 1))
                        Hm4 = Hm[:, :, :].rearrange("p r (t f) -> p r t f", f=VAL)[:, :, :, 0:HEADS]
                        ad4 = PS[:, 4 + h, 0:BC * NHI * HEADS].rearrange("p (r t f) -> p r t f", r=BC, f=HEADS)
                        link(vec.tensor_tensor(sel[:, :, :, :].rearrange("p r f t -> p r t f"), ad4, Hm4, ALU.mult))
                        link(vec.tensor_reduce(adu[:, :, :], sel[:, :, :, :], AX.X, ALU.add))
                        v.wait_ge(arows_in[h], lv * ROWS_LEVEL + i * (16 * BC) + 16 * BC)
                        link(vec.scalar_tensor_tensor(ez[:, :, :], adu[:, :, :], sc[:, 5:6], rows[:, h, :, 0:HEADS], ALU.mult, ALU.add),
                             vec.scalar_tensor_tensor(er[:, :, :], adu[:, :, :], sc[:, 5:6], Gk[:, :].unsqueeze(1).to_broadcast([P, BC, HEADS]), ALU.mult, ALU.add))
                        link(vec.scalar_tensor_tensor(ez2[:, :, :], ez[:, :, :], 0.2, ez[:, :, :], ALU.mult, ALU.max),
                             vec.scalar_tensor_tensor(er2[:, :, :], er[:, :, :], 0.2, er[:, :, :], ALU.mult, ALU.max))
                        vec.tensor_tensor(ez[:, :, :], ez2[:, :, :], er2[:, :, :], ALU.subtract).then_inc(e_ready, 1)
                        copy_stage(i * 2 + (h + 1), 1 - h)
                        v.wait_ge(w_ready, i * 2 + (h + 1))
                        link(vec.tensor_tensor(val[:, :, :].rearrange("p r (h e) -> p r h e", e=1 + NX), wexp[:, :, :].unsqueeze(3).to_broadcast([P, BC, HEADS, 1 + NX]),
                                               rows[:, h, :, HEADS:ROWW].rearrange("p r (h e) -> p r h e", e=1 + NX), ALU.mult))
                        v.sem_inc(rows_used, 1)
                        link(vec.tensor_copy(vh[:, :, 0, :], val[:, :, :]))
                        link(vec.tensor_tensor(vh[:, :, 1, :], val[:, :, :], vh[:, :, 0, :], ALU.subtract))
                        for part in range(2):
                            last = vec.tensor_tensor(M[:, h, :, part * HIV:(part + 1) * HIV].rearrange("p r (t f) -> p r t f", f=VAL),
                                                     vh[:, :, part, :].unsqueeze(2).to_broadcast([P, BC, NHI, VAL]),
                                                     Hm[:, :, :].rearrange("p r (t f) -> p r t f", f=VAL), ALU.mult)
                        last.then_inc(spread_ready, 1)
                        v.wait_ge(acc_done, i * 2 + (h + 1))
                        make_S(1 - h)
                link(vec.scalar_tensor_tensor(n4[:, :, :], n1[:, :, :], 0.2, n1[:, :, :], ALU.mult, ALU.max), ops(n2[:, :, :], AD[:, :, :], NTB[:, :, 0:HEADS], ALU.add))
                link(vec.scalar_tensor_tensor(n3[:, :, :], n2[:, :, :], 0.2, n2[:, :, :], ALU.mult, ALU.max))
                link(ops(n2[:, :, :], n3[:, :, :], n4[:, :, :], ALU.subtract))
                link(vec.tensor_copy(n1[:, :, :], n4[:, :, :]))
                v.sem_inc(self_e, 1)
                v.wait_ge(sums_ready, 1)
                link(*[vec.tensor_copy(L[:, :, :].rearrange("p (t j) f -> p j t f", j=NJ)[:, j, :, :], PS[:, j, 0:HIV].rearrange("p (t f) -> p t f", f=VAL)) for j in range(NJ)])
                v.wait_ge(self_w, 1)
                w5 = [P, NTP, HEADS, 1 + NX]
                tmp5 = tmp16[:, :, :].rearrange("p t (h e) -> p t h e", e=1 + NX)
                acc5 = acc[:, :, :].rearrange("p t (h e) -> p t h e", e=1 + NX)
                link(ops(tmp5, n3[:, :, :].unsqueeze(3).to_broadcast(w5), NT5, ALU.mult),
                     vec.tensor_scalar(n4[:, :, :], acc5[:, :, :, 0], 0.0, None, ALU.is_equal))
                link(ops(L[:, :, :], L[:, :, :], tmp16[:, :, :], ALU.add), ops(n2[:, :, :], n1[:, :, :], n4[:, :, :], ALU.mult),
                     vec.tensor_scalar(n3[:, :, :], n4[:, :, :], -1.0, 1.0, ALU.mult, ALU.add))
                link(ops(Rsh[:, :, :], Rsh[:, :, :], n3[:, :, :], ALU.mult))
                link(ops(Rsh[:, :, :], Rsh[:, :, :], n2[:, :, :], ALU.add))
                link(ops(n2[:, :, :], n1[:, :, :], Rsh[:, :, :], ALU.subtract))
                v.sem_inc(mg_ready, 1)
                v.wait_ge(mg_exp, 1)
                link(ops(tmp5, n4[:, :, :].unsqueeze(3).to_broadcast(w5), L[:, :, :].rearrange("p t (h e) -> p t h e", e=1 + NX), ALU.mult),
                     vec.tensor_copy(Gk[:, :], Gk1[:, :]))
                link(ops(acc[:, :, :], acc[:, :, :], tmp16[:, :, :], ALU.add))
                v.sem_inc(level_done, 3)
                v.sem_inc(level_end, 1)
                v.wait_ge(level_go, lv + 1)
                v.sem_inc(dve_go, 1)
            steps = Chain(v, gate_steps)
            link = steps.link
            acc5 = acc[:, :, :].rearrange("p t (h e) -> p t h e", e=1 + NX)
            A4 = A16[:, :, :].rearrange("p t (h e) -> p t h e", e=NX)
            T1 = [P, NTP, HX]
            link(vec.tensor_scalar(rank[:, :, :], acc5[:, :, :, 0], 1.0 / DEN_SCALE, 1e-16, ALU.mult, ALU.add))
            link(vec.reciprocal(pick[:, :, :], rank[:, :, :]))
            link(vec.tensor_scalar(pick[:, :, :], pick[:, :, :], sc[:, 7:8], None, ALU.mult))
            link(ops(A4, acc5[:, :, :, 1:1 + NX], pick[:, :, :].unsqueeze(3).to_broadcast([P, NTP, HEADS, NX]), ALU.mult))
            link(ops(A16[:, :, :], A16[:, :, :], small[:, 2:3, :].to_broadcast(T1), ALU.add))
            link(vec.tensor_reduce(m1[:, :], A16[:, :, :], AX.X, ALU.add))
            link(vec.tensor_scalar(m1[:, :], m1[:, :], 1.0 / HX, None, ALU.mult))
            link(ops(A16[:, :, :], A16[:, :, :], m1[:, :].unsqueeze(2).to_broadcast(T1), ALU.subtract))
            link(ops(B16[:, :, :], A16[:, :, :], A16[:, :, :], ALU.mult))
            link(vec.tensor_reduce(m2[:, :], B16[:, :, :], AX.X, ALU.add))
            link(vec.tensor_scalar(m2[:, :], m2[:, :], 1.0 / HX, None, ALU.mult))
            v.sem_inc(gate_in, 1)
            v.wait_ge(gate_std_r, 1)
            link(vec.reciprocal(m1[:, :], m3[:, :]))
            link(ops(A16[:, :, :], A16[:, :, :], m1[:, :].unsqueeze(2).to_broadcast(T1), ALU.mult))
            link(ops(A16[:, :, :], A16[:, :, :], small[:, 3:4, :].to_broadcast(T1), ALU.mult))
            link(ops(A16[:, :, :], A16[:, :, :], small[:, 4:5, :].to_broadcast(T1), ALU.add))
            link(vec.tensor_reduce(scr4[:, :, :], A16[:, :, :].rearrange("p t (h e) -> p t e h", e=NX), AX.X, ALU.add))
            link(vec.tensor_scalar(scr4[:, :, :], scr4[:, :, :], 1.0 / HEADS, None, ALU.mult))
            link(vec.memset(rank[:, :, :], 0.0))
            for a in range(NX):
                for c in range(a + 1, NX):
                    link(ops(cmp[:, :], scr4[:, :, a], scr4[:, :, c], ALU.is_ge), ops(m3[:, :], scr4[:, :, a], scr4[:, :, c], ALU.is_lt))
                    link(ops(rank[:, :, c], rank[:, :, c], cmp[:, :], ALU.add), ops(rank[:, :, a], rank[:, :, a], m3[:, :], ALU.add))
            for place, to in ((0.0, s1), (1.0, s2)):
                link(vec.tensor_scalar(pick[:, :, :], rank[:, :, :], place, None, ALU.is_equal))
                link(ops(B16[:, :, 0:NX], pick[:, :, :], scr4[:, :, :], ALU.mult))
                link(vec.tensor_reduce(to[:, :], B16[:, :, 0:NX], AX.X, ALU.add))
            link(ops(cmp[:, :], s2[:, :], s1[:, :], ALU.subtract))
            v.sem_inc(gate_in, 1)
            v.wait_ge(gate_exp, 1)
            link(vec.tensor_scalar(m1[:, :], dexp[:, :], 1.0, None, ALU.add))
            link(vec.reciprocal(m2[:, :], m1[:, :]))
            link(ops(m3[:, :], m2[:, :], dexp[:, :], ALU.mult), vec.tensor_scalar(pick[:, :, :], rank[:, :, :], 0.0, None, ALU.is_equal),
                 vec.tensor_scalar(scr4[:, :, :], rank[:, :, :], 1.0, None, ALU.is_equal))
            link(ops(pick[:, :, :], pick[:, :, :], m2[:, :].unsqueeze(2).to_broadcast([P, NTP, NX]), ALU.mult),
                 ops(scr4[:, :, :], scr4[:, :, :], m3[:, :].unsqueeze(2).to_broadcast([P, NTP, NX]), ALU.mult))
            link(ops(gate[:, :].rearrange("p (t e) -> p t e", e=NX), pick[:, 0:NT, :], scr4[:, 0:NT, :], ALU.add),
                 vec.memset(ones1[:, :], 1.0))
            v.sem_inc(gates_ready, 1)
            v.wait_ge(b1_turned, 1)
            link(vec.tensor_copy(b1T[:, :], PS[:, 7, 0:NE_X * HID // P]))
            v.sem_inc(exp_ready, 2)
            v.sem_inc(o_used, 2)

            def gated(base, tile0, nt):
                for e in range(NE_X):
                    v.wait_ge(o_mm, base * 4 + (e + 1))
                    for t in range(nt):
                        at = X3[:, ds(tile0 + t, 1), :].rearrange("p a d -> p (a d)")
                        last = vec.scalar_tensor_tensor(at, PS[:, 4 + 2 * (e % 2) + t // 2, (t % 2) * D:(t % 2 + 1) * D],
                                                        gate[:, ds((tile0 + t) * NX + e, 1)], at, ALU.mult, ALU.add)
                    last.then_inc(o_used, 1)
                    v.wait_ge(o_used, base * 4 + (e + 3))

            with v.Fori(0, NT // NJ) as i:
                gated(i, i * NJ, NJ)
            gated(NT // NJ, (NT // NJ) * NJ, 1)


_INS = ['x', 'src', 'dst', 'L0_gnn_W', 'L0_gnn_b', 'L0_ffn_W_gat', 'L0_ffn_att_src', 'L0_ffn_att_dst', 'L0_ffn_b_gat',
        'L0_ffn_ln_gamma', 'L0_ffn_ln_beta', 'L0_ffn_W1', 'L0_ffn_b1', 'L0_ffn_W2', 'L0_ffn_b2', 'L0_ffn_edge_index']
_OUTS = [((6250, 256), 'float32')]


def kernel(**inputs):
    import numpy as _np
    import concourse.bacc as _bacc
    from concourse import mybir as _mybir
    from concourse.bass_utils import run_bass_kernel_spmd as _run

    nc = _bacc.Bacc("TRN2", target_bir_lowering=False, num_devices=1)
    arrays, args = {}, []
    for name in _INS:
        a = _np.ascontiguousarray(inputs[name])
        arrays[f"in_{name}_dram"] = a
        args.append(nc.dram_tensor(f"in_{name}_dram", a.shape, _mybir.dt.from_np(a.dtype), kind="ExternalInput").ap())
    for i, (shape, dtype) in enumerate(_OUTS):
        dt = _mybir.dt.from_np(_np.dtype(dtype))
        args.append(nc.dram_tensor(f"out_{i}_dram", shape, dt, kind="ExternalOutput").ap())
    gnn_moe(nc, *args)
    r = _run(nc, [arrays], core_ids=[0])
    got = tuple(r.results[0][f"out_{i}_dram"] for i in range(len(_OUTS)))
    return got[0]
```

```python
from contextlib import ExitStack, contextmanager

import numpy as np

import concourse.bass as bass
from concourse import mybir

F32 = mybir.dt.float32
F16 = mybir.dt.float16
I32 = mybir.dt.int32
ALU = mybir.AluOpType
ACT = mybir.ActivationFunctionType
AX = mybir.AxisListType
RED = bass.bass_isa.ReduceOp
ds = bass.ds

P = 128
D = 256
EPS = 1e-5

CH = 16
GROUP = CH * P
AGW = D + 1
TAB_SCALE = 1024.0

HEADS, NX = 4, 4
HX = HEADS * NX
XSCALE = 1024.0
LO = 512
NJ = LO // P
BC = 8
ROWW = HEADS + HEADS * (1 + NX)
VAL = HEADS * (1 + NX)
LEVEL = 8.0
DEN_SCALE = 4096.0
FULL = 16384.0
BIG = 1e30
HID = 512


class Chain:

    def __init__(self, eng, sem):
        self.eng, self.sem, self.base, self.n = eng, sem, 0, 0

    def link(self, *instructions):
        self.mark(*instructions)
        self.catch()

    def mark(self, *instructions):
        instructions[-1].then_inc(self.sem, 1)
        self.n += 1

    def catch(self):
        self.eng.wait_ge(self.sem, self.base + self.n)

    @contextmanager
    def loop(self, count, steps):
        base, n = self.base, self.n
        with self.eng.Fori(0, count) as i:
            self.base, self.n = i * steps + (base + n), 0
            yield i
            assert self.n == steps, (self.n, steps)
        self.base, self.n = base, n + count * steps


def gnn_moe(nc, x, src, dst, W, b, W_gat, att_src, att_dst, b_gat, ln_g, ln_b, W1, b1, W2, b2, edges, out):
    N = x.shape[0]
    NT = -(-N // P)
    LAST = N - (NT - 1) * P
    NE = src.shape[0]
    NG = -(-NE // GROUP)
    TAIL = NE - (NG - 1) * GROUP
    NA = edges.shape[1]
    NB = NA // (BC * P)
    NHI = -(-N // LO)
    NTP = NHI * NJ
    HIV = NHI * VAL
    NE_X = W1.shape[0]
    PADN = NT * P - 1
    LOB_LEVEL = 16 * (NB // 2 + 1)
    ROWS_LEVEL = 16 * BC * NB // 2
    BT = 7
    assert NT % BT == 0 and NG % 2 == 0 and NB % 2 == 0 and NA % (BC * P) == 0
    WSTEP = -(-(2 * NE_X * HID - 1) // (NT // BT))
    assert WSTEP * (NT // BT) + 1 == 2 * NE_X * HID
    BATCHES = ((0, 4), (4, 3))

    table = nc.dram_tensor("ln_table", (NT * P, 2 * D), F16, kind="Internal").ap()
    lo_rows = nc.dram_tensor("lo_rows", (NB + 2, BC * P), F16, kind="Internal").ap()
    atable = nc.dram_tensor("att_table", (NTP * P, ROWW), F32, kind="Internal").ap()

    with ExitStack() as ctx:
        def sb(name, shape, dt, where=ctx):
            return where.enter_context(nc.sbuf_tensor(name, shape, dt))

        def sem(name):
            return ctx.enter_context(nc.semaphore(name))

        X = sb("X", [P, NT * D], F32)
        AG = sb("AG", [P, (NT + 1) * AGW], F32)
        identf = sb("identf", [P, P], F32)
        identh = sb("identh", [P, P], F16)
        H = sb("H", [P, NTP, HX], F32)
        acc = sb("acc", [P, NTP, VAL], F32)
        sc = sb("sc", [P, 16], F32)
        g0 = ExitStack()
        lohi = sb("lohi", [P, NB + 1, 2, BC], F32, g0)
        asrc_idx = sb("asrc_idx", [P, NB + 2, BC], I32, g0)
        g0_end = nc.sbuf_base
        g0.close()
        A16 = sb("A16", [P, NTP, HX], F32)
        B16 = sb("B16", [P, NTP, HX], F32)
        m1 = sb("m1", [P, NTP], F32)
        m2 = sb("m2", [P, NTP], F32)
        m3 = sb("m3", [P, NTP], F32)
        scr4 = sb("scr4", [P, NTP, NX], F32)
        rank = sb("rank", [P, NTP, NX], F32)
        cmp = sb("cmp", [P, NTP], F32)
        pick = sb("pick", [P, NTP, NX], F32)
        s1 = sb("s1", [P, NTP], F32)
        s2 = sb("s2", [P, NTP], F32)
        dexp = sb("dexp", [P, NTP], F32)
        assert nc.sbuf_base < g0_end
        rest_of_edges = sb("rest_of_edges", [P, g0_end - nc.sbuf_base], mybir.dt.uint8)
        iota_lo = sb("iota_lo", [P, LO], F16)
        minus_node = sb("minus_node", [P, NJ], F32)
        consts = sb("consts", [P, 8], F32)
        W_sb = sb("W_sb", [P, 2, D], F32)
        WT = sb("WT", [P, 2, D], F32)
        Wg = sb("Wg", [P, 2, HX], F32)
        b_bc = sb("b_bc", [P, D], F32)
        wmax = sb("wmax", [P, 3], F32)
        esc = sb("esc", [P, 12], F32)
        small = sb("small", [P, 5, HX], F32)
        stats = sb("stats", [P, BT, 6], F32)
        mv = sb("mv", [P, BT, 2], F32)
        std = sb("std", [P, BT], F32)
        rstd = sb("rstd", [P, BT], F32)
        shift = sb("shift", [P, BT], F32)
        scratch = nc.sbuf_base

        g1 = ExitStack()
        ring = sb("ring", [P, 2 * CH, 2 * D + 2], F16, g1)
        OH = sb("OH", [P, CH, 2 * P], F16, g1)
        drel_all = sb("drel_all", [P, NG * CH], F32, g1)
        sidx_all = sb("sidx_all", [P, NG * CH], I32, g1)
        drelw = sb("drelw", [P, CH], F32, g1)
        sstage = sb("sstage", [P, 2 * CH], I32, g1)
        info = sb("info", [1, 4 * NG], I32, g1)
        cols = sb("cols", [P, 16], I32, g1)
        colf = sb("colf", [P, 16], F32, g1)
        tri = sb("tri", [P, NG + 1], F32, g1)
        nat = ring[:, :, :].rearrange("p a b -> p (a b)").bitcast(F32)
        srcf = nat[0:NG, 0:GROUP]
        dstf = nat[0:NG, GROUP:2 * GROUP]
        srcn = nat[:, 2 * GROUP:3 * GROUP].bitcast(I32)
        dstn = nat[:, 3 * GROUP:4 * GROUP].bitcast(I32)
        tstage = sb("tstage", [P, BT, 2 * D], F16, g1)
        xs = sb("xs", [P, BT, D], F32, g1)
        g1.close()

        g2 = ExitStack()
        y = sb("y", [P, BT, D], F32, g2)
        yT = sb("yT", [P, BT, 2, P], F32, g2)
        xnb = sb("xnb", [P, BT, D], F32, g2)
        xT = sb("xT", [P, BT, 2, P], F32, g2)
        dgs = sb("dgs", [P, 4, BT], F32, g2)
        W1_see = sb("W1_see", [P, 2 * NE_X * HID], F32, g2)
        W2_see = sb("W2_see", [P, 2 * NE_X * HID], F32, g2)
        b1_see = sb("b1_see", [NE_X * HID // P, P], F32, g2)
        wtmp = sb("wtmp", [P, 2], F32, g2)
        g2.close()

        g3 = ExitStack()
        S = sb("S", [P, 2, BC, LO], F16, g3)
        lob = sb("lob", [P, 2, BC * P], F16, g3)
        ST = sb("ST", [P, 2, NJ, BC * P], F16, g3)
        Hm = sb("Hm", [P, BC, HIV], F16, g3)
        M = sb("M", [P, 2, BC, 2 * HIV], F16, g3)
        iota_hi = sb("iota_hi", [P, HIV], F16, g3)
        zero_l = sb("zero_l", [P, P], F16, g3)
        rows = sb("rows", [P, 2, BC, ROWW], F32, g3)
        estage = sb("estage", [P, 2, 2 * BC], F32, g3)
        istage = sb("istage", [P, 2 * BC], I32, g3)
        sel = sb("sel", [P, BC, HEADS, NHI], F32, g3)
        adu = sb("adu", [P, BC, HEADS], F32, g3)
        ez = sb("ez", [P, BC, HEADS], F32, g3)
        ez2 = sb("ez2", [P, BC, HEADS], F32, g3)
        er = sb("er", [P, BC, HEADS], F32, g3)
        er2 = sb("er2", [P, BC, HEADS], F32, g3)
        wexp = sb("wexp", [P, BC, HEADS], F32, g3)
        val = sb("val", [P, BC, VAL], F32, g3)
        vh = sb("vh", [P, BC, 2, VAL], F16, g3)
        Tad = sb("Tad", [P, 2, NJ, NHI, HEADS], F16, g3)
        AS = sb("AS", [P, NTP, HEADS], F32, g3)
        AD = sb("AD", [P, NTP, HEADS], F32, g3)
        ADs = sb("ADs", [P, NTP, HEADS], F32, g3)
        NTB = sb("NTB", [P, NTP, ROWW], F32, g3)
        n1 = sb("n1", [P, NTP, HEADS], F32, g3)
        n2 = sb("n2", [P, NTP, HEADS], F32, g3)
        n3 = sb("n3", [P, NTP, HEADS], F32, g3)
        n4 = sb("n4", [P, NTP, HEADS], F32, g3)
        Rsh = sb("Rsh", [P, NTP, HEADS], F32, g3)
        ext = sb("ext", [P, 16], F32, g3)
        extr = sb("extr", [P, 16], F32, g3)
        Gk = sb("Gk", [P, HEADS], F32, g3)
        Gk1 = sb("Gk1", [P, HEADS], F32, g3)
        nlev = sb("nlev", [P, 1], I32, g3)
        g3.close()
        SF = S[:, :, :, :].rearrange("p a r n -> p (a r n)").bitcast(F32)
        L = SF[:, 0:NTP * VAL].rearrange("p (t f) -> p t f", f=VAL)
        tmp16 = SF[:, NTP * VAL:2 * NTP * VAL].rearrange("p (t f) -> p t f", f=VAL)

        g4 = ExitStack()
        W1h = sb("W1h", [P, 2, 2, NE_X, HID], F16, g4)
        W2h = sb("W2h", [P, 2, NE_X, HID // P, D], F16, g4)
        b1n = sb("b1n", [NE_X * HID // P, P], F32, g4)
        b1T = sb("b1T", [P, NE_X * HID // P], F32, g4)
        b2_bc = sb("b2_bc", [P, NE_X * D], F32, g4)
        hh_base = nc.sbuf_base
        hh = sb("hh", [P, 2, 2, HID // P, LO], F16, g4)
        hh32 = sb("hh32", [P, HID // P, LO], F32, g4)
        wstage_rest = sb("wstage_rest", [P, HID // P, LO], F32, g4)
        gate = sb("gate", [P, NT * NX], F32, g4)
        gates = sb("gates", [P, NT * NX], F32, g4)
        g4.close()
        g4 = ExitStack()
        sb("below_wstage", [P, hh_base - -(-scratch // 32) * 32], mybir.dt.uint8, g4)
        wstage1 = sb("wstage1", [P, 2, NE_X, HID], F32, g4)
        wstage2 = sb("wstage2", [P, NE_X, HID // P, D], F32, g4)
        g4.close()
        PS = ctx.enter_context(nc.psum_tensor("PS", [P, 8, 512], F32))

        pads_set = sem("pads_set")
        x_loaded = sem("x_loaded")
        edges_loaded = sem("edges_loaded")
        edges2_loaded = sem("edges2_loaded")
        small_loaded = sem("small_loaded")
        tslot_free = sem("tslot_free")
        lo_ready = sem("lo_ready")
        table_stored = sem("table_stored")
        ext_reduced = sem("ext_reduced")
        nlev_ready = sem("nlev_ready")
        atable_ready = sem("atable_ready")
        atable_stored = sem("atable_stored")
        level_end = sem("level_end")
        level_go = sem("level_go")
        exp_loaded = sem("exp_loaded")
        o_used = sem("o_used")
        stored = sem("stored")
        pool_steps = sem("pool_steps")
        iotas_ready = sem("iotas_ready")
        staged = sem("staged")
        pool_go = sem("pool_go")
        xT_ready = sem("xT_ready")
        xh_kept = sem("xh_kept")
        gnn_done = sem("gnn_done")
        see_loaded = sem("see_loaded")
        w_split = sem("w_split")
        hi_hid = sem("hi_hid")
        bias_added = sem("bias_added")
        hid32_ready = sem("hid32_ready")
        ext_ready = sem("ext_ready")
        iota_hi_ready = sem("iota_hi_ready")
        estaged = sem("estaged")
        att_go = sem("att_go")
        stats_ready = sem("stats_ready")
        std_ready = sem("std_ready")
        rstd_ready = sem("rstd_ready")
        hi_ready = sem("hi_ready")
        idx_ready = sem("idx_ready")
        win_done = sem("win_done")
        scales_ready = sem("scales_ready")
        y_ready = sem("y_ready")
        yT_turned = sem("yT_turned")
        yT_ready = sem("yT_ready")
        node_stats = sem("node_stats")
        node_std = sem("node_std")
        xn_turned = sem("xn_turned")
        turned = sem("turned")
        lev_ready = sem("lev_ready")
        e_ready = sem("e_ready")
        w_ready = sem("w_ready")
        self_e = sem("self_e")
        self_w = sem("self_w")
        mg_ready = sem("mg_ready")
        mg_exp = sem("mg_exp")
        level_done = sem("level_done")
        act_go = sem("act_go")
        gate_in = sem("gate_in")
        gate_std_r = sem("gate_std_r")
        gate_exp = sem("gate_exp")
        exp_ready = sem("exp_ready")
        h_mm = sem("h_mm")
        hid_ready = sem("hid_ready")
        nat_ready = sem("nat_ready")
        nat_turned = sem("nat_turned")
        nat_evacuated = sem("nat_evacuated")
        info_turned = sem("info_turned")
        ef_ready = sem("ef_ready")
        ef_turned = sem("ef_turned")
        info_ready = sem("info_ready")
        wt_turned = sem("wt_turned")
        prep_done = sem("prep_done")
        agg_done = sem("agg_done")
        oh_ready = sem("oh_ready")
        mm_done = sem("mm_done")
        xn_ready = sem("xn_ready")
        h_done = sem("h_done")
        ad_done = sem("ad_done")
        acc_done = sem("acc_done")
        sums_ready = sem("sums_ready")
        pe_go = sem("pe_go")
        b1_turned = sem("b1_turned")
        o_mm = sem("o_mm")
        prep_steps = sem("prep_steps")
        info_zeroed = sem("info_zeroed")
        win_steps = sem("win_steps")
        drel_ready = sem("drel_ready")
        node_steps = sem("node_steps")
        att_steps = sem("att_steps")
        level_steps = sem("level_steps")
        dve_go = sem("dve_go")
        gate_steps = sem("gate_steps")
        sp_go = sem("sp_go")
        away_ready = sem("away_ready")
        rows_used = sem("rows_used")
        loh_ready = sem("loh_ready")
        lo_stored = sem("lo_stored")
        lob_in = [sem(f"lob_in{h}") for h in range(2)]
        turned_kept = sem("turned_kept")
        lo_hot_ready = sem("lo_hot_ready")
        spread_ready = sem("spread_ready")
        rows_in = [sem(f"rows_in{h}") for h in range(2)]
        arows_in = [sem(f"arows_in{h}") for h in range(2)]
        LEVEL_SEMS = [away_ready, rows_used, turned_kept, lo_hot_ready, spread_ready, estaged, att_go, turned, lev_ready, e_ready, w_ready, self_e, self_w, mg_ready, mg_exp, level_done, ad_done, acc_done, sums_ready, level_steps]
        block = ctx.enter_context(nc.Block())
        x_t = x[0:(NT - 1) * P, :].rearrange("(t p) d -> p t d", p=P)
        out_t = out[0:(NT - 1) * P, :].rearrange("(t p) d -> p t d", p=P)
        X3 = X[:, :].rearrange("p (t d) -> p t d", d=D)
        AG3 = AG[:, :].rearrange("p (t n) -> p t n", n=AGW)
        AGh = AG[:, :].bitcast(F16).rearrange("p (t n) -> p t n", n=2 * AGW)
        PSF = PS[:, :, :].rearrange("p a b -> p (a b)")

        YT, XNT, PROD = 0, 1024, (2048, 3072)
        HOUT = XNT

        def node_phase(eng, chain, steps, prologue, body, epilogue):
            prologue()
            body(0, 0, True, False)
            body(0, 1, False, False)
            if chain is None:
                with eng.Fori(1, NT // BT - 1) as i:
                    body(i, 0, False, False)
                    body(i, 1, False, False)
            else:
                with chain.loop(NT // BT - 2, steps) as j:
                    body(j + 1, 0, False, False)
                    body(j + 1, 1, False, False)
            body(NT // BT - 1, 0, False, False, no_after_next=True)
            body(NT // BT - 1, 1, False, True, no_after_next=True)
            epilogue()

        def tile_of(i, k):
            return X3[:, ds(i * BT + k, 1), :].rearrange("p a d -> p (a d)")

        table_t = table.rearrange("(t p) w -> p t w", p=P)
        atable_t = atable.rearrange("(t p) w -> p t w", p=P)

        AGf = AG[:, :]
        en = AGf[:, 0:2 * BC * P].bitcast(I32)
        eni = AGf[:, 2 * BC * P:4 * BC * P].bitcast(I32)
        ef = AGf[:, 4 * BC * P:7 * BC * P]
        E1 = BC * P
        loh = AGf[:, 7 * BC * P:7 * BC * P + BC * P // 2].bitcast(F16)

        def w_chunk(c):
            if c < 4:
                k, e = c // 2, c % 2 * 2
                return W1h[:, 0, k, e:e + 2, :], W1h[:, 1, k, e:e + 2, :], wstage1[:, k, e:e + 2, :], 0
            return W2h[:, 0, c - 4, :, :], W2h[:, 1, c - 4, :, :], wstage2[:, c - 4, :, :], 1

        def bcast(dram_row, n):
            return dram_row.to_broadcast([P, n])

        def flat(a):
            return a.rearrange("(a n) -> a n", a=1)

        @block.sync
        def _(sp):
            sp.wait_ge(pads_set, 2)
            sp.dma_start(X3[0:LAST, NT - 1, :], x[(NT - 1) * P:N, :]).then_inc(x_loaded, 16)
            for a in range(4):
                q = (NT - 1) // 4
                sp.dma_start(X3[:, a * q:(a + 1) * q, :], x_t[:, a * q:(a + 1) * q, :]).then_inc(x_loaded, 16)
            for nat_t, e in ((srcn, src), (dstn, dst)):
                sp.dma_start(nat_t[0:NG - 1, :], e[0:(NG - 1) * GROUP].rearrange("(g e) -> g e", e=GROUP)).then_inc(edges_loaded, 16)
                sp.dma_start(nat_t[NG - 1:NG, 0:TAIL], flat(e[(NG - 1) * GROUP:NE])).then_inc(edges_loaded, 16)
            for a in range(2):
                sp.dma_start(en[:, a * E1:(a + 1) * E1], edges[a:a + 1, :].rearrange("a (q e) -> (a q) e", e=E1)).then_inc(edges2_loaded, 16)
            sp.dma_start(W_sb[:, :, :], W.rearrange("(a p) i -> p a i", p=P)).then_inc(small_loaded, 16)
            sp.dma_start(Wg[:, :, :], W_gat.rearrange("(k p) c -> p k c", p=P)).then_inc(small_loaded, 16)
            sp.dma_start(b_bc[:, :], bcast(flat(b), D)).then_inc(small_loaded, 16)
            for a, row in enumerate((att_src.rearrange("h e -> (h e)"), att_dst.rearrange("h e -> (h e)"), b_gat, ln_g, ln_b)):
                sp.dma_start(small[:, a, :], bcast(flat(row), HX)).then_inc(small_loaded, 16)
            sp.sem_inc(tslot_free, 1)
            with sp.Fori(0, NT // BT) as i:
                for h, (k0, nk) in enumerate(BATCHES):
                    sp.wait_ge(lo_ready, i * 2 + (h + 1))
                    sp.dma_start(table_t[:, ds(i * BT + k0, nk), :], tstage[:, k0:k0 + nk, :]).then_inc(table_stored, 16)
                sp.wait_ge(table_stored, i * 32 + 32)
                sp.sem_inc(tslot_free, 1)
            sp.wait_ge(loh_ready, 1)
            sp.dma_start(lo_rows[0:NB, :], loh[:, :]).then_inc(lo_stored, 16)
            sp.dma_start(lo_rows[NB:NB + 2, :], loh[0:2, :]).then_inc(lo_stored, 16)
            sp.wait_ge(lo_stored, 32)
            sp.wait_ge(gnn_done, 1)
            for k in range(2):
                sp.dma_start(W1_see[:, k * NE_X * HID:(k + 1) * NE_X * HID].rearrange("p (e n) -> p e n", e=NE_X),
                             W1[:, k * P:(k + 1) * P, :].rearrange("e p n -> p e n")).then_inc(see_loaded, 16)
            for e in range(NE_X):
                sp.dma_start(W2_see[:, e * 4 * D:(e + 1) * 4 * D].rearrange("p (c n) -> p c n", n=D),
                             W2[e, :, :].rearrange("(c p) n -> p c n", p=P)).then_inc(see_loaded, 16)
            sp.dma_start(b1_see[:, :], b1.rearrange("e (c p) -> (e c) p", p=P)).then_inc(see_loaded, 16)
            sp.wait_ge(ext_reduced, 1)
            sp.wait_ge(nlev_ready, 1)
            levels = sp.value_load(nlev[0:1, 0:1], min_val=1, max_val=1 << 17)
            with sp.Fori(0, levels) as lv:
                sp.dma_start(lob[:, 0, :], bcast(lo_rows[0:1, :], BC * P)).then_inc(lob_in[0], 16)
                sp.dma_start(lob[:, 1, :], bcast(lo_rows[1:2, :], BC * P)).then_inc(lob_in[1], 16)
                sp.wait_ge(atable_ready, lv + 1)
                sp.dma_start(atable_t, NTB[:, :, :]).then_inc(atable_stored, 16)
                with sp.Fori(0, NB // 2) as i:
                    for h in range(2):
                        sp.wait_ge(away_ready, i * 2 + (h + 1))
                        sp.dma_start(lob[:, h, :], bcast(lo_rows[ds(i * 2 + (h + 2), 1), :], BC * P)).then_inc(lob_in[h], 16)
                for h in range(2):
                    sp.wait_ge(lob_in[h], lv * LOB_LEVEL + LOB_LEVEL)
                sp.wait_ge(level_end, lv * 4 + 4)
                sp.sem_inc(sp_go, 1)
                for q in LEVEL_SEMS:
                    sp.sem_clear(q)
                sp.sem_inc(level_go, 1)
            for k in range(2):
                sp.dma_start(wstage1[:, k, :, :], W1[:, k * P:(k + 1) * P, :].rearrange("e p n -> p e n")).then_inc(exp_loaded, 16)
            for e in range(NE_X):
                sp.dma_start(wstage2[:, e, :, :], W2[e, :, :].rearrange("(c p) n -> p c n", p=P)).then_inc(exp_loaded, 16)
            sp.dma_start(b1n[:, :], b1.rearrange("e (c p) -> (e c) p", p=P)).then_inc(exp_loaded, 16)
            sp.dma_start(b2_bc[:, :], bcast(flat(b2.rearrange("e n -> (e n)")), NE_X * D)).then_inc(exp_loaded, 16)
            with sp.Fori(0, NT // NJ) as i:
                sp.wait_ge(o_used, i * 4 + 6)
                sp.dma_start(out_t[:, ds(i * NJ, NJ), :], X3[:, ds(i * NJ, NJ), :]).then_inc(stored, 16)
            sp.wait_ge(o_used, (NT // NJ) * 4 + 6)
            sp.dma_start(out[(NT - 1) * P:N, :], X3[0:LAST, NT - 1, :]).then_inc(stored, 16)
            sp.wait_ge(stored, 16 * (NT // NJ + 1))

        @block.gpsimd
        def _(pool):
            steps = Chain(pool, pool_steps)
            steps.link(nc.gpsimd.memset(identf[:, :], 0.0), nc.gpsimd.memset(identh[:, :], 0.0), nc.gpsimd.memset(tri[:, :], 0.0))
            nc.gpsimd.affine_select(out=identf[:, :], in_=identf[:, :], compare_op=ALU.not_equal, fill=1.0, base=0,
                                    pattern=[[-1, P]], channel_multiplier=1)
            nc.gpsimd.affine_select(out=identh[:, :], in_=identh[:, :], compare_op=ALU.not_equal, fill=1.0, base=0,
                                    pattern=[[-1, P]], channel_multiplier=1)
            nc.gpsimd.affine_select(out=tri[:, :], in_=tri[:, :], compare_op=ALU.is_ge, fill=1.0, base=0,
                                    pattern=[[-1, NG + 1]], channel_multiplier=1)
            nc.gpsimd.iota(minus_node[:, :], [[-P, NJ]], base=0, channel_multiplier=-1, allow_small_or_imprecise_dtypes=True)
            nc.gpsimd.iota(iota_lo[:, :], [[1, LO]], base=0, channel_multiplier=0,
                           allow_small_or_imprecise_dtypes=True).then_inc(iotas_ready, 1)
            with pool.Fori(0, NG // 2) as i:
                for h in range(2):
                    pool.wait_ge(staged, i * 2 + (h + 1))
                    pool.sem_inc(pool_go, 1)
                    pool.wait_ge(table_stored, 32 * (NT // BT))
                    for k in range(h * CH, (h + 1) * CH):
                        pool.indirect_dma_start(ring[:, k, 0:2 * D], None, table,
                                                bass.IndirectOffsetOnAxis(ap=sstage[:, k:k + 1], axis=0)).then_inc(rows_in[h], 16)
            pool.wait_ge(ext_ready, 1)
            nc.gpsimd.partition_all_reduce(extr[:, :], ext[:, :], P, RED.max).then_inc(ext_reduced, 1)
            nc.gpsimd.iota(iota_hi[:, :], [[1, NHI], [0, VAL]], base=0, channel_multiplier=0,
                           allow_small_or_imprecise_dtypes=True).then_inc(iota_hi_ready, 1)
            pool.wait_ge(nlev_ready, 1)
            levels = pool.value_load(nlev[0:1, 0:1], min_val=1, max_val=1 << 17)
            with pool.Fori(0, levels) as lv:
                pool.wait_ge(atable_stored, lv * 16 + 16)
                pool.sem_inc(pool_go, 1)
                with pool.Fori(0, NB // 2) as i:
                    for h in range(2):
                        pool.wait_ge(estaged, i * 2 + (h + 1))
                        pool.sem_inc(att_go, 1)
                        pool.wait_ge(iota_hi_ready, 1)
                        for k in range(BC):
                            pool.indirect_dma_start(rows[:, h, k, :], None, atable,
                                                    bass.IndirectOffsetOnAxis(ap=istage[:, h * BC + k:h * BC + k + 1], axis=0)).then_inc(arows_in[h], 16)
                for h in range(2):
                    pool.wait_ge(arows_in[h], lv * ROWS_LEVEL + ROWS_LEVEL)
                pool.sem_inc(level_end, 1)
                pool.wait_ge(level_go, lv + 1)
                pool.sem_inc(pool_go, 1)

        @block.scalar
        def _(act):
            act.wait_ge(pads_set, 2)
            with act.Fori(0, NT // BT) as i:
                for h, (k0, nk) in enumerate(BATCHES):
                    act.wait_ge(stats_ready, i * 2 + (h + 1))
                    nc.scalar.activation(std[:, k0:k0 + nk], mv[:, k0:k0 + nk, 1], ACT.Sqrt, bias=consts[:, 0:1]).then_inc(std_ready, 1)
                    act.wait_ge(rstd_ready, i * 2 + (h + 1))
                    if h == 0:
                        act.wait_ge(tslot_free, i + 1)
                    act.wait_ge(pads_set, 2)
                    for k in range(k0, k0 + nk):
                        last = nc.scalar.activation(tstage[:, k, D:2 * D], X3[:, ds(i * BT + k, 1), :].rearrange("p a d -> p (a d)"), ACT.Identity,
                                                    bias=shift[:, k:k + 1], scale=rstd[:, k:k + 1])
                    last.then_inc(hi_ready, 1)
            act.wait_ge(idx_ready, 1)
            with act.Fori(0, NG // 2) as i:
                for h in range(2):
                    before = act.value_load(info[0:1, ds(i * 2 + (NG + 2 + h), 1)], min_val=0, max_val=32 * NG)
                    act.wait_ge(win_done, before + 1)
                    act.wait_ge(idx_ready, 1)
                    nc.scalar.copy(sstage[:, h * CH:(h + 1) * CH], sidx_all[:, ds((i * 2 + h) * CH, CH)]).then_inc(staged, 1)
            def mean_rows(i, h):
                k0, nk = BATCHES[h]
                act.wait_ge(scales_ready, i * 2 + (h + 1))
                act.wait_ge(idx_ready, 1)
                for k in range(k0, k0 + nk):
                    last = nc.scalar.activation(y[:, k, :], AG[:, ds((i * BT + k) * AGW, D)], ACT.Copy, scale=dgs[:, 2, k:k + 1])
                last.then_inc(y_ready, 1)

            def keep_yT(i, h):
                k0, nk = BATCHES[h]
                act.wait_ge(yT_turned, i * 2 + (h + 1))
                nc.scalar.copy(yT[:, k0:k0 + nk, :, :].rearrange("p k a n -> p (k a n)"), PSF[:, YT:YT + nk * D]).then_inc(yT_ready, 1)

            def body(i, h, first, last, no_after_next=False):
                k0, nk = BATCHES[h]
                if not last:
                    keep_yT(i + h, 1 - h)
                act.wait_ge(node_stats, i * 2 + (h + 1))
                nc.scalar.activation(std[:, k0:k0 + nk], mv[:, k0:k0 + nk, 1], ACT.Sqrt, bias=consts[:, 1:2], scale=XSCALE ** -2).then_inc(node_std, 1)
                if not no_after_next:
                    mean_rows(i + 1, h)
                act.wait_ge(xn_turned, i * 2 + (h + 1))
                turned_rows = PSF[:, XNT:XNT + nk * D]
                nc.scalar.copy(xT[:, k0:k0 + nk, :, :].rearrange("p k a n -> p (k a n)"), turned_rows).then_inc(xT_ready, 1)
                nc.scalar.copy(AGh[:, ds(i * BT + k0, nk), 0:D], turned_rows.rearrange("p (k n) -> p k n", n=D)).then_inc(xh_kept, 1)

            def prologue():
                mean_rows(0, 0)
                mean_rows(0, 1)
                keep_yT(0, 0)

            node_phase(act, None, 0, prologue, body, lambda: None)
            act.wait_ge(nlev_ready, 1)
            levels = act.value_load(nlev[0:1, 0:1], min_val=1, max_val=1 << 17)
            with act.Fori(0, levels) as lv:

                def stage_rows(q, h):
                    nc.scalar.copy(istage[:, h * BC:(h + 1) * BC],
                                   asrc_idx[:, ds(q, 1), :].rearrange("p a r -> p (a r)")).then_inc(estaged, 1)

                def one_hot_columns(h):
                    for j in range(NJ):
                        last = nc.scalar.activation(ST[:, h, j, :], lob[:, h, :], ACT.Abs, bias=minus_node[:, j:j + 1])
                    last.then_inc(away_ready, 1)

                def cut(h):
                    flat_st = ST[:, h, :, :].rearrange("p j e -> p (j e)")
                    nc.scalar.activation(flat_st, flat_st, ACT.Relu, bias=1.0, scale=-1.0).then_inc(turned_kept, 1)

                act.wait_ge(nlev_ready, 1)
                stage_rows(0, 0)
                stage_rows(1, 1)
                for h in range(2):
                    act.wait_ge(lob_in[h], lv * LOB_LEVEL + 16)
                    one_hot_columns(h)
                    act.wait_ge(away_ready, h + 1)
                    cut(h)
                with act.Fori(0, NB // 2) as i:
                    for h in range(2):
                        act.wait_ge(e_ready, i * 2 + (h + 1))
                        nc.scalar.activation(wexp[:, :, :], ez[:, :, :], ACT.Exp).then_inc(w_ready, 1)
                        act.wait_ge(lob_in[h], lv * LOB_LEVEL + i * 16 + 32)
                        act.wait_ge(ad_done, i * 2 + (h + 1))
                        one_hot_columns(h)
                        act.wait_ge(rows_used, i * 2 + (h + 1))
                        act.wait_ge(lev_ready, 1)
                        stage_rows(i * 2 + (h + 2), h)
                        act.wait_ge(away_ready, i * 2 + (h + 3))
                        cut(h)
                act.wait_ge(self_e, 1)
                nc.scalar.activation(n3[:, :, :], n2[:, :, :], ACT.Exp).then_inc(self_w, 1)
                act.wait_ge(mg_ready, 1)
                nc.scalar.activation(n4[:, :, :], n2[:, :, :], ACT.Exp).then_inc(mg_exp, 1)
                act.wait_ge(level_done, 1)
                act.sem_inc(level_end, 1)
                act.wait_ge(level_go, lv + 1)
                act.sem_inc(act_go, 1)
            act.wait_ge(gate_in, 1)
            nc.scalar.activation(m3[:, :], m2[:, :], ACT.Sqrt, bias=consts[:, 0:1]).then_inc(gate_std_r, 1)
            act.wait_ge(gate_in, 2)
            nc.scalar.activation(dexp[:, :], cmp[:, :], ACT.Exp).then_inc(gate_exp, 1)
            act.wait_ge(exp_ready, 1)
            act.wait_ge(exp_loaded, 16 * (2 + NE_X + 2))
            for c in range(8):
                hi, lo, st, a = w_chunk(c)
                nc.scalar.activation(hi, st, ACT.Copy, scale=esc[:, a:a + 1]).then_inc(w_split, 1)
            act.wait_ge(exp_ready, 3)

            def hidden(base, w):
                for e in range(NE_X):
                    act.wait_ge(o_mm, base * 4 + (e + 1))
                    for c in range(HID // P + 1):
                        if c < HID // P:
                            act.wait_ge(h_mm, base * 16 + (e * 4 + c + 1))
                            act.wait_ge(hid_ready, base * 16 + (e * 4 + c + 1))
                            nc.scalar.activation(hh32[:, c, 0:w], PS[:, c, 0:w], ACT.Gelu,
                                                 bias=b1T[:, e * 4 + c:e * 4 + c + 1], scale=esc[:, 2:3]).then_inc(hid32_ready, 1)
                        if c > 0:
                            act.wait_ge(hid32_ready, base * 16 + (e * 4 + c))
                            nc.scalar.activation(hh[:, e % 2, 0, c - 1, 0:w], hh32[:, c - 1, 0:w], ACT.Copy, scale=esc[:, 3:4]).then_inc(hi_hid, 1)

            with act.Fori(0, NT // NJ) as i:
                hidden(i, LO)
            hidden(NT // NJ, P)

        @block.tensor
        def _(pe):
            pe.wait_ge(iotas_ready, 1)
            pe.wait_ge(nat_ready, 1)
            for r in range(8):
                for k in range(4):
                    f = (srcf, dstf)[r // 4][:, ((r % 4) * 4 + k) * P:((r % 4) * 4 + k + 1) * P]
                    last = nc.tensor.transpose(PS[:, r, k * NG:(k + 1) * NG], f, identf[0:NG, 0:NG])
                last.then_inc(nat_turned, 1)
            pe.wait_ge(nat_evacuated, 8)
            nc.tensor.matmul(PS[0:1, 0, 0:NG], colf[0:NG, 2:3], identf[0:NG, 0:NG], start=True, stop=True)
            nc.tensor.matmul(PS[0:1, 1, 0:NG + 1], colf[0:NG, 5:6], tri[0:NG, 0:NG + 1], start=True, stop=True).then_inc(info_turned, 1)
            pe.wait_ge(ef_ready, 1)
            for r in range(6):
                for k in range(4):
                    last = nc.tensor.transpose(PS[:, 2 + r, k * P:(k + 1) * P], ef[:, (r * 4 + k) * P:(r * 4 + k + 1) * P], identf[:, :])
                last.then_inc(ef_turned, 1)
            pe.wait_ge(info_ready, 1)
            pe.wait_ge(small_loaded, 16 * 8)
            for kin in range(2):
                for a in range(2):
                    last = nc.tensor.transpose(PS[:, 0, (kin * 2 + a) * P:(kin * 2 + a + 1) * P], W_sb[:, a, kin * P:(kin + 1) * P], identf[:, :])
            last.then_inc(wt_turned, 1)
            pe.wait_ge(prep_done, 1)
            pe.sem_inc(win_done, 1)
            with pe.Fori(0, NG // 2) as i:
                for h in range(2):
                    w0 = pe.value_load(info[0:1, ds(i * 2 + (NG + 3 + h), 1)], min_val=0, max_val=32 * NG)
                    w1 = pe.value_load(info[0:1, ds(i * 2 + (NG + 4 + h), 1)], min_val=1, max_val=32 * NG)
                    pe.wait_ge(rows_in[h], i * (16 * CH) + 16 * CH)
                    pe.sem_inc(pe_go, 1)
                    with pe.Fori(w0, w1) as v:
                        pe.wait_ge(agg_done, v + 1)
                        pe.wait_ge(oh_ready, v + 1)
                        for k in range(CH):
                            for t in range(2):
                                oh = OH[:, k, t * P:(t + 1) * P]
                                nc.tensor.matmul(PS[:, t, 0:AGW], oh, ring[:, h * CH + k, D:2 * D + 1], start=(k == 0), stop=False, skip_group_check=True)
                                last = nc.tensor.matmul(PS[:, t, 0:D], oh, ring[:, h * CH + k, 0:D], start=False, stop=(k == CH - 1), skip_group_check=True)
                        last.then_inc(win_done, 1)
            def turn_y(i, h):
                k0, nk = BATCHES[h]
                pe.wait_ge(y_ready, i * 2 + (h + 1))
                for k in range(nk):
                    for a in range(2):
                        last = nc.tensor.transpose(PSF[:, YT + (k * 2 + a) * P:YT + (k * 2 + a + 1) * P], y[:, k0 + k, a * P:(a + 1) * P], identf[:, :])
                last.then_inc(yT_turned, 1)

            def through_W(i, h):
                k0, nk = BATCHES[h]
                pe.wait_ge(yT_ready, i * 2 + (h + 1))
                for k in range(nk):
                    o = PROD[h] + k * D
                    for a in range(2):
                        last = nc.tensor.matmul(PSF[:, o:o + D], yT[:, k0 + k, a, :], WT[:, a, :], start=(a == 0), stop=(a == 1))
                last.then_inc(mm_done, 1)

            def body(i, h, first, last, no_after_next=False):
                k0, nk = BATCHES[h]
                if not last:
                    turn_y(i + h, 1 - h)
                    through_W(i + h, 1 - h)
                pe.wait_ge(xn_ready, i * 2 + (h + 1))
                for k in range(nk):
                    for a in range(2):
                        done = nc.tensor.transpose(PSF[:, XNT + (k * 2 + a) * P:XNT + (k * 2 + a + 1) * P], xnb[:, k0 + k, a * P:(a + 1) * P], identf[:, :])
                done.then_inc(xn_turned, 1)
                pe.wait_ge(xh_kept, i * 2 + (h + 1))
                for k in range(nk):
                    o = HOUT + k * HX
                    for a in range(2):
                        done = nc.tensor.matmul(PSF[:, o:o + HX], xT[:, k0 + k, a, :], Wg[:, a, :], start=(a == 0), stop=(a == 1))
                done.then_inc(h_done, 1)

            def prologue():
                turn_y(0, 0)
                through_W(0, 0)

            node_phase(pe, None, 0, prologue, body, lambda: None)
            pe.wait_ge(nlev_ready, 1)
            levels = pe.value_load(nlev[0:1, 0:1], min_val=1, max_val=1 << 17)
            with pe.Fori(0, levels) as lv:

                def look_up(h):
                    for r in range(BC):
                        for j in range(NJ):
                            for part in range(2):
                                last = nc.tensor.matmul(PS[:, 4 + h, r * NHI * HEADS:(r + 1) * NHI * HEADS], ST[:, h, j, r * P:(r + 1) * P],
                                                        Tad[:, part, j, :, :].rearrange("p a b -> p (a b)"),
                                                        start=(j == 0 and part == 0), stop=(j == NJ - 1 and part == 1))
                    last.then_inc(ad_done, 1)

                def add_up(h):
                    for r in range(BC):
                        for j in range(NJ):
                            for part in range(2):
                                last = nc.tensor.matmul(PS[:, j, 0:HIV], S[:, h, r, j * P:(j + 1) * P], M[:, h, r, part * HIV:(part + 1) * HIV],
                                                        start=False, stop=False, skip_group_check=True)
                    last.then_inc(acc_done, 1)

                def clear_sums(start):
                    for j in range(NJ):
                        last = nc.tensor.matmul(PS[:, j, 0:HIV], zero_l[:, :], iota_hi[:, 0:HIV], start=start, stop=not start, skip_group_check=True)
                    return last

                pe.wait_ge(lev_ready, 1)
                clear_sums(True).then_inc(acc_done, 2)
                pe.wait_ge(turned_kept, 1)
                look_up(0)
                with pe.Fori(0, NB // 2) as i:
                    for h in range(2):
                        pe.wait_ge(turned_kept, i * 2 + (h + 2))
                        pe.wait_ge(spread_ready, i * 2 + (h + 1))
                        look_up(1 - h)
                        pe.wait_ge(lo_hot_ready, i * 2 + (h + 1))
                        pe.wait_ge(spread_ready, i * 2 + (h + 2))
                        add_up(h)
                clear_sums(False).then_inc(sums_ready, 1)
                pe.wait_ge(level_done, 1)
                pe.sem_inc(level_end, 1)
                pe.wait_ge(level_go, lv + 1)
                pe.sem_inc(pe_go, 1)
            pe.wait_ge(exp_loaded, 16 * (2 + NE_X + 2))
            nb1 = NE_X * HID // P
            nc.tensor.transpose(PS[:, 7, 0:nb1], b1n[:, :], identf[0:nb1, 0:nb1]).then_inc(b1_turned, 1)
            pe.wait_ge(exp_ready, 3)
            pe.sem_inc(o_mm, 2)

            def hid_products(e, base, tile0, nt):
                for c in range(HID // P):
                    if e > 0:
                        pe.wait_ge(hid32_ready, base * 16 + ((e - 1) * 4 + c + 1))
                    for a in range(2):
                        for wpart, xpart in ((0, 0), (0, 1), (1, 0)):
                            rhs = AGh[:, ds(tile0, nt), xpart * D + a * P:xpart * D + (a + 1) * P]
                            last = nc.tensor.matmul(PS[:, c, 0:nt * P], W1h[:, wpart, a, e, c * P:(c + 1) * P], rhs,
                                                    start=(a == 0 and wpart + xpart == 0), stop=(a == 1 and wpart == 1))
                    last.then_inc(h_mm, 1)

            def out_products(e, base, nt):
                pe.wait_ge(o_used, base * 4 + (e + 1))
                pe.wait_ge(hid_ready, base * 16 + (e * 4 + 8))
                for t in range(nt):
                    o = PS[:, 4 + 2 * (e % 2) + t // 2, (t % 2) * D:(t % 2 + 1) * D]
                    for c in range(HID // P):
                        for hpart, wpart in ((0, 0), (0, 1), (1, 0)):
                            last = nc.tensor.matmul(o, hh[:, e % 2, hpart, c, t * P:(t + 1) * P], W2h[:, wpart, e, c, :],
                                                    start=(c == 0 and hpart + wpart == 0), stop=(c == HID // P - 1 and hpart == 1))
                last.then_inc(o_mm, 1)

            def experts(base, tile0, nt):
                hid_products(0, base, tile0, nt)
                for e in range(1, NE_X):
                    hid_products(e, base, tile0, nt)
                    out_products(e - 1, base, nt)
                out_products(NE_X - 1, base, nt)

            with pe.Fori(0, NT // NJ) as i:
                experts(i, i * NJ, NJ)
            experts(NT // NJ, (NT // NJ) * NJ, 1)

        @block.vector
        def _(v):
            vec = nc.vector
            steps = Chain(v, prep_steps)
            link = steps.link
            vec.memset(X3[:, NT - 1, :], 0.0)
            vec.memset(consts[:, 0:1], EPS)
            vec.memset(consts[:, 1:2], EPS * XSCALE ** -2)
            vec.memset(srcn[P - 32:P, :], 0).then_inc(pads_set, 1)
            vec.memset(dstn[P - 32:P, :], PADN).then_inc(pads_set, 1)
            v.wait_ge(x_loaded, 16 * 5)
            v.wait_ge(pads_set, 2)
            with steps.loop(NT // BT, 12) as i:
                for h, (k0, nk) in enumerate(BATCHES):
                    ks = slice(k0, k0 + nk)

                    def tile(k):
                        return X3[:, ds(i * BT + k, 1), :].rearrange("p a d -> p (a d)")

                    link(*[vec.bn_stats(stats[:, k, :], tile(k)) for k in range(k0, k0 + nk)])
                    v.sem_inc(dve_go, 1)
                    link(*[vec.bn_aggr(mv[:, k, :], stats[:, k, :]) for k in range(k0, k0 + nk)])
                    v.sem_inc(stats_ready, 1)
                    v.wait_ge(std_ready, i * 2 + (h + 1))
                    link(vec.reciprocal(rstd[:, ks], std[:, ks]))
                    link(vec.tensor_scalar(rstd[:, ks], rstd[:, ks], TAB_SCALE, None, ALU.mult))
                    link(vec.scalar_tensor_tensor(shift[:, ks], mv[:, ks, 0], -1.0, rstd[:, ks], ALU.mult, ALU.mult))
                    v.sem_inc(rstd_ready, 1)
                    link(*[vec.tensor_scalar(xs[:, k, :], tile(k), mv[:, k, 0:1], rstd[:, k:k + 1], ALU.subtract, ALU.mult) for k in range(k0, k0 + nk)])
                    v.wait_ge(hi_ready, i * 2 + (h + 1))
                    vec.tensor_tensor(tstage[:, ks, 0:D], xs[:, ks, :], tstage[:, ks, D:2 * D], ALU.subtract).then_inc(lo_ready, 1)
            v.wait_ge(edges_loaded, 64)
            link(vec.tensor_scalar(dstf, dstn[0:NG, :], PADN, None, ALU.min),
                 vec.tensor_scalar(srcf, srcn[0:NG, :], N - 1, None, ALU.min))
            link(vec.tensor_reduce(colf[0:NG, 0:1], dstf, AX.X, ALU.min), vec.tensor_reduce(colf[0:NG, 1:2], dstf, AX.X, ALU.max))
            link(vec.tensor_copy(cols[0:NG, 0:2], colf[0:NG, 0:2]))
            link(vec.tensor_scalar(cols[0:NG, 2:4], cols[0:NG, 0:2], 7, None, ALU.arith_shift_right))
            link(vec.tensor_copy(colf[0:NG, 2:4], cols[0:NG, 2:4]))
            link(vec.tensor_tensor(cols[0:NG, 4:5], colf[0:NG, 3:4], colf[0:NG, 2:3], ALU.subtract),
                 vec.tensor_scalar(colf[0:NG, 6:7], colf[0:NG, 2:3], float(P), None, ALU.mult))
            link(vec.tensor_scalar(cols[0:NG, 5:6], cols[0:NG, 4:5], 1, None, ALU.arith_shift_right))
            link(vec.tensor_scalar(colf[0:NG, 5:6], cols[0:NG, 5:6], 1.0, None, ALU.add),
                 vec.tensor_scalar(dstf, dstf, colf[0:NG, 6:7], None, ALU.subtract))
            v.sem_inc(nat_ready, 1)
            for r in range(8):
                v.wait_ge(nat_turned, r + 1)
                to = (sidx_all, drel_all)[r // 4][:, :].rearrange("p (g k) -> p k g", k=CH)[:, 4 * (r % 4):4 * (r % 4) + 4, :]
                vec.tensor_copy(to, PS[:, r, 0:4 * NG].rearrange("p (k g) -> p k g", k=4)).then_inc(nat_evacuated, 1)
            vec.memset(info[0:1, :], 0).then_inc(info_zeroed, 1)
            v.wait_ge(info_turned, 1)
            v.wait_ge(info_zeroed, 1)
            link(vec.tensor_copy(info[0:1, 0:NG], PS[0:1, 0, 0:NG]), vec.tensor_copy(info[0:1, NG + 3:2 * NG + 4], PS[0:1, 1, 0:NG + 1]))
            v.wait_ge(nat_evacuated, 8)
            v.sem_inc(idx_ready, 1)
            v.sem_inc(info_ready, 1)
            v.wait_ge(edges2_loaded, 32)
            link(vec.tensor_scalar(eni[:, 0:E1], en[:, E1:2 * E1], LO - 1, None, ALU.bitwise_and),
                 vec.tensor_scalar(eni[:, E1:2 * E1], en[:, E1:2 * E1], int(np.log2(LO)), None, ALU.arith_shift_right),
                 vec.tensor_scalar(ef[:, 0:E1], en[:, 0:E1], N - 1, None, ALU.min))
            link(vec.tensor_copy(ef[:, E1:3 * E1], eni[:, :]), vec.tensor_copy(loh, eni[:, 0:E1]),
                 vec.memset(asrc_idx[:, NB:NB + 2, :], 0), vec.memset(lohi[:, NB:NB + 1, :, :], 0.0))
            v.sem_inc(ef_ready, 1)
            v.sem_inc(loh_ready, 1)
            for r in range(6):
                v.wait_ge(ef_turned, r + 1)
                turn4 = PS[:, 2 + r, :].rearrange("p (k q) -> p k q", k=4)
                ks = slice(4 * (r % 2), 4 * (r % 2) + 4)
                to = asrc_idx[:, 0:NB, ks].rearrange("p q r -> p r q") if r < 2 else lohi[:, 0:NB, r // 2 - 1, ks].rearrange("p q r -> p r q")
                last = vec.tensor_copy(to, turn4)
            link(last)
            v.wait_ge(wt_turned, 1)
            link(vec.tensor_copy(WT[:, :, :].rearrange("p a n -> p (a n)"), PS[:, 0, :]),
                 vec.memset(ring[:, :, 2 * D:2 * D + 1], 1.0))
            v.wait_ge(lo_stored, 32)
            vec.memset(AG[:, :], 0.0).then_inc(agg_done, 1)
            v.wait_ge(agg_done, 1)
            v.sem_inc(prep_done, 1)
            wsteps = Chain(v, win_steps)
            with v.Fori(0, NG // 2) as i:
                for h in range(2):
                    w0 = v.value_load(info[0:1, ds(i * 2 + (NG + 3 + h), 1)], min_val=0, max_val=32 * NG)
                    w1 = v.value_load(info[0:1, ds(i * 2 + (NG + 4 + h), 1)], min_val=1, max_val=32 * NG)
                    t0 = v.value_load(info[0:1, ds(i * 2 + h, 1)], min_val=0, max_val=NT - 1)
                    vec.tensor_copy(drelw[:, :], drel_all[:, ds((i * 2 + h) * CH, CH)]).then_inc(drel_ready, 1)
                    v.wait_ge(drel_ready, i * 2 + (h + 1))
                    v.sem_inc(dve_go, 1)
                    with v.Fori(w0, w1) as w:
                        for k in range(CH):
                            last = vec.tensor_scalar(OH[:, k, :], iota_lo[:, 0:2 * P], drelw[:, k:k + 1], None, ALU.is_equal)
                        last.then_inc(oh_ready, 1)
                        v.wait_ge(oh_ready, w + 1)
                        vec.tensor_scalar(drelw[:, :], drelw[:, :], 2.0 * P, None, ALU.subtract).then_inc(win_steps, 1)
                        v.wait_ge(win_steps, w + 1)
                        v.wait_ge(win_done, w + 2)
                        tile = nc.s_assert_within(t0 + (w - w0) * 2, 0, NT - 1,
                                                  skip_runtime_bounds_check_because="the windows of a group end with its last tile")
                        at = AG[:, ds(tile * AGW, 2 * AGW)].rearrange("p (t n) -> p t n", t=2)
                        vec.tensor_tensor(at, at, PS[:, 0:2, 0:AGW], ALU.add).then_inc(agg_done, 1)
                        v.wait_ge(agg_done, w + 2)
            steps = Chain(v, node_steps)
            link = steps.link
            v.sem_inc(gnn_done, 1)
            v.wait_ge(small_loaded, 16 * 8)
            link(vec.memset(wmax[:, :], 0.0))

            def scales(i, h):
                k0, nk = BATCHES[h]
                ks = slice(k0, k0 + nk)
                deg = AG3[:, ds(i * BT + k0, nk), D:D + 1].rearrange("p t a -> p (t a)")
                link(vec.tensor_scalar(dgs[:, 0, ks], deg, 1.0, None, ALU.add))
                link(vec.reciprocal(dgs[:, 1, ks], dgs[:, 0, ks]))
                link(vec.tensor_scalar(dgs[:, 2, ks], dgs[:, 1, ks], 1.0 / TAB_SCALE, None, ALU.mult),
                     vec.tensor_tensor(dgs[:, 3, ks], dgs[:, 1, ks], deg, ALU.mult))
                v.sem_inc(scales_ready, 1)

            def keep_h(i, h):
                k0, nk = BATCHES[h]
                v.wait_ge(h_done, i * 2 + (h + 1))
                link(vec.tensor_scalar(H[:, ds(i * BT + k0, nk), :].rearrange("p t n -> p (t n)"), PSF[:, HOUT:HOUT + nk * HX], 1.0 / XSCALE, None, ALU.mult))
                v.wait_ge(xh_kept, i * 2 + (h + 1))
                at = AGh[:, ds(i * BT + k0, nk), :]
                link(vec.tensor_tensor(at[:, :, D:2 * D], xT[:, k0:k0 + nk, :, :].rearrange("p k a n -> p k (a n)"), at[:, :, 0:D], ALU.subtract))

            def body(i, h, first, last, no_after_next=False):
                k0, nk = BATCHES[h]
                ks = slice(k0, k0 + nk)
                v.wait_ge(mm_done, i * 2 + (h + 1))
                Xb = X3[:, ds(i * BT + k0, nk), :]
                link(vec.tensor_tensor(Xb, Xb, PSF[:, PROD[h]:PROD[h] + nk * D].rearrange("p (t n) -> p t n", n=D), ALU.add))
                link(*[vec.scalar_tensor_tensor(tile_of(i, k), b_bc[:, :], dgs[:, 3, k:k + 1], tile_of(i, k), ALU.mult, ALU.add) for k in range(k0, k0 + nk)])
                v.sem_inc(dve_go, 1)
                link(*[vec.bn_stats(stats[:, k, :], tile_of(i, k)) for k in range(k0, k0 + nk)])
                v.sem_inc(dve_go, 1)
                link(*[vec.bn_aggr(mv[:, k, :], stats[:, k, :]) for k in range(k0, k0 + nk)])
                v.sem_inc(node_stats, 1)
                if not no_after_next:
                    scales(i + 1, h)
                if not first:
                    keep_h(i - (1 - h), 1 - h)
                v.wait_ge(node_std, i * 2 + (h + 1))
                link(vec.reciprocal(rstd[:, ks], std[:, ks]))
                link(*[vec.tensor_scalar(xnb[:, k, :], tile_of(i, k), mv[:, k, 0:1], rstd[:, k:k + 1], ALU.subtract, ALU.mult) for k in range(k0, k0 + nk)])
                v.sem_inc(xn_ready, 1)
                if h == 1:
                    v.wait_ge(see_loaded, 16 * (2 + NE_X + 1))
                    link(*[vec.tensor_reduce(wtmp[:, a:a + 1], see[:, ds(i * WSTEP, WSTEP + 1)], AX.X, ALU.max, apply_absolute_value=True)
                           for a, see in enumerate((W1_see, W2_see))])
                    link(vec.tensor_tensor(wmax[:, 0:2], wmax[:, 0:2], wtmp[:, :], ALU.max))

            def prologue():
                scales(0, 0)
                scales(0, 1)

            node_phase(v, steps, 2 * (4 + 3 + 2 + 2) + 2, prologue, body, lambda: keep_h(NT // BT - 1, 1))
            link(vec.tensor_reduce(wmax[0:NE_X * HID // P, 2:3], b1_see[:, :], AX.X, ALU.max, apply_absolute_value=True))
            steps = Chain(v, att_steps)
            link = steps.link
            ops = lambda o, a, b_, op: vec.tensor_tensor(o, a, b_, op)
            link(vec.memset(H[:, NT:NTP, :], 0.0), vec.memset(acc[:, :, :], 0.0), vec.memset(Rsh[:, :, :], 0.0),
                 vec.memset(zero_l[:, :], 0.0), vec.memset(ext[:, :], 0.0))
            for a, to in ((0, AS), (1, AD)):
                link(ops(tmp16[:, :, 0:HX], H[:, :, :], small[:, a:a + 1, :].to_broadcast([P, NTP, HX]), ALU.mult))
                link(vec.tensor_reduce(to[:, :, :], tmp16[:, :, 0:HX].rearrange("p t (h e) -> p t h e", e=NX), AX.X, ALU.add))
            link(vec.tensor_reduce(ext[:, 0:4], AS[:, :, :].rearrange("p t h -> p h t"), AX.X, ALU.max),
                 vec.tensor_reduce(ext[:, 4:8], AS[:, :, :].rearrange("p t h -> p h t"), AX.X, ALU.min),
                 vec.tensor_reduce(ext[:, 8:9], AD[:, :, :].rearrange("p t h -> p (t h)"), AX.X, ALU.max, apply_absolute_value=True),
                 vec.tensor_reduce(ext[:, 9:10], H[:, :, :].rearrange("p t h -> p (t h)"), AX.X, ALU.max, apply_absolute_value=True))
            link(vec.tensor_scalar(ext[:, 4:8], ext[:, 4:8], -1.0, None, ALU.mult), vec.tensor_copy(ext[:, 10:13], wmax[:, :]))
            v.sem_inc(ext_ready, 1)
            v.wait_ge(ext_reduced, 1)
            link(vec.tensor_scalar(sc[:, 0:2], extr[:, 8:10], 1e-25, None, ALU.max),
                 vec.tensor_tensor(n1[:, 0, :], extr[:, 0:4], extr[:, 4:8], ALU.add))
            link(vec.reciprocal(sc[:, 2:4], sc[:, 0:2]), vec.tensor_reduce(sc[:, 8:9], n1[:, 0, :], AX.X, ALU.max))
            link(vec.tensor_scalar(sc[:, 4:5], sc[:, 2:3], FULL, None, ALU.mult), vec.tensor_scalar(sc[:, 5:6], sc[:, 0:1], 1.0 / FULL, None, ALU.mult),
                 vec.tensor_scalar(sc[:, 6:7], sc[:, 3:4], FULL, None, ALU.mult), vec.tensor_scalar(sc[:, 7:8], sc[:, 1:2], 1.0 / FULL, None, ALU.mult),
                 vec.tensor_scalar(nlev[:, :], sc[:, 8:9], 1.0 / LEVEL, 1.0, ALU.mult, ALU.add))
            v.sem_inc(nlev_ready, 1)
            NT5 = NTB[:, :, HEADS:ROWW].rearrange("p t (h e) -> p t h e", e=1 + NX)
            link(vec.tensor_scalar(ADs[:, :, :], AD[:, :, :], sc[:, 4:5], None, ALU.mult),
                 vec.memset(NTB[:, :, :], DEN_SCALE), vec.tensor_copy(Gk[:, :], extr[:, 0:4]))
            Tp = [Tad[:, a, :, :, :].rearrange("p j t h -> p t j h") for a in range(2)]
            AD4 = ADs[:, :, :].rearrange("p (t j) h -> p t j h", j=NJ)
            link(*[vec.tensor_scalar(NT5[:, :, hd, 1:1 + NX], H[:, :, hd * NX:(hd + 1) * NX], sc[:, 6:7], None, ALU.mult) for hd in range(HEADS)])
            link(*[vec.tensor_copy(Tp[0][:, :, j, :], AD4[:, :, j, :]) for j in range(NJ)])
            link(*[ops(Tp[1][:, :, j, :], AD4[:, :, j, :], Tp[0][:, :, j, :], ALU.subtract) for j in range(NJ)])
            v.wait_ge(iota_hi_ready, 1)
            levels = v.value_load(nlev[0:1, 0:1], min_val=1, max_val=1 << 17)
            NTH = [P, NTP, HEADS]
            with v.Fori(0, levels) as lv:
                steps = Chain(v, level_steps)
                link = steps.link
                Gb = Gk[:, :].unsqueeze(1).to_broadcast(NTH)
                link(vec.tensor_scalar(Gk1[:, :], Gk[:, :], LEVEL, None, ALU.subtract), ops(n3[:, :, :], AS[:, :, :], Gb, ALU.is_le),
                     ops(n1[:, :, :], AD[:, :, :], Gb, ALU.add))
                link(ops(n2[:, :, :], AS[:, :, :], Gk1[:, :].unsqueeze(1).to_broadcast(NTH), ALU.is_gt))
                link(ops(n2[:, :, :], n2[:, :, :], n3[:, :, :], ALU.mult))
                link(ops(NTB[:, :, 0:HEADS], AS[:, :, :], n2[:, :, :], ALU.mult), vec.tensor_scalar(n3[:, :, :], n2[:, :, :], 1.0, BIG, ALU.subtract, ALU.mult))
                link(ops(NTB[:, :, 0:HEADS], NTB[:, :, 0:HEADS], n3[:, :, :], ALU.add))
                v.sem_inc(atable_ready, 1)
                v.sem_inc(lev_ready, 1)

                def copy_stage(q, h):
                    link(vec.tensor_copy(estage[:, h, :], lohi[:, ds(q, 1), :, :].rearrange("p a b r -> p (a b r)")))

                def hot(h, r):
                    return vec.tensor_scalar(S[:, h, r, :], iota_lo[:, :], estage[:, h, r:r + 1], None, ALU.is_equal)

                copy_stage(0, 0)
                v.sem_inc(spread_ready, 1)
                with steps.loop(NB // 2, 2 * 9) as i:
                    for h in range(2):
                        v.wait_ge(spread_ready, i * 2 + (h + 1))
                        steps.mark(*[vec.tensor_scalar(Hm[:, r, :], iota_hi[:, :], estage[:, h, BC + r:BC + r + 1], None, ALU.is_equal) for r in range(BC)])
                        v.wait_ge(acc_done, i * 2 + (h + 1))
                        hot(h, 0)
                        steps.catch()
                        v.wait_ge(ad_done, i * 2 + (h + 1))
                        Hm4 = Hm[:, :, :].rearrange("p r (t f) -> p r t f", f=VAL)[:, :, :, 0:HEADS]
                        ad4 = PS[:, 4 + h, 0:BC * NHI * HEADS].rearrange("p (r t f) -> p r t f", r=BC, f=HEADS)
                        steps.mark(vec.tensor_tensor(sel[:, :, :, :].rearrange("p r f t -> p r t f"), ad4, Hm4, ALU.mult))
                        hot(h, 1)
                        steps.catch()
                        steps.mark(vec.tensor_reduce(adu[:, :, :], sel[:, :, :, :], AX.X, ALU.add))
                        hot(h, 2)
                        steps.catch()
                        v.wait_ge(arows_in[h], lv * ROWS_LEVEL + i * (16 * BC) + 16 * BC)
                        steps.mark(vec.scalar_tensor_tensor(ez[:, :, :], adu[:, :, :], sc[:, 5:6], rows[:, h, :, 0:HEADS], ALU.mult, ALU.add),
                                   vec.scalar_tensor_tensor(er[:, :, :], adu[:, :, :], sc[:, 5:6], Gk[:, :].unsqueeze(1).to_broadcast([P, BC, HEADS]), ALU.mult, ALU.add))
                        hot(h, 3)
                        steps.catch()
                        steps.mark(vec.scalar_tensor_tensor(ez2[:, :, :], ez[:, :, :], 0.2, ez[:, :, :], ALU.mult, ALU.max),
                                   vec.scalar_tensor_tensor(er2[:, :, :], er[:, :, :], 0.2, er[:, :, :], ALU.mult, ALU.max))
                        hot(h, 4)
                        steps.catch()
                        vec.tensor_tensor(ez[:, :, :], ez2[:, :, :], er2[:, :, :], ALU.subtract).then_inc(e_ready, 1)
                        steps.mark(vec.tensor_copy(estage[:, 1 - h, :], lohi[:, ds(i * 2 + (h + 1), 1), :, :].rearrange("p a b r -> p (a b r)")))
                        hot(h, 5)
                        hot(h, 6)
                        steps.catch()
                        v.wait_ge(w_ready, i * 2 + (h + 1))
                        steps.mark(vec.tensor_tensor(val[:, :, :].rearrange("p r (h e) -> p r h e", e=1 + NX), wexp[:, :, :].unsqueeze(3).to_broadcast([P, BC, HEADS, 1 + NX]),
                                                     rows[:, h, :, HEADS:ROWW].rearrange("p r (h e) -> p r h e", e=1 + NX), ALU.mult))
                        hot(h, 7).then_inc(lo_hot_ready, 1)
                        steps.catch()
                        v.sem_inc(rows_used, 1)
                        link(vec.tensor_copy(vh[:, :, 0, :], val[:, :, :]))
                        link(vec.tensor_tensor(vh[:, :, 1, :], val[:, :, :], vh[:, :, 0, :], ALU.subtract))
                        for part in range(2):
                            last = vec.tensor_tensor(M[:, h, :, part * HIV:(part + 1) * HIV].rearrange("p r (t f) -> p r t f", f=VAL),
                                                     vh[:, :, part, :].unsqueeze(2).to_broadcast([P, BC, NHI, VAL]),
                                                     Hm[:, :, :].rearrange("p r (t f) -> p r t f", f=VAL), ALU.mult)
                        last.then_inc(spread_ready, 1)
                link(vec.scalar_tensor_tensor(n4[:, :, :], n1[:, :, :], 0.2, n1[:, :, :], ALU.mult, ALU.max), ops(n2[:, :, :], AD[:, :, :], NTB[:, :, 0:HEADS], ALU.add))
                link(vec.scalar_tensor_tensor(n3[:, :, :], n2[:, :, :], 0.2, n2[:, :, :], ALU.mult, ALU.max))
                link(ops(n2[:, :, :], n3[:, :, :], n4[:, :, :], ALU.subtract))
                link(vec.tensor_copy(n1[:, :, :], n4[:, :, :]))
                v.sem_inc(self_e, 1)
                v.wait_ge(sums_ready, 1)
                link(*[vec.tensor_copy(L[:, :, :].rearrange("p (t j) f -> p j t f", j=NJ)[:, j, :, :], PS[:, j, 0:HIV].rearrange("p (t f) -> p t f", f=VAL)) for j in range(NJ)])
                v.wait_ge(self_w, 1)
                w5 = [P, NTP, HEADS, 1 + NX]
                tmp5 = tmp16[:, :, :].rearrange("p t (h e) -> p t h e", e=1 + NX)
                acc5 = acc[:, :, :].rearrange("p t (h e) -> p t h e", e=1 + NX)
                link(ops(tmp5, n3[:, :, :].unsqueeze(3).to_broadcast(w5), NT5, ALU.mult),
                     vec.tensor_scalar(n4[:, :, :], acc5[:, :, :, 0], 0.0, None, ALU.is_equal))
                link(ops(L[:, :, :], L[:, :, :], tmp16[:, :, :], ALU.add), ops(n2[:, :, :], n1[:, :, :], n4[:, :, :], ALU.mult),
                     vec.tensor_scalar(n3[:, :, :], n4[:, :, :], -1.0, 1.0, ALU.mult, ALU.add))
                link(ops(Rsh[:, :, :], Rsh[:, :, :], n3[:, :, :], ALU.mult))
                link(ops(Rsh[:, :, :], Rsh[:, :, :], n2[:, :, :], ALU.add))
                link(ops(n2[:, :, :], n1[:, :, :], Rsh[:, :, :], ALU.subtract))
                v.sem_inc(mg_ready, 1)
                v.wait_ge(mg_exp, 1)
                link(ops(tmp5, n4[:, :, :].unsqueeze(3).to_broadcast(w5), L[:, :, :].rearrange("p t (h e) -> p t h e", e=1 + NX), ALU.mult),
                     vec.tensor_copy(Gk[:, :], Gk1[:, :]))
                link(ops(acc[:, :, :], acc[:, :, :], tmp16[:, :, :], ALU.add))
                v.sem_inc(level_done, 3)
                v.sem_inc(level_end, 1)
                v.wait_ge(level_go, lv + 1)
                v.sem_inc(dve_go, 1)
            steps = Chain(v, gate_steps)
            link = steps.link
            link(vec.tensor_scalar(esc[:, 8:11], extr[:, 10:13], 1e-20, None, ALU.max))
            link(vec.reciprocal(esc[:, 6:8], esc[:, 8:10]), vec.scalar_tensor_tensor(esc[:, 11:12], esc[:, 8:9], float(D), esc[:, 10:11], ALU.mult, ALU.add),
                 vec.tensor_scalar(esc[:, 2:3], esc[:, 8:9], 1.0 / (FULL * XSCALE), None, ALU.mult))
            link(vec.tensor_scalar(esc[:, 0:2], esc[:, 6:8], FULL, None, ALU.mult), vec.reciprocal(esc[:, 5:6], esc[:, 11:12]),
                 vec.scalar_tensor_tensor(esc[:, 4:5], esc[:, 9:10], 1.0 / (FULL * FULL), esc[:, 11:12], ALU.mult, ALU.mult))
            link(vec.tensor_scalar(esc[:, 3:4], esc[:, 5:6], FULL, None, ALU.mult))
            v.sem_inc(exp_ready, 1)
            acc5 = acc[:, :, :].rearrange("p t (h e) -> p t h e", e=1 + NX)
            A4 = A16[:, :, :].rearrange("p t (h e) -> p t h e", e=NX)
            T1 = [P, NTP, HX]
            link(vec.tensor_scalar(rank[:, :, :], acc5[:, :, :, 0], 1.0 / DEN_SCALE, 1e-16, ALU.mult, ALU.add))
            link(vec.reciprocal(pick[:, :, :], rank[:, :, :]))
            link(vec.tensor_scalar(pick[:, :, :], pick[:, :, :], sc[:, 7:8], None, ALU.mult))
            link(ops(A4, acc5[:, :, :, 1:1 + NX], pick[:, :, :].unsqueeze(3).to_broadcast([P, NTP, HEADS, NX]), ALU.mult))
            link(ops(A16[:, :, :], A16[:, :, :], small[:, 2:3, :].to_broadcast(T1), ALU.add))
            link(vec.tensor_reduce(m1[:, :], A16[:, :, :], AX.X, ALU.add))
            link(vec.tensor_scalar(m1[:, :], m1[:, :], 1.0 / HX, None, ALU.mult))
            link(ops(A16[:, :, :], A16[:, :, :], m1[:, :].unsqueeze(2).to_broadcast(T1), ALU.subtract))
            link(ops(B16[:, :, :], A16[:, :, :], A16[:, :, :], ALU.mult))
            link(vec.tensor_reduce(m2[:, :], B16[:, :, :], AX.X, ALU.add))
            link(vec.tensor_scalar(m2[:, :], m2[:, :], 1.0 / HX, None, ALU.mult))
            v.sem_inc(gate_in, 1)
            v.wait_ge(gate_std_r, 1)
            link(vec.reciprocal(m1[:, :], m3[:, :]))
            link(ops(A16[:, :, :], A16[:, :, :], m1[:, :].unsqueeze(2).to_broadcast(T1), ALU.mult))
            link(ops(A16[:, :, :], A16[:, :, :], small[:, 3:4, :].to_broadcast(T1), ALU.mult))
            link(ops(A16[:, :, :], A16[:, :, :], small[:, 4:5, :].to_broadcast(T1), ALU.add))
            link(vec.tensor_reduce(scr4[:, :, :], A16[:, :, :].rearrange("p t (h e) -> p t e h", e=NX), AX.X, ALU.add))
            link(vec.tensor_scalar(scr4[:, :, :], scr4[:, :, :], 1.0 / HEADS, None, ALU.mult))
            link(vec.memset(rank[:, :, :], 0.0))
            for a in range(NX):
                for c in range(a + 1, NX):
                    link(ops(cmp[:, :], scr4[:, :, a], scr4[:, :, c], ALU.is_ge), ops(m3[:, :], scr4[:, :, a], scr4[:, :, c], ALU.is_lt))
                    link(ops(rank[:, :, c], rank[:, :, c], cmp[:, :], ALU.add), ops(rank[:, :, a], rank[:, :, a], m3[:, :], ALU.add))
            for place, to in ((0.0, s1), (1.0, s2)):
                link(vec.tensor_scalar(pick[:, :, :], rank[:, :, :], place, None, ALU.is_equal))
                link(ops(B16[:, :, 0:NX], pick[:, :, :], scr4[:, :, :], ALU.mult))
                link(vec.tensor_reduce(to[:, :], B16[:, :, 0:NX], AX.X, ALU.add))
            link(ops(cmp[:, :], s2[:, :], s1[:, :], ALU.subtract))
            v.sem_inc(gate_in, 1)
            v.wait_ge(gate_exp, 1)
            link(vec.tensor_scalar(m1[:, :], dexp[:, :], 1.0, None, ALU.add))
            link(vec.reciprocal(m2[:, :], m1[:, :]))
            link(ops(m3[:, :], m2[:, :], dexp[:, :], ALU.mult), vec.tensor_scalar(pick[:, :, :], rank[:, :, :], 0.0, None, ALU.is_equal),
                 vec.tensor_scalar(scr4[:, :, :], rank[:, :, :], 1.0, None, ALU.is_equal))
            link(ops(pick[:, :, :], pick[:, :, :], m2[:, :].unsqueeze(2).to_broadcast([P, NTP, NX]), ALU.mult),
                 ops(scr4[:, :, :], scr4[:, :, :], m3[:, :].unsqueeze(2).to_broadcast([P, NTP, NX]), ALU.mult))
            link(ops(gate[:, :].rearrange("p (t e) -> p t e", e=NX), pick[:, 0:NT, :], scr4[:, 0:NT, :], ALU.add))
            link(vec.tensor_scalar(gates[:, :], gate[:, :], esc[:, 4:5], None, ALU.mult))
            v.wait_ge(b1_turned, 1)
            link(vec.tensor_copy(b1T[:, :], PS[:, 7, 0:NE_X * HID // P]))
            for c in range(8):
                v.wait_ge(w_split, c + 1)
                hi, lo, st, a = w_chunk(c)
                last = vec.scalar_tensor_tensor(lo, st, esc[:, a:a + 1], hi, ALU.mult, ALU.subtract)
            link(last)
            v.sem_inc(exp_ready, 2)
            v.sem_inc(o_used, 2)
            v.sem_inc(hid_ready, 4)

            def low_parts(e, base, w):
                for c in range(HID // P):
                    v.wait_ge(hi_hid, base * 16 + (e * 4 + c + 1))
                    vec.scalar_tensor_tensor(hh[:, e % 2, 1, c, 0:w], hh32[:, c, 0:w], esc[:, 3:4], hh[:, e % 2, 0, c, 0:w],
                                             ALU.mult, ALU.subtract).then_inc(hid_ready, 1)

            def gated(e, base, tile0, nt):
                ats = [X3[:, ds(tile0 + t, 1), :].rearrange("p a d -> p (a d)") for t in range(nt)]
                for t in range(nt):
                    last = vec.scalar_tensor_tensor(ats[t], b2_bc[:, e * D:(e + 1) * D], gate[:, ds((tile0 + t) * NX + e, 1)], ats[t], ALU.mult, ALU.add)
                last.then_inc(bias_added, 1)
                v.wait_ge(bias_added, base * 4 + (e + 1))
                v.wait_ge(o_mm, base * 4 + (e + 3))
                for t in range(nt):
                    last = vec.scalar_tensor_tensor(ats[t], PS[:, 4 + 2 * (e % 2) + t // 2, (t % 2) * D:(t % 2 + 1) * D],
                                                    gates[:, ds((tile0 + t) * NX + e, 1)], ats[t], ALU.mult, ALU.add)
                last.then_inc(o_used, 1)
                v.wait_ge(o_used, base * 4 + (e + 3))

            def add_experts(base, tile0, nt):
                low_parts(0, base, nt * P)
                for e in range(1, NE_X):
                    low_parts(e, base, nt * P)
                    gated(e - 1, base, tile0, nt)
                gated(NE_X - 1, base, tile0, nt)

            with v.Fori(0, NT // NJ) as i:
                add_experts(i, i * NJ, NJ)
            add_experts(NT // NJ, (NT // NJ) * NJ, 1)


_INS = ['x', 'src', 'dst', 'L0_gnn_W', 'L0_gnn_b', 'L0_ffn_W_gat', 'L0_ffn_att_src', 'L0_ffn_att_dst', 'L0_ffn_b_gat',
        'L0_ffn_ln_gamma', 'L0_ffn_ln_beta', 'L0_ffn_W1', 'L0_ffn_b1', 'L0_ffn_W2', 'L0_ffn_b2', 'L0_ffn_edge_index']
_OUTS = [((6250, 256), 'float32')]


def kernel(**inputs):
    import numpy as _np
    import concourse.bacc as _bacc
    from concourse import mybir as _mybir
    from concourse.bass_utils import run_bass_kernel_spmd as _run

    nc = _bacc.Bacc("TRN2", target_bir_lowering=False, num_devices=1)
    arrays, args = {}, []
    for name in _INS:
        a = _np.ascontiguousarray(inputs[name])
        arrays[f"in_{name}_dram"] = a
        args.append(nc.dram_tensor(f"in_{name}_dram", a.shape, _mybir.dt.from_np(a.dtype), kind="ExternalInput").ap())
    for i, (shape, dtype) in enumerate(_OUTS):
        dt = _mybir.dt.from_np(_np.dtype(dtype))
        args.append(nc.dram_tensor(f"out_{i}_dram", shape, dt, kind="ExternalOutput").ap())
    gnn_moe(nc, *args)
    r = _run(nc, [arrays], core_ids=[0])
    got = tuple(r.results[0][f"out_{i}_dram"] for i in range(len(_OUTS)))
    return got[0]
```

```python
from contextlib import ExitStack, contextmanager

import numpy as np

import concourse.bass as bass
from concourse import mybir

F32 = mybir.dt.float32
F16 = mybir.dt.float16
I32 = mybir.dt.int32
ALU = mybir.AluOpType
ACT = mybir.ActivationFunctionType
AX = mybir.AxisListType
RED = bass.bass_isa.ReduceOp
ds = bass.ds

P = 128
D = 256
EPS = 1e-5

CH = 16
GROUP = CH * P
AGW = D + 1
TAB_SCALE = 1024.0

HEADS, NX = 4, 4
HX = HEADS * NX
XSCALE = 1024.0
LO = 512
NJ = LO // P
BC = 8
ROWW = HEADS + HEADS * (1 + NX)
VAL = HEADS * (1 + NX)
LEVEL = 8.0
DEN_SCALE = 4096.0
FULL = 16384.0
BIG = 1e30
HID = 512


class Chain:

    def __init__(self, eng, sem):
        self.eng, self.sem, self.base, self.n = eng, sem, 0, 0

    def link(self, *instructions):
        self.mark(*instructions)
        self.catch()

    def mark(self, *instructions):
        instructions[-1].then_inc(self.sem, 1)
        self.n += 1

    def catch(self):
        self.eng.wait_ge(self.sem, self.base + self.n)

    @contextmanager
    def loop(self, count, steps):
        base, n = self.base, self.n
        with self.eng.Fori(0, count) as i:
            self.base, self.n = i * steps + (base + n), 0
            yield i
            assert self.n == steps, (self.n, steps)
        self.base, self.n = base, n + count * steps


def gnn_moe(nc, x, src, dst, W, b, W_gat, att_src, att_dst, b_gat, ln_g, ln_b, W1, b1, W2, b2, edges, out):
    N = x.shape[0]
    NT = -(-N // P)
    SPARE = NT + 1
    LAST = N - (NT - 1) * P
    NE = src.shape[0]
    NG = -(-NE // GROUP)
    TAIL = NE - (NG - 1) * GROUP
    NA = edges.shape[1]
    NB = NA // (BC * P)
    NHI = -(-N // LO)
    NTP = NHI * NJ
    HIV = NHI * VAL
    NE_X = W1.shape[0]
    PADN = NT * P - 1
    LOB_LEVEL = 16 * (NB // 2 + 1)
    ROWS_LEVEL = 16 * BC * NB // 2
    BT = 7
    assert NT % BT == 0 and NG % 2 == 0 and NB % 2 == 0 and NA % (BC * P) == 0
    NI = NG // 2
    WSTEP = 2 * NE_X * HID // NI
    WIDE = 2 * NE_X * HID - (NI - 1) * WSTEP
    LAG = 1
    BATCHES = ((0, 4), (4, 3))

    table = nc.dram_tensor("ln_table", (NT * P, 2 * D), F16, kind="Internal").ap()
    lo_rows = nc.dram_tensor("lo_rows", (NB + 2, BC * P), F16, kind="Internal").ap()
    atable = nc.dram_tensor("att_table", (NTP * P, ROWW), F32, kind="Internal").ap()

    with ExitStack() as ctx:
        def sb(name, shape, dt, where=ctx):
            return where.enter_context(nc.sbuf_tensor(name, shape, dt))

        def sem(name):
            return ctx.enter_context(nc.semaphore(name))

        X = sb("X", [P, (SPARE + 1) * D], F32)
        AG = sb("AG", [P, (SPARE + 1) * AGW], F32)
        identf = sb("identf", [P, P], F32)
        H = sb("H", [P, NTP, HX], F32)
        acc = sb("acc", [P, NTP, VAL], F32)
        sc = sb("sc", [P, 16], F32)
        g0 = ExitStack()
        lohi = sb("lohi", [P, NB + 1, 2, BC], F32, g0)
        asrc_idx = sb("asrc_idx", [P, NB + 2, BC], I32, g0)
        g0_end = nc.sbuf_base
        g0.close()
        A16 = sb("A16", [P, NTP, HX], F32)
        B16 = sb("B16", [P, NTP, HX], F32)
        m1 = sb("m1", [P, NTP], F32)
        m2 = sb("m2", [P, NTP], F32)
        m3 = sb("m3", [P, NTP], F32)
        scr4 = sb("scr4", [P, NTP, NX], F32)
        rank = sb("rank", [P, NTP, NX], F32)
        cmp = sb("cmp", [P, NTP], F32)
        pick = sb("pick", [P, NTP, NX], F32)
        s1 = sb("s1", [P, NTP], F32)
        s2 = sb("s2", [P, NTP], F32)
        dexp = sb("dexp", [P, NTP], F32)
        assert nc.sbuf_base < g0_end
        sb("rest_of_edges", [P, g0_end - nc.sbuf_base], mybir.dt.uint8)
        iota_lo = sb("iota_lo", [P, LO], F16)
        minus_node = sb("minus_node", [P, NJ], F32)
        consts = sb("consts", [P, 8], F32)
        W_sb = sb("W_sb", [P, 2, D], F32)
        WT = sb("WT", [P, 2, D], F32)
        Wg = sb("Wg", [P, 2, HX], F32)
        b_bc = sb("b_bc", [P, D], F32)
        wmax = sb("wmax", [P, 3], F32)
        esc = sb("esc", [P, 12], F32)
        small = sb("small", [P, 5, HX], F32)
        stats = sb("stats", [P, BT, 6], F32)
        mv = sb("mv", [P, BT, 2], F32)
        std = sb("std", [P, BT], F32)
        rstd = sb("rstd", [P, BT], F32)
        shift = sb("shift", [P, BT], F32)
        scratch = nc.sbuf_base

        g1 = ExitStack()
        ring = sb("ring", [P, 2 * CH, 2 * D + 2], F16, g1)
        OH = sb("OH", [P, CH, 2 * P], F16, g1)
        drel_all = sb("drel_all", [P, NG * CH], F32, g1)
        sidx_all = sb("sidx_all", [P, (NG + 2) * CH], I32, g1)
        drelw = sb("drelw", [P, CH], F32, g1)
        sstage = sb("sstage", [P, 2 * CH], I32, g1)
        info = sb("info", [1, 4 * NG], I32, g1)
        cols = sb("cols", [P, 16], I32, g1)
        colf = sb("colf", [P, 16], F32, g1)
        tri = sb("tri", [P, NG + 1], F32, g1)
        nat = ring[:, :, :].rearrange("p a b -> p (a b)").bitcast(F32)
        srcf = nat[0:NG, 0:GROUP]
        dstf = nat[0:NG, GROUP:2 * GROUP]
        srcn = nat[:, 2 * GROUP:3 * GROUP].bitcast(I32)
        dstn = nat[:, 3 * GROUP:4 * GROUP].bitcast(I32)
        tstage = sb("tstage", [P, BT, 2 * D], F16, g1)
        xs = sb("xs", [P, BT, D], F32, g1)
        y = sb("y", [P, D], F32, g1)
        yT = sb("yT", [P, 2, P], F32, g1)
        xnb = sb("xnb", [P, D], F32, g1)
        xT = sb("xT", [P, 2, P], F32, g1)
        dgs = sb("dgs", [P, 4], F32, g1)
        ready = sb("ready", [1, 8, NG // 2 + 2], F32, g1)
        turn = sb("turn", [1, NG // 2 + 3], I32, g1)
        W_see = sb("W_see", [P, 2, WIDE], F32, g1)
        b1_see = sb("b1_see", [NE_X * HID // P, P], F32, g1)
        wtmp = sb("wtmp", [P, 2], F32, g1)
        g1.close()

        g3 = ExitStack()
        S = sb("S", [P, 2, BC, LO], F16, g3)
        lob = sb("lob", [P, 2, BC * P], F16, g3)
        ST = sb("ST", [P, 2, NJ, BC * P], F16, g3)
        Hm = sb("Hm", [P, BC, HIV], F16, g3)
        M = sb("M", [P, 2, BC, 2 * HIV], F16, g3)
        iota_hi = sb("iota_hi", [P, HIV], F16, g3)
        zero_l = sb("zero_l", [P, P], F16, g3)
        rows = sb("rows", [P, 2, BC, ROWW], F32, g3)
        estage = sb("estage", [P, 2, 2 * BC], F32, g3)
        istage = sb("istage", [P, 2 * BC], I32, g3)
        sel = sb("sel", [P, BC, HEADS, NHI], F32, g3)
        adu = sb("adu", [P, BC, HEADS], F32, g3)
        ez = sb("ez", [P, BC, HEADS], F32, g3)
        ez2 = sb("ez2", [P, BC, HEADS], F32, g3)
        er = sb("er", [P, BC, HEADS], F32, g3)
        er2 = sb("er2", [P, BC, HEADS], F32, g3)
        wexp = sb("wexp", [P, BC, HEADS], F32, g3)
        val = sb("val", [P, BC, VAL], F32, g3)
        vh = sb("vh", [P, BC, 2, VAL], F16, g3)
        Tad = sb("Tad", [P, 2, NJ, NHI, HEADS], F16, g3)
        AS = sb("AS", [P, NTP, HEADS], F32, g3)
        AD = sb("AD", [P, NTP, HEADS], F32, g3)
        ADs = sb("ADs", [P, NTP, HEADS], F32, g3)
        NTB = sb("NTB", [P, NTP, ROWW], F32, g3)
        n1 = sb("n1", [P, NTP, HEADS], F32, g3)
        n2 = sb("n2", [P, NTP, HEADS], F32, g3)
        n3 = sb("n3", [P, NTP, HEADS], F32, g3)
        n4 = sb("n4", [P, NTP, HEADS], F32, g3)
        Rsh = sb("Rsh", [P, NTP, HEADS], F32, g3)
        ext = sb("ext", [P, 16], F32, g3)
        extr = sb("extr", [P, 16], F32, g3)
        Gk = sb("Gk", [P, HEADS], F32, g3)
        Gk1 = sb("Gk1", [P, HEADS], F32, g3)
        nlev = sb("nlev", [P, 1], I32, g3)
        g3.close()
        SF = S[:, :, :, :].rearrange("p a r n -> p (a r n)").bitcast(F32)
        L = SF[:, 0:NTP * VAL].rearrange("p (t f) -> p t f", f=VAL)
        tmp16 = SF[:, NTP * VAL:2 * NTP * VAL].rearrange("p (t f) -> p t f", f=VAL)

        g4 = ExitStack()
        W1h = sb("W1h", [P, 2, 2, NE_X, HID], F16, g4)
        W2h = sb("W2h", [P, 2, NE_X, HID // P, D], F16, g4)
        b1n = sb("b1n", [NE_X * HID // P, P], F32, g4)
        b1T = sb("b1T", [P, NE_X * HID // P], F32, g4)
        b2_bc = sb("b2_bc", [P, NE_X * D], F32, g4)
        hh_base = nc.sbuf_base
        hh = sb("hh", [P, 2, 2, HID // P, LO], F16, g4)
        hh32 = sb("hh32", [P, HID // P, LO], F32, g4)
        sb("wstage_rest", [P, HID // P, LO], F32, g4)
        gate = sb("gate", [P, NT * NX], F32, g4)
        gates = sb("gates", [P, NT * NX], F32, g4)
        g4.close()
        g4 = ExitStack()
        below_hh = hh_base - -(-scratch // 32) * 32
        sb("below_wstage", [P, below_hh], mybir.dt.uint8, g4)
        wstage1 = sb("wstage1", [P, 2, NE_X, HID], F32, g4)
        wstage2 = sb("wstage2", [P, NE_X, HID // P, D], F32, g4)
        g4.close()
        PS = ctx.enter_context(nc.psum_tensor("PS", [P, 8, 512], F32))

        pads_set = sem("pads_set")
        x_loaded = sem("x_loaded")
        edges_loaded = sem("edges_loaded")
        edges2_loaded = sem("edges2_loaded")
        small_loaded = sem("small_loaded")
        tslot_free = sem("tslot_free")
        lo_ready = sem("lo_ready")
        table_stored = sem("table_stored")
        ext_reduced = sem("ext_reduced")
        nlev_ready = sem("nlev_ready")
        atable_ready = sem("atable_ready")
        atable_stored = sem("atable_stored")
        level_end = sem("level_end")
        level_go = sem("level_go")
        exp_loaded = sem("exp_loaded")
        o_used = sem("o_used")
        stored = sem("stored")
        pool_steps = sem("pool_steps")
        iotas_ready = sem("iotas_ready")
        staged = sem("staged")
        pool_go = sem("pool_go")
        xT_ready = sem("xT_ready")
        xh_kept = sem("xh_kept")
        b1_in = sem("b1_in")
        see_free = sem("see_free")
        see_loaded = sem("see_loaded")
        w_split = sem("w_split")
        hi_hid = sem("hi_hid")
        bias_added = sem("bias_added")
        hid32_ready = sem("hid32_ready")
        ext_ready = sem("ext_ready")
        iota_hi_ready = sem("iota_hi_ready")
        estaged = sem("estaged")
        att_go = sem("att_go")
        stats_ready = sem("stats_ready")
        std_ready = sem("std_ready")
        rstd_ready = sem("rstd_ready")
        hi_ready = sem("hi_ready")
        idx_ready = sem("idx_ready")
        win_done = sem("win_done")
        scales_ready = sem("scales_ready")
        y_ready = sem("y_ready")
        yT_turned = sem("yT_turned")
        yT_ready = sem("yT_ready")
        node_stats = sem("node_stats")
        node_std = sem("node_std")
        xn_turned = sem("xn_turned")
        turned = sem("turned")
        lev_ready = sem("lev_ready")
        e_ready = sem("e_ready")
        w_ready = sem("w_ready")
        self_e = sem("self_e")
        self_w = sem("self_w")
        mg_ready = sem("mg_ready")
        mg_exp = sem("mg_exp")
        level_done = sem("level_done")
        act_go = sem("act_go")
        gate_in = sem("gate_in")
        gate_std_r = sem("gate_std_r")
        gate_exp = sem("gate_exp")
        exp_ready = sem("exp_ready")
        h_mm = sem("h_mm")
        hid_ready = sem("hid_ready")
        nat_ready = sem("nat_ready")
        nat_turned = sem("nat_turned")
        nat_evacuated = sem("nat_evacuated")
        info_turned = sem("info_turned")
        ef_ready = sem("ef_ready")
        ef_turned = sem("ef_turned")
        info_ready = sem("info_ready")
        wt_turned = sem("wt_turned")
        prep_done = sem("prep_done")
        agg_done = sem("agg_done")
        oh_ready = sem("oh_ready")
        mm_done = sem("mm_done")
        xn_ready = sem("xn_ready")
        h_done = sem("h_done")
        ad_done = sem("ad_done")
        acc_done = sem("acc_done")
        sums_ready = sem("sums_ready")
        pe_go = sem("pe_go")
        b1_turned = sem("b1_turned")
        o_mm = sem("o_mm")
        prep_steps = sem("prep_steps")
        info_zeroed = sem("info_zeroed")
        win_steps = sem("win_steps")
        drel_ready = sem("drel_ready")
        see_steps = sem("see_steps")
        left_steps = sem("left_steps")
        b1_steps = sem("b1_steps")
        att_steps = sem("att_steps")
        level_steps = sem("level_steps")
        dve_go = sem("dve_go")
        gate_steps = sem("gate_steps")
        sp_go = sem("sp_go")
        away_ready = sem("away_ready")
        rows_used = sem("rows_used")
        loh_ready = sem("loh_ready")
        lo_stored = sem("lo_stored")
        lob_in = [sem(f"lob_in{h}") for h in range(2)]
        turned_kept = sem("turned_kept")
        lo_hot_ready = sem("lo_hot_ready")
        spread_ready = sem("spread_ready")
        rows_in = [sem(f"rows_in{h}") for h in range(2)]
        arows_in = [sem(f"arows_in{h}") for h in range(2)]
        LEVEL_SEMS = [away_ready, rows_used, turned_kept, lo_hot_ready, spread_ready, estaged, att_go, turned, lev_ready, e_ready, w_ready, self_e, self_w, mg_ready, mg_exp, level_done, ad_done, acc_done, sums_ready, level_steps]
        block = ctx.enter_context(nc.Block())
        x_t = x[0:(NT - 1) * P, :].rearrange("(t p) d -> p t d", p=P)
        out_t = out[0:(NT - 1) * P, :].rearrange("(t p) d -> p t d", p=P)
        X3 = X[:, :].rearrange("p (t d) -> p t d", d=D)
        AG3 = AG[:, :].rearrange("p (t n) -> p t n", n=AGW)
        AGh = AG[:, :].bitcast(F16).rearrange("p (t n) -> p t n", n=2 * AGW)
        PSF = PS[:, :, :].rearrange("p a b -> p (a b)")

        YT, PROD, XNT, HOUT = 2 * 512, 3 * 512, 4 * 512, 5 * 512

        def left_over(eng):
            return (eng.value_load(turn[0:1, NI + 1:NI + 2], min_val=0, max_val=NT - 1),
                    eng.value_load(turn[0:1, NI + 2:NI + 3], min_val=1, max_val=NT))

        def tile_of(eng, j):
            return eng.value_load(turn[0:1, ds(j, 1)], min_val=0, max_val=SPARE)

        def nth_left(done, u):
            return nc.s_assert_within(done + u, 0, NT - 1, skip_runtime_bounds_check_because="done and left are NT together")

        def x_of(tile):
            return X[:, ds(tile * D, D)]

        table_t = table.rearrange("(t p) w -> p t w", p=P)
        atable_t = atable.rearrange("(t p) w -> p t w", p=P)

        AGf = AG[:, :]
        en = AGf[:, 0:2 * BC * P].bitcast(I32)
        eni = AGf[:, 2 * BC * P:4 * BC * P].bitcast(I32)
        ef = AGf[:, 4 * BC * P:7 * BC * P]
        E1 = BC * P
        EDGES_END = 7 * BC * P + BC * P // 2
        loh = AGf[:, 7 * BC * P:7 * BC * P + BC * P // 2].bitcast(F16)

        CHUNKS = (0, 2, 1, 3, 4, 5, 6, 7)

        def w_chunk(c):
            if c < 4:
                k, e = c // 2, c % 2 * 2
                return W1h[:, 0, k, e:e + 2, :], W1h[:, 1, k, e:e + 2, :], wstage1[:, k, e:e + 2, :], 0
            return W2h[:, 0, c - 4, :, :], W2h[:, 1, c - 4, :, :], wstage2[:, c - 4, :, :], 1

        def bcast(dram_row, n):
            return dram_row.to_broadcast([P, n])

        def flat(a):
            return a.rearrange("(a n) -> a n", a=1)

        @block.sync
        def _(sp):
            sp.wait_ge(pads_set, 2)
            for nat_t, e in ((srcn, src), (dstn, dst)):
                sp.dma_start(nat_t[0:NG - 1, :], e[0:(NG - 1) * GROUP].rearrange("(g e) -> g e", e=GROUP)).then_inc(edges_loaded, 16)
                sp.dma_start(nat_t[NG - 1:NG, 0:TAIL], flat(e[(NG - 1) * GROUP:NE])).then_inc(edges_loaded, 16)
            sp.dma_start(X3[0:LAST, NT - 1, :], x[(NT - 1) * P:N, :]).then_inc(x_loaded, 16)
            for a in range(4):
                q = (NT - 1) // 4
                sp.dma_start(X3[:, a * q:(a + 1) * q, :], x_t[:, a * q:(a + 1) * q, :]).then_inc(x_loaded, 16)
            for a in range(2):
                sp.dma_start(en[:, a * E1:(a + 1) * E1], edges[a:a + 1, :].rearrange("a (q e) -> (a q) e", e=E1)).then_inc(edges2_loaded, 16)
            sp.dma_start(W_sb[:, :, :], W.rearrange("(a p) i -> p a i", p=P)).then_inc(small_loaded, 16)
            sp.dma_start(Wg[:, :, :], W_gat.rearrange("(k p) c -> p k c", p=P)).then_inc(small_loaded, 16)
            sp.dma_start(b_bc[:, :], bcast(flat(b), D)).then_inc(small_loaded, 16)
            for a, row in enumerate((att_src.rearrange("h e -> (h e)"), att_dst.rearrange("h e -> (h e)"), b_gat, ln_g, ln_b)):
                sp.dma_start(small[:, a, :], bcast(flat(row), HX)).then_inc(small_loaded, 16)
            sp.sem_inc(tslot_free, 1)
            with sp.Fori(0, NT // BT) as i:
                for h, (k0, nk) in enumerate(BATCHES):
                    sp.wait_ge(lo_ready, i * 2 + (h + 1))
                    sp.dma_start(table_t[:, ds(i * BT + k0, nk), :], tstage[:, k0:k0 + nk, :]).then_inc(table_stored, 16)
                sp.wait_ge(table_stored, i * 32 + 32)
                sp.sem_inc(tslot_free, 1)
            sp.wait_ge(loh_ready, 1)
            sp.dma_start(lo_rows[0:NB, :], loh[:, :]).then_inc(lo_stored, 16)
            sp.dma_start(lo_rows[NB:NB + 2, :], loh[0:2, :]).then_inc(lo_stored, 16)
            sp.wait_ge(lo_stored, 32)
            sp.dma_start(b1_see[:, :], b1.rearrange("e (c p) -> (e c) p", p=P)).then_inc(b1_in, 16)
            W1_flat = W1.rearrange("e (q r) n -> (e q) (r n)", r=NE_X * D // P)
            W2_flat = W2.rearrange("e (q r) n -> (e q) (r n)", r=NE_X * HID // P)
            with sp.Fori(0, NI) as i:
                sp.wait_ge(see_free, i + 1)
                for a, flat_w in enumerate((W1_flat, W2_flat)):
                    sp.dma_start(W_see[:, a, :], flat_w[:, ds(i * WSTEP, WIDE)]).then_inc(see_loaded, 16)
            sp.wait_ge(ext_reduced, 1)
            sp.wait_ge(nlev_ready, 1)
            levels = sp.value_load(nlev[0:1, 0:1], min_val=1, max_val=1 << 17)
            with sp.Fori(0, levels) as lv:
                sp.dma_start(lob[:, 0, :], bcast(lo_rows[0:1, :], BC * P)).then_inc(lob_in[0], 16)
                sp.dma_start(lob[:, 1, :], bcast(lo_rows[1:2, :], BC * P)).then_inc(lob_in[1], 16)
                sp.wait_ge(atable_ready, lv + 1)
                sp.dma_start(atable_t, NTB[:, :, :]).then_inc(atable_stored, 16)
                with sp.Fori(0, NB // 2) as i:
                    for h in range(2):
                        sp.wait_ge(away_ready, i * 2 + (h + 1))
                        sp.dma_start(lob[:, h, :], bcast(lo_rows[ds(i * 2 + (h + 2), 1), :], BC * P)).then_inc(lob_in[h], 16)
                for h in range(2):
                    sp.wait_ge(lob_in[h], lv * LOB_LEVEL + LOB_LEVEL)
                sp.wait_ge(level_end, lv * 4 + 4)
                sp.sem_inc(sp_go, 1)
                for q in LEVEL_SEMS:
                    sp.sem_clear(q)
                sp.sem_inc(level_go, 1)
            for k in range(2):
                sp.dma_start(wstage1[:, k, :, :], W1[:, k * P:(k + 1) * P, :].rearrange("e p n -> p e n")).then_inc(exp_loaded, 16)
            for e in range(NE_X):
                sp.dma_start(wstage2[:, e, :, :], W2[e, :, :].rearrange("(c p) n -> p c n", p=P)).then_inc(exp_loaded, 16)
            sp.dma_start(b1n[:, :], b1.rearrange("e (c p) -> (e c) p", p=P)).then_inc(exp_loaded, 16)
            sp.dma_start(b2_bc[:, :], bcast(flat(b2.rearrange("e n -> (e n)")), NE_X * D)).then_inc(exp_loaded, 16)
            with sp.Fori(0, NT // NJ) as i:
                sp.wait_ge(o_used, i * 4 + 6)
                sp.dma_start(out_t[:, ds(i * NJ, NJ), :], X3[:, ds(i * NJ, NJ), :]).then_inc(stored, 16)
            sp.wait_ge(o_used, (NT // NJ) * 4 + 6)
            sp.dma_start(out[(NT - 1) * P:N, :], X3[0:LAST, NT - 1, :]).then_inc(stored, 16)
            sp.wait_ge(stored, 16 * (NT // NJ + 1))

        @block.gpsimd
        def _(pool):
            steps = Chain(pool, pool_steps)
            steps.link(nc.gpsimd.memset(identf[:, :], 0.0), nc.gpsimd.memset(tri[:, :], 0.0))
            nc.gpsimd.affine_select(out=identf[:, :], in_=identf[:, :], compare_op=ALU.not_equal, fill=1.0, base=0,
                                    pattern=[[-1, P]], channel_multiplier=1)
            nc.gpsimd.affine_select(out=tri[:, :], in_=tri[:, :], compare_op=ALU.is_ge, fill=1.0, base=0,
                                    pattern=[[-1, NG + 1]], channel_multiplier=1)
            nc.gpsimd.iota(minus_node[:, :], [[-P, NJ]], base=0, channel_multiplier=-1, allow_small_or_imprecise_dtypes=True)
            nc.gpsimd.iota(iota_lo[:, :], [[1, LO]], base=0, channel_multiplier=0,
                           allow_small_or_imprecise_dtypes=True).then_inc(iotas_ready, 1)
            with pool.Fori(0, NG // 2) as i:
                for h in range(2):
                    pool.wait_ge(staged, i * 2 + (h + 1))
                    pool.sem_inc(pool_go, 1)
                    pool.wait_ge(table_stored, 32 * (NT // BT))
                    for k in range(h * CH, (h + 1) * CH):
                        pool.indirect_dma_start(ring[:, k, 0:2 * D], None, table,
                                                bass.IndirectOffsetOnAxis(ap=sstage[:, k:k + 1], axis=0)).then_inc(rows_in[h], 16)
            pool.wait_ge(ext_ready, 1)
            nc.gpsimd.partition_all_reduce(extr[:, :], ext[:, :], P, RED.max).then_inc(ext_reduced, 1)
            nc.gpsimd.iota(iota_hi[:, :], [[1, NHI], [0, VAL]], base=0, channel_multiplier=0,
                           allow_small_or_imprecise_dtypes=True).then_inc(iota_hi_ready, 1)
            pool.wait_ge(nlev_ready, 1)
            levels = pool.value_load(nlev[0:1, 0:1], min_val=1, max_val=1 << 17)
            with pool.Fori(0, levels) as lv:
                pool.wait_ge(atable_stored, lv * 16 + 16)
                pool.sem_inc(pool_go, 1)
                with pool.Fori(0, NB // 2) as i:
                    for h in range(2):
                        pool.wait_ge(estaged, i * 2 + (h + 1))
                        pool.sem_inc(att_go, 1)
                        pool.wait_ge(iota_hi_ready, 1)
                        for k in range(BC):
                            pool.indirect_dma_start(rows[:, h, k, :], None, atable,
                                                    bass.IndirectOffsetOnAxis(ap=istage[:, h * BC + k:h * BC + k + 1], axis=0)).then_inc(arows_in[h], 16)
                for h in range(2):
                    pool.wait_ge(arows_in[h], lv * ROWS_LEVEL + ROWS_LEVEL)
                pool.sem_inc(level_end, 1)
                pool.wait_ge(level_go, lv + 1)
                pool.sem_inc(pool_go, 1)

        @block.scalar
        def _(act):
            act.wait_ge(pads_set, 2)
            with act.Fori(0, NT // BT) as i:
                for h, (k0, nk) in enumerate(BATCHES):
                    act.wait_ge(stats_ready, i * 2 + (h + 1))
                    nc.scalar.activation(std[:, k0:k0 + nk], mv[:, k0:k0 + nk, 1], ACT.Sqrt, bias=consts[:, 0:1]).then_inc(std_ready, 1)
                for h, (k0, nk) in enumerate(BATCHES):
                    act.wait_ge(rstd_ready, i * 2 + (h + 1))
                    if h == 0:
                        act.wait_ge(tslot_free, i + 1)
                    act.wait_ge(pads_set, 2)
                    for k in range(k0, k0 + nk):
                        last = nc.scalar.activation(tstage[:, k, D:2 * D], X3[:, ds(i * BT + k, 1), :].rearrange("p a d -> p (a d)"), ACT.Identity,
                                                    bias=shift[:, k:k + 1], scale=rstd[:, k:k + 1])
                    last.then_inc(hi_ready, 1)
            act.wait_ge(idx_ready, 1)
            def stage(i, h):
                before = act.value_load(info[0:1, ds(i * 2 + (NG + 2 + h), 1)], min_val=0, max_val=32 * NG)
                act.wait_ge(win_done, before + 1)
                act.wait_ge(idx_ready, 1)
                nc.scalar.copy(sstage[:, h * CH:(h + 1) * CH], sidx_all[:, ds((i * 2 + h) * CH, CH)]).then_inc(staged, 1)

            def mean(j, tile):
                act.wait_ge(scales_ready, j + 1)
                act.wait_ge(idx_ready, 1)
                nc.scalar.activation(y[:, :], AG[:, ds(tile * AGW, D)], ACT.Copy, scale=dgs[:, 2:3]).then_inc(y_ready, 1)

            def keep_yT(j):
                act.wait_ge(yT_turned, j + 1)
                nc.scalar.copy(yT[:, :, :].rearrange("p a n -> p (a n)"), PSF[:, YT:YT + D]).then_inc(yT_ready, 1)

            def deviation(j):
                act.wait_ge(node_stats, j + 1)
                nc.scalar.activation(std[:, 0:1], mv[:, 0, 1:2], ACT.Sqrt, bias=consts[:, 1:2], scale=XSCALE ** -2).then_inc(node_std, 1)

            def keep_xT(j):
                act.wait_ge(xn_turned, j + 1)
                nc.scalar.copy(xT[:, :, :].rearrange("p a n -> p (a n)"), PSF[:, XNT:XNT + D]).then_inc(xT_ready, 1)

            def keep_high(tile):
                nc.scalar.copy(AGh[:, ds(tile, 1), 0:D].rearrange("p a n -> p (a n)"), PSF[:, XNT:XNT + D]).then_inc(xh_kept, 1)

            stage(0, 0)
            stage(0, 1)
            mean(0, SPARE)
            keep_yT(0)
            deviation(0)
            with act.Fori(0, NI) as i:
                before, now = tile_of(act, i), tile_of(act, i + 1)
                stage(i + 1, 0)
                mean(i + 1, now)
                keep_xT(i)
                keep_yT(i + 1)
                keep_high(before)
                stage(i + 1, 1)
                deviation(i + 1)
            keep_xT(NI)
            keep_high(tile_of(act, NI))
            done, left = left_over(act)
            with act.Fori(0, left) as u:
                j, tile = u + (NI + 1), nth_left(done, u)
                mean(j, tile)
                keep_yT(j)
                deviation(j)
                keep_xT(j)
                keep_high(tile)
            act.wait_ge(nlev_ready, 1)
            levels = act.value_load(nlev[0:1, 0:1], min_val=1, max_val=1 << 17)
            with act.Fori(0, levels) as lv:

                def stage_rows(q, h):
                    nc.scalar.copy(istage[:, h * BC:(h + 1) * BC],
                                   asrc_idx[:, ds(q, 1), :].rearrange("p a r -> p (a r)")).then_inc(estaged, 1)

                def one_hot_columns(h):
                    for j in range(NJ):
                        last = nc.scalar.activation(ST[:, h, j, :], lob[:, h, :], ACT.Abs, bias=minus_node[:, j:j + 1])
                    last.then_inc(away_ready, 1)

                def cut(h):
                    flat_st = ST[:, h, :, :].rearrange("p j e -> p (j e)")
                    nc.scalar.activation(flat_st, flat_st, ACT.Relu, bias=1.0, scale=-1.0).then_inc(turned_kept, 1)

                act.wait_ge(nlev_ready, 1)
                stage_rows(0, 0)
                stage_rows(1, 1)
                for h in range(2):
                    act.wait_ge(lob_in[h], lv * LOB_LEVEL + 16)
                    one_hot_columns(h)
                    act.wait_ge(away_ready, h + 1)
                    cut(h)
                with act.Fori(0, NB // 2) as i:
                    for h in range(2):
                        act.wait_ge(e_ready, i * 2 + (h + 1))
                        nc.scalar.activation(wexp[:, :, :], ez[:, :, :], ACT.Exp).then_inc(w_ready, 1)
                        act.wait_ge(lob_in[h], lv * LOB_LEVEL + i * 16 + 32)
                        act.wait_ge(ad_done, i * 2 + (h + 1))
                        one_hot_columns(h)
                        act.wait_ge(rows_used, i * 2 + (h + 1))
                        act.wait_ge(lev_ready, 1)
                        stage_rows(i * 2 + (h + 2), h)
                        act.wait_ge(away_ready, i * 2 + (h + 3))
                        cut(h)
                act.wait_ge(self_e, 1)
                nc.scalar.activation(n3[:, :, :], n2[:, :, :], ACT.Exp).then_inc(self_w, 1)
                act.wait_ge(mg_ready, 1)
                nc.scalar.activation(n4[:, :, :], n2[:, :, :], ACT.Exp).then_inc(mg_exp, 1)
                act.wait_ge(level_done, 1)
                act.sem_inc(level_end, 1)
                act.wait_ge(level_go, lv + 1)
                act.sem_inc(act_go, 1)
            act.wait_ge(gate_in, 1)
            nc.scalar.activation(m3[:, :], m2[:, :], ACT.Sqrt, bias=consts[:, 0:1]).then_inc(gate_std_r, 1)
            act.wait_ge(gate_in, 2)
            nc.scalar.activation(dexp[:, :], cmp[:, :], ACT.Exp).then_inc(gate_exp, 1)
            act.wait_ge(exp_ready, 1)
            act.wait_ge(exp_loaded, 16 * (2 + NE_X + 2))
            for c in CHUNKS:
                hi, lo, st, a = w_chunk(c)
                nc.scalar.activation(hi, st, ACT.Copy, scale=esc[:, a:a + 1]).then_inc(w_split, 1)
            act.wait_ge(exp_ready, 3)

            def hidden(base, w):
                for e in range(NE_X):
                    act.wait_ge(o_mm, base * 4 + (e + 1))
                    for c in range(HID // P + 1):
                        if c < HID // P:
                            act.wait_ge(h_mm, base * 16 + (e * 4 + c + 1))
                            act.wait_ge(hid_ready, base * 16 + (e * 4 + c + 1))
                            nc.scalar.activation(hh32[:, c, 0:w], PS[:, c, 0:w], ACT.Gelu,
                                                 bias=b1T[:, e * 4 + c:e * 4 + c + 1], scale=esc[:, 2:3]).then_inc(hid32_ready, 1)
                        if c > 0:
                            act.wait_ge(hid32_ready, base * 16 + (e * 4 + c))
                            nc.scalar.activation(hh[:, e % 2, 0, c - 1, 0:w], hh32[:, c - 1, 0:w], ACT.Copy, scale=esc[:, 3:4]).then_inc(hi_hid, 1)

            with act.Fori(0, NT // NJ) as i:
                hidden(i, LO)
            hidden(NT // NJ, P)

        @block.tensor
        def _(pe):
            pe.wait_ge(iotas_ready, 1)
            pe.wait_ge(nat_ready, 1)
            for r in range(8):
                for k in range(4):
                    f = (srcf, dstf)[r // 4][:, ((r % 4) * 4 + k) * P:((r % 4) * 4 + k + 1) * P]
                    last = nc.tensor.transpose(PS[:, r, k * NG:(k + 1) * NG], f, identf[0:NG, 0:NG])
                last.then_inc(nat_turned, 1)
            pe.wait_ge(nat_evacuated, 8)
            nc.tensor.matmul(PS[0:1, 0, 0:NG], colf[0:NG, 2:3], identf[0:NG, 0:NG], start=True, stop=True)
            nc.tensor.matmul(PS[0:1, 1, 0:NG + 1], colf[0:NG, 5:6], tri[0:NG, 0:NG + 1], start=True, stop=True).then_inc(info_turned, 1)
            pe.sem_inc(win_done, 1)
            pe.wait_ge(ef_ready, 1)
            for r in range(6):
                for k in range(4):
                    last = nc.tensor.transpose(PS[:, 2 + r, k * P:(k + 1) * P], ef[:, (r * 4 + k) * P:(r * 4 + k + 1) * P], identf[:, :])
                last.then_inc(ef_turned, 1)
            pe.wait_ge(info_ready, 1)
            pe.wait_ge(small_loaded, 16 * 8)
            for kin in range(2):
                for a in range(2):
                    last = nc.tensor.transpose(PS[:, 0, (kin * 2 + a) * P:(kin * 2 + a + 1) * P], W_sb[:, a, kin * P:(kin + 1) * P], identf[:, :])
            last.then_inc(wt_turned, 1)
            pe.wait_ge(prep_done, 1)
            def turn_y(j):
                pe.wait_ge(y_ready, j + 1)
                for a in range(2):
                    last = nc.tensor.transpose(PSF[:, YT + a * P:YT + (a + 1) * P], y[:, a * P:(a + 1) * P], identf[:, :])
                last.then_inc(yT_turned, 1)

            def through_W(j):
                pe.wait_ge(yT_ready, j + 1)
                for a in range(2):
                    last = nc.tensor.matmul(PSF[:, PROD:PROD + D], yT[:, a, :], WT[:, a, :], start=(a == 0), stop=(a == 1))
                last.then_inc(mm_done, 1)

            def turn_xn(j):
                pe.wait_ge(xn_ready, j + 1)
                for a in range(2):
                    last = nc.tensor.transpose(PSF[:, XNT + a * P:XNT + (a + 1) * P], xnb[:, a * P:(a + 1) * P], identf[:, :])
                last.then_inc(xn_turned, 1)

            def h_product(j):
                pe.wait_ge(xT_ready, j + 1)
                for a in range(2):
                    last = nc.tensor.matmul(PSF[:, HOUT:HOUT + HX], xT[:, a, :], Wg[:, a, :], start=(a == 0), stop=(a == 1))
                last.then_inc(h_done, 1)

            turn_y(0)
            through_W(0)
            with pe.Fori(0, NG // 2) as i:
                for h in range(2):
                    w0 = pe.value_load(info[0:1, ds(i * 2 + (NG + 3 + h), 1)], min_val=0, max_val=32 * NG)
                    w1 = pe.value_load(info[0:1, ds(i * 2 + (NG + 4 + h), 1)], min_val=1, max_val=32 * NG)
                    pe.wait_ge(rows_in[h], i * (16 * CH) + 16 * CH)
                    pe.sem_inc(pe_go, 1)
                    with pe.Fori(w0, w1) as v:
                        pe.wait_ge(agg_done, v + 1)
                        pe.wait_ge(oh_ready, v + 1)
                        for k in range(CH):
                            for t in range(2):
                                oh = OH[:, k, t * P:(t + 1) * P]
                                nc.tensor.matmul(PS[:, t, 0:AGW], oh, ring[:, h * CH + k, D:2 * D + 1], start=(k == 0), stop=False, skip_group_check=True)
                                last = nc.tensor.matmul(PS[:, t, 0:D], oh, ring[:, h * CH + k, 0:D], start=False, stop=(k == CH - 1), skip_group_check=True)
                        last.then_inc(win_done, 1)
                    if h == 0:
                        turn_xn(i)
                        turn_y(i + 1)
                        h_product(i)
                        through_W(i + 1)
            turn_xn(NI)
            h_product(NI)
            done, left = left_over(pe)
            with pe.Fori(0, left) as u:
                j = u + (NI + 1)
                turn_y(j)
                through_W(j)
                turn_xn(j)
                h_product(j)
            pe.wait_ge(nlev_ready, 1)
            levels = pe.value_load(nlev[0:1, 0:1], min_val=1, max_val=1 << 17)
            with pe.Fori(0, levels) as lv:

                def look_up(h):
                    for r in range(BC):
                        for j in range(NJ):
                            for part in range(2):
                                last = nc.tensor.matmul(PS[:, 4 + h, r * NHI * HEADS:(r + 1) * NHI * HEADS], ST[:, h, j, r * P:(r + 1) * P],
                                                        Tad[:, part, j, :, :].rearrange("p a b -> p (a b)"),
                                                        start=(j == 0 and part == 0), stop=(j == NJ - 1 and part == 1))
                    last.then_inc(ad_done, 1)

                def add_up(h):
                    for r in range(BC):
                        for j in range(NJ):
                            for part in range(2):
                                last = nc.tensor.matmul(PS[:, j, 0:HIV], S[:, h, r, j * P:(j + 1) * P], M[:, h, r, part * HIV:(part + 1) * HIV],
                                                        start=False, stop=False, skip_group_check=True)
                    last.then_inc(acc_done, 1)

                def clear_sums(start):
                    for j in range(NJ):
                        last = nc.tensor.matmul(PS[:, j, 0:HIV], zero_l[:, :], iota_hi[:, 0:HIV], start=start, stop=not start, skip_group_check=True)
                    return last

                pe.wait_ge(lev_ready, 1)
                clear_sums(True).then_inc(acc_done, 2)
                pe.wait_ge(turned_kept, 1)
                look_up(0)
                with pe.Fori(0, NB // 2) as i:
                    for h in range(2):
                        pe.wait_ge(turned_kept, i * 2 + (h + 2))
                        pe.wait_ge(spread_ready, i * 2 + (h + 1))
                        look_up(1 - h)
                        pe.wait_ge(lo_hot_ready, i * 2 + (h + 1))
                        pe.wait_ge(spread_ready, i * 2 + (h + 2))
                        add_up(h)
                clear_sums(False).then_inc(sums_ready, 1)
                pe.wait_ge(level_done, 1)
                pe.sem_inc(level_end, 1)
                pe.wait_ge(level_go, lv + 1)
                pe.sem_inc(pe_go, 1)
            pe.wait_ge(exp_loaded, 16 * (2 + NE_X + 2))
            nb1 = NE_X * HID // P
            nc.tensor.transpose(PS[:, 7, 0:nb1], b1n[:, :], identf[0:nb1, 0:nb1]).then_inc(b1_turned, 1)
            pe.wait_ge(exp_ready, 2)
            pe.sem_inc(o_mm, 2)

            def hid_products(e, base, tile0, nt):
                for c in range(HID // P):
                    if e > 0:
                        pe.wait_ge(hid32_ready, base * 16 + ((e - 1) * 4 + c + 1))
                    for a in range(2):
                        for wpart, xpart in ((0, 0), (0, 1), (1, 0)):
                            rhs = AGh[:, ds(tile0, nt), xpart * D + a * P:xpart * D + (a + 1) * P]
                            last = nc.tensor.matmul(PS[:, c, 0:nt * P], W1h[:, wpart, a, e, c * P:(c + 1) * P], rhs,
                                                    start=(a == 0 and wpart + xpart == 0), stop=(a == 1 and wpart == 1))
                    last.then_inc(h_mm, 1)

            def out_products(e, base, nt):
                pe.wait_ge(o_used, base * 4 + (e + 1))
                pe.wait_ge(hid_ready, base * 16 + (e * 4 + 8))
                for t in range(nt):
                    o = PS[:, 4 + 2 * (e % 2) + t // 2, (t % 2) * D:(t % 2 + 1) * D]
                    for c in range(HID // P):
                        for hpart, wpart in ((0, 0), (0, 1), (1, 0)):
                            last = nc.tensor.matmul(o, hh[:, e % 2, hpart, c, t * P:(t + 1) * P], W2h[:, wpart, e, c, :],
                                                    start=(c == 0 and hpart + wpart == 0), stop=(c == HID // P - 1 and hpart == 1))
                last.then_inc(o_mm, 1)

            def experts(base, tile0, nt):
                hid_products(0, base, tile0, nt)
                for e in range(1, NE_X):
                    hid_products(e, base, tile0, nt)
                    out_products(e - 1, base, nt)
                out_products(NE_X - 1, base, nt)

            with pe.Fori(0, NT // NJ) as i:
                experts(i, i * NJ, NJ)
            experts(NT // NJ, (NT // NJ) * NJ, 1)

        @block.vector
        def _(v):
            vec = nc.vector
            steps = Chain(v, prep_steps)
            link = steps.link
            vec.memset(X3[:, NT - 1:SPARE + 1, :], 0.0)
            vec.memset(consts[:, 0:1], EPS)
            vec.memset(consts[:, 1:2], EPS * XSCALE ** -2)
            vec.memset(srcn[P - 32:P, :], 0).then_inc(pads_set, 1)
            vec.memset(dstn[P - 32:P, :], PADN).then_inc(pads_set, 1)
            v.wait_ge(edges_loaded, 64)
            link(vec.tensor_scalar(dstf, dstn[0:NG, :], PADN, None, ALU.min),
                 vec.tensor_scalar(srcf, srcn[0:NG, :], N - 1, None, ALU.min))
            link(vec.tensor_reduce(colf[0:NG, 0:1], dstf, AX.X, ALU.min), vec.tensor_reduce(colf[0:NG, 1:2], dstf, AX.X, ALU.max))
            link(vec.tensor_copy(cols[0:NG, 0:2], colf[0:NG, 0:2]))
            link(vec.tensor_scalar(cols[0:NG, 2:4], cols[0:NG, 0:2], 7, None, ALU.arith_shift_right))
            link(vec.tensor_copy(colf[0:NG, 2:4], cols[0:NG, 2:4]))
            link(vec.tensor_tensor(cols[0:NG, 4:5], colf[0:NG, 3:4], colf[0:NG, 2:3], ALU.subtract),
                 vec.tensor_scalar(colf[0:NG, 6:7], colf[0:NG, 2:3], float(P), None, ALU.mult))
            link(vec.tensor_scalar(cols[0:NG, 5:6], cols[0:NG, 4:5], 1, None, ALU.arith_shift_right))
            link(vec.tensor_scalar(colf[0:NG, 5:6], cols[0:NG, 5:6], 1.0, None, ALU.add),
                 vec.tensor_scalar(dstf, dstf, colf[0:NG, 6:7], None, ALU.subtract))
            v.sem_inc(nat_ready, 1)
            for r in range(8):
                v.wait_ge(nat_turned, r + 1)
                to = (sidx_all, drel_all)[r // 4][:, 0:NG * CH].rearrange("p (g k) -> p k g", k=CH)[:, 4 * (r % 4):4 * (r % 4) + 4, :]
                vec.tensor_copy(to, PS[:, r, 0:4 * NG].rearrange("p (k g) -> p k g", k=4)).then_inc(nat_evacuated, 1)
            vec.memset(info[0:1, :], 0).then_inc(info_zeroed, 1)
            v.wait_ge(info_turned, 1)
            v.wait_ge(info_zeroed, 1)
            link(vec.tensor_copy(info[0:1, 0:NG], PS[0:1, 0, 0:NG]), vec.tensor_copy(info[0:1, NG + 3:2 * NG + 4], PS[0:1, 1, 0:NG + 1]))
            R = [ready[0:1, a, :] for a in range(8)]
            pairs = info[0:1, 0:NG].rearrange("o (i two) -> o i two", two=2)
            link(vec.memset(sidx_all[:, NG * CH:(NG + 2) * CH], 0), vec.memset(ready[:, :, :], 0.0), vec.memset(turn[:, :], SPARE))
            link(vec.tensor_tensor(R[0][:, 0:NI], pairs[:, :, 0], pairs[:, :, 1], ALU.min))
            a, far = 0, 1
            while far < NI:
                link(vec.tensor_tensor(R[1 - a][:, 0:NI - far], R[a][:, 0:NI - far], R[a][:, far:NI], ALU.min),
                     vec.tensor_copy(R[1 - a][:, NI - far:NI], R[a][:, NI - far:NI]))
                a, far = 1 - a, far * 2
            link(vec.tensor_scalar(R[3][:, 0:NI], iota_lo[0:1, 0:NI], float(LAG), 0.0, ALU.subtract, ALU.max),
                 vec.tensor_scalar(R[2][:, 0:NI + 1], iota_lo[0:1, 0:NI + 1], 1.0, None, ALU.add))
            link(vec.tensor_tensor(R[4][:, 0:NI], R[a][:, 0:NI], R[3][:, 0:NI], ALU.min))
            link(vec.tensor_tensor(R[a][:, 0:NI], R[4][:, 0:NI], R[2][:, 0:NI], ALU.subtract))
            far = 1
            while far < NI:
                link(vec.tensor_tensor(R[1 - a][:, far:NI], R[a][:, far:NI], R[a][:, 0:NI - far], ALU.min),
                     vec.tensor_copy(R[1 - a][:, 0:far], R[a][:, 0:far]))
                a, far = 1 - a, far * 2
            link(vec.tensor_tensor(R[5][:, 1:NI + 1], R[a][:, 0:NI], R[2][:, 0:NI], ALU.add))
            link(vec.tensor_tensor(R[6][:, 0:NI], R[5][:, 1:NI + 1], R[5][:, 0:NI], ALU.subtract),
                 vec.tensor_scalar(R[7][:, 0:NI], R[5][:, 0:NI], float(SPARE), None, ALU.subtract))
            link(vec.tensor_tensor(R[7][:, 0:NI], R[7][:, 0:NI], R[6][:, 0:NI], ALU.mult))
            link(vec.tensor_scalar(turn[:, 1:NI + 1], R[7][:, 0:NI], float(SPARE), None, ALU.add),
                 vec.tensor_copy(turn[:, NI + 1:NI + 2], R[5][:, NI:NI + 1]),
                 vec.tensor_scalar(turn[:, NI + 2:NI + 3], R[5][:, NI:NI + 1], -1.0, float(NT), ALU.mult, ALU.add))
            v.wait_ge(nat_evacuated, 8)
            v.sem_inc(idx_ready, 1)
            v.sem_inc(info_ready, 1)
            link(vec.memset(AG[:, EDGES_END:], 0.0))
            v.wait_ge(x_loaded, 16 * 5)
            v.wait_ge(pads_set, 2)
            with steps.loop(NT // BT, 12) as i:

                def tile(k):
                    return X3[:, ds(i * BT + k, 1), :].rearrange("p a d -> p (a d)")

                for h, (k0, nk) in enumerate(BATCHES):
                    link(*[vec.bn_stats(stats[:, k, :], tile(k)) for k in range(k0, k0 + nk)])
                    v.sem_inc(dve_go, 1)
                    link(*[vec.bn_aggr(mv[:, k, :], stats[:, k, :]) for k in range(k0, k0 + nk)])
                    v.sem_inc(stats_ready, 1)
                for h, (k0, nk) in enumerate(BATCHES):
                    ks = slice(k0, k0 + nk)
                    v.wait_ge(std_ready, i * 2 + (h + 1))
                    link(vec.reciprocal(rstd[:, ks], std[:, ks]))
                    link(vec.tensor_scalar(rstd[:, ks], rstd[:, ks], TAB_SCALE, None, ALU.mult))
                    link(vec.scalar_tensor_tensor(shift[:, ks], mv[:, ks, 0], -1.0, rstd[:, ks], ALU.mult, ALU.mult))
                    v.sem_inc(rstd_ready, 1)
                    link(*[vec.tensor_scalar(xs[:, k, :], tile(k), mv[:, k, 0:1], rstd[:, k:k + 1], ALU.subtract, ALU.mult) for k in range(k0, k0 + nk)])
                for h, (k0, nk) in enumerate(BATCHES):
                    ks = slice(k0, k0 + nk)
                    v.wait_ge(hi_ready, i * 2 + (h + 1))
                    vec.tensor_tensor(tstage[:, ks, 0:D], xs[:, ks, :], tstage[:, ks, D:2 * D], ALU.subtract).then_inc(lo_ready, 1)
            v.wait_ge(edges2_loaded, 32)
            link(vec.tensor_scalar(eni[:, 0:E1], en[:, E1:2 * E1], LO - 1, None, ALU.bitwise_and),
                 vec.tensor_scalar(eni[:, E1:2 * E1], en[:, E1:2 * E1], int(np.log2(LO)), None, ALU.arith_shift_right),
                 vec.tensor_scalar(ef[:, 0:E1], en[:, 0:E1], N - 1, None, ALU.min))
            link(vec.tensor_copy(ef[:, E1:3 * E1], eni[:, :]), vec.tensor_copy(loh, eni[:, 0:E1]),
                 vec.memset(asrc_idx[:, NB:NB + 2, :], 0), vec.memset(lohi[:, NB:NB + 1, :, :], 0.0))
            v.sem_inc(ef_ready, 1)
            v.sem_inc(loh_ready, 1)
            for r in range(6):
                v.wait_ge(ef_turned, r + 1)
                turn4 = PS[:, 2 + r, :].rearrange("p (k q) -> p k q", k=4)
                ks = slice(4 * (r % 2), 4 * (r % 2) + 4)
                to = asrc_idx[:, 0:NB, ks].rearrange("p q r -> p r q") if r < 2 else lohi[:, 0:NB, r // 2 - 1, ks].rearrange("p q r -> p r q")
                last = vec.tensor_copy(to, turn4)
            link(last)
            v.wait_ge(wt_turned, 1)
            link(vec.tensor_copy(WT[:, :, :].rearrange("p a n -> p (a n)"), PS[:, 0, :]),
                 vec.memset(ring[:, :, 2 * D:2 * D + 1], 1.0))
            v.wait_ge(lo_stored, 32)
            vec.memset(AG[:, 0:EDGES_END], 0.0).then_inc(agg_done, 1)
            v.wait_ge(agg_done, 1)
            v.sem_inc(prep_done, 1)
            def scales(tile):
                deg = AG[:, ds(tile * AGW + D, 1)]
                steps.link(vec.tensor_scalar(dgs[:, 0:1], deg, 1.0, None, ALU.add))
                steps.link(vec.reciprocal(dgs[:, 1:2], dgs[:, 0:1]))
                steps.link(vec.tensor_scalar(dgs[:, 2:3], dgs[:, 1:2], 1.0 / TAB_SCALE, None, ALU.mult),
                           vec.tensor_tensor(dgs[:, 3:4], dgs[:, 1:2], deg, ALU.mult))
                v.sem_inc(scales_ready, 1)

            def add_means(j, tile):
                v.wait_ge(mm_done, j + 1)
                steps.link(vec.tensor_tensor(x_of(tile), x_of(tile), PSF[:, PROD:PROD + D], ALU.add))
                steps.link(vec.scalar_tensor_tensor(x_of(tile), b_bc[:, :], dgs[:, 3:4], x_of(tile), ALU.mult, ALU.add))
                v.sem_inc(dve_go, 1)
                steps.link(vec.bn_stats(stats[:, 0, :], x_of(tile)))
                v.sem_inc(dve_go, 1)
                steps.link(vec.bn_aggr(mv[:, 0, :], stats[:, 0, :]))
                v.sem_inc(node_stats, 1)

            def normalise(j, tile):
                v.wait_ge(node_std, j + 1)
                steps.link(vec.reciprocal(rstd[:, 0:1], std[:, 0:1]))
                steps.link(vec.tensor_scalar(xnb[:, :], x_of(tile), mv[:, 0, 0:1], rstd[:, 0:1], ALU.subtract, ALU.mult))
                v.sem_inc(xn_ready, 1)

            def keep_h(j, tile):
                v.wait_ge(h_done, j + 1)
                at = AGh[:, ds(tile, 1), :].rearrange("p a n -> p (a n)")
                steps.mark(vec.tensor_scalar(H[:, ds(tile, 1), :].rearrange("p a n -> p (a n)"), PSF[:, HOUT:HOUT + HX], 1.0 / XSCALE, None, ALU.mult))
                v.wait_ge(xh_kept, j + 1)
                steps.link(vec.tensor_tensor(at[:, D:2 * D], xT[:, :, :].rearrange("p a n -> p (a n)"), at[:, 0:D], ALU.subtract))

            v.wait_ge(small_loaded, 16 * 8)
            steps = Chain(v, see_steps)
            link = steps.link
            link(vec.memset(wmax[:, :], 0.0))
            v.sem_inc(see_free, 1)

            def see(i):
                v.wait_ge(see_loaded, i * 32 + 32)
                steps.link(vec.tensor_reduce(wtmp[:, :], W_see[:, :, :], AX.X, ALU.max, apply_absolute_value=True))
                steps.link(vec.tensor_tensor(wmax[:, 0:2], wmax[:, 0:2], wtmp[:, :], ALU.max))
                v.sem_inc(see_free, 1)

            def window_rows():
                for k in range(CH):
                    last = vec.tensor_scalar(OH[:, k, :], iota_lo[:, 0:2 * P], drelw[:, k:k + 1], None, ALU.is_equal)
                last.then_inc(oh_ready, 1)

            def move_window(w):
                v.wait_ge(oh_ready, w + 1)
                vec.tensor_scalar(drelw[:, :], drelw[:, :], 2.0 * P, None, ALU.subtract).then_inc(win_steps, 1)
                v.wait_ge(win_steps, w + 1)

            def add_window(w, tile):
                v.wait_ge(win_done, w + 2)
                at = AG[:, ds(tile * AGW, 2 * AGW)].rearrange("p (t n) -> p t n", t=2)
                vec.tensor_tensor(at, at, PS[:, 0:2, 0:AGW], ALU.add).then_inc(agg_done, 1)
                v.wait_ge(agg_done, w + 2)
                v.sem_inc(dve_go, 1)

            scales(SPARE)
            add_means(0, SPARE)
            with steps.loop(NI, 13) as i:
                for h in range(2):
                    vec.tensor_copy(drelw[:, :], drel_all[:, ds((i * 2 + h) * CH, CH)]).then_inc(drel_ready, 1)
                    v.wait_ge(drel_ready, i * 2 + (h + 1))
                    window_rows()
                    w0 = v.value_load(info[0:1, ds(i * 2 + (NG + 3 + h), 1)], min_val=0, max_val=32 * NG)
                    w1 = v.value_load(info[0:1, ds(i * 2 + (NG + 4 + h), 1)], min_val=1, max_val=32 * NG)
                    t0 = v.value_load(info[0:1, ds(i * 2 + h, 1)], min_val=0, max_val=NT - 1)
                    move_window(w0)
                    if h == 0:
                        before, now = tile_of(v, i), tile_of(v, i + 1)
                        normalise(i, before)
                        scales(now)
                    else:
                        add_means(i + 1, now)
                        keep_h(i, before)
                        see(i)
                    add_window(w0, t0)
                    with v.If(w0 + 1 < w1):
                        with v.Fori(w0 + 1, w1) as w:
                            window_rows()
                            move_window(w)
                            add_window(w, nc.s_assert_within(t0 + (w - w0) * 2, 0, NT - 1,
                                                             skip_runtime_bounds_check_because="the windows of a group end with its last tile"))
            normalise(NI, tile_of(v, NI))
            keep_h(NI, tile_of(v, NI))
            done, left = left_over(v)
            steps = Chain(v, left_steps)
            link = steps.link
            with steps.loop(left, 11) as u:
                j, tile = u + (NI + 1), nth_left(done, u)
                scales(tile)
                add_means(j, tile)
                normalise(j, tile)
                keep_h(j, tile)
            steps = Chain(v, b1_steps)
            link = steps.link
            v.wait_ge(b1_in, 16)
            link(vec.tensor_reduce(wmax[0:NE_X * HID // P, 2:3], b1_see[:, :], AX.X, ALU.max, apply_absolute_value=True))
            steps = Chain(v, att_steps)
            link = steps.link
            ops = lambda o, a, b_, op: vec.tensor_tensor(o, a, b_, op)
            link(vec.memset(H[:, NT:NTP, :], 0.0), vec.memset(acc[:, :, :], 0.0), vec.memset(Rsh[:, :, :], 0.0),
                 vec.memset(zero_l[:, :], 0.0), vec.memset(ext[:, :], 0.0))
            for a, to in ((0, AS), (1, AD)):
                link(ops(tmp16[:, :, 0:HX], H[:, :, :], small[:, a:a + 1, :].to_broadcast([P, NTP, HX]), ALU.mult))
                link(vec.tensor_reduce(to[:, :, :], tmp16[:, :, 0:HX].rearrange("p t (h e) -> p t h e", e=NX), AX.X, ALU.add))
            link(vec.tensor_reduce(ext[:, 0:4], AS[:, :, :].rearrange("p t h -> p h t"), AX.X, ALU.max),
                 vec.tensor_reduce(ext[:, 4:8], AS[:, :, :].rearrange("p t h -> p h t"), AX.X, ALU.min),
                 vec.tensor_reduce(ext[:, 8:9], AD[:, :, :].rearrange("p t h -> p (t h)"), AX.X, ALU.max, apply_absolute_value=True),
                 vec.tensor_reduce(ext[:, 9:10], H[:, :, :].rearrange("p t h -> p (t h)"), AX.X, ALU.max, apply_absolute_value=True))
            link(vec.tensor_scalar(ext[:, 4:8], ext[:, 4:8], -1.0, None, ALU.mult), vec.tensor_copy(ext[:, 10:13], wmax[:, :]))
            v.sem_inc(ext_ready, 1)
            v.wait_ge(ext_reduced, 1)
            link(vec.tensor_scalar(sc[:, 0:2], extr[:, 8:10], 1e-25, None, ALU.max),
                 vec.tensor_tensor(n1[:, 0, :], extr[:, 0:4], extr[:, 4:8], ALU.add))
            link(vec.reciprocal(sc[:, 2:4], sc[:, 0:2]), vec.tensor_reduce(sc[:, 8:9], n1[:, 0, :], AX.X, ALU.max))
            link(vec.tensor_scalar(sc[:, 4:5], sc[:, 2:3], FULL, None, ALU.mult), vec.tensor_scalar(sc[:, 5:6], sc[:, 0:1], 1.0 / FULL, None, ALU.mult),
                 vec.tensor_scalar(sc[:, 6:7], sc[:, 3:4], FULL, None, ALU.mult), vec.tensor_scalar(sc[:, 7:8], sc[:, 1:2], 1.0 / FULL, None, ALU.mult),
                 vec.tensor_scalar(nlev[:, :], sc[:, 8:9], 1.0 / LEVEL, 1.0, ALU.mult, ALU.add))
            v.sem_inc(nlev_ready, 1)
            NT5 = NTB[:, :, HEADS:ROWW].rearrange("p t (h e) -> p t h e", e=1 + NX)
            link(vec.tensor_scalar(ADs[:, :, :], AD[:, :, :], sc[:, 4:5], None, ALU.mult),
                 vec.memset(NTB[:, :, :], DEN_SCALE), vec.tensor_copy(Gk[:, :], extr[:, 0:4]))
            Tp = [Tad[:, a, :, :, :].rearrange("p j t h -> p t j h") for a in range(2)]
            AD4 = ADs[:, :, :].rearrange("p (t j) h -> p t j h", j=NJ)
            link(*[vec.tensor_scalar(NT5[:, :, hd, 1:1 + NX], H[:, :, hd * NX:(hd + 1) * NX], sc[:, 6:7], None, ALU.mult) for hd in range(HEADS)])
            link(*[vec.tensor_copy(Tp[0][:, :, j, :], AD4[:, :, j, :]) for j in range(NJ)])
            link(*[ops(Tp[1][:, :, j, :], AD4[:, :, j, :], Tp[0][:, :, j, :], ALU.subtract) for j in range(NJ)])
            v.wait_ge(iota_hi_ready, 1)
            levels = v.value_load(nlev[0:1, 0:1], min_val=1, max_val=1 << 17)
            NTH = [P, NTP, HEADS]
            with v.Fori(0, levels) as lv:
                steps = Chain(v, level_steps)
                link = steps.link
                Gb = Gk[:, :].unsqueeze(1).to_broadcast(NTH)
                link(vec.tensor_scalar(Gk1[:, :], Gk[:, :], LEVEL, None, ALU.subtract), ops(n3[:, :, :], AS[:, :, :], Gb, ALU.is_le),
                     ops(n1[:, :, :], AD[:, :, :], Gb, ALU.add))
                link(ops(n2[:, :, :], AS[:, :, :], Gk1[:, :].unsqueeze(1).to_broadcast(NTH), ALU.is_gt))
                link(ops(n2[:, :, :], n2[:, :, :], n3[:, :, :], ALU.mult))
                link(ops(NTB[:, :, 0:HEADS], AS[:, :, :], n2[:, :, :], ALU.mult), vec.tensor_scalar(n3[:, :, :], n2[:, :, :], 1.0, BIG, ALU.subtract, ALU.mult))
                link(ops(NTB[:, :, 0:HEADS], NTB[:, :, 0:HEADS], n3[:, :, :], ALU.add))
                v.sem_inc(atable_ready, 1)
                v.sem_inc(lev_ready, 1)

                def copy_stage(q, h):
                    link(vec.tensor_copy(estage[:, h, :], lohi[:, ds(q, 1), :, :].rearrange("p a b r -> p (a b r)")))

                def hot(h, r):
                    return vec.tensor_scalar(S[:, h, r, :], iota_lo[:, :], estage[:, h, r:r + 1], None, ALU.is_equal)

                copy_stage(0, 0)
                v.sem_inc(spread_ready, 1)
                with steps.loop(NB // 2, 2 * 9) as i:
                    for h in range(2):
                        v.wait_ge(spread_ready, i * 2 + (h + 1))
                        steps.mark(*[vec.tensor_scalar(Hm[:, r, :], iota_hi[:, :], estage[:, h, BC + r:BC + r + 1], None, ALU.is_equal) for r in range(BC)])
                        v.wait_ge(acc_done, i * 2 + (h + 1))
                        hot(h, 0)
                        steps.catch()
                        v.wait_ge(ad_done, i * 2 + (h + 1))
                        Hm4 = Hm[:, :, :].rearrange("p r (t f) -> p r t f", f=VAL)[:, :, :, 0:HEADS]
                        ad4 = PS[:, 4 + h, 0:BC * NHI * HEADS].rearrange("p (r t f) -> p r t f", r=BC, f=HEADS)
                        steps.mark(vec.tensor_tensor(sel[:, :, :, :].rearrange("p r f t -> p r t f"), ad4, Hm4, ALU.mult))
                        hot(h, 1)
                        steps.catch()
                        steps.mark(vec.tensor_reduce(adu[:, :, :], sel[:, :, :, :], AX.X, ALU.add))
                        hot(h, 2)
                        steps.catch()
                        v.wait_ge(arows_in[h], lv * ROWS_LEVEL + i * (16 * BC) + 16 * BC)
                        steps.mark(vec.scalar_tensor_tensor(ez[:, :, :], adu[:, :, :], sc[:, 5:6], rows[:, h, :, 0:HEADS], ALU.mult, ALU.add),
                                   vec.scalar_tensor_tensor(er[:, :, :], adu[:, :, :], sc[:, 5:6], Gk[:, :].unsqueeze(1).to_broadcast([P, BC, HEADS]), ALU.mult, ALU.add))
                        hot(h, 3)
                        steps.catch()
                        steps.mark(vec.scalar_tensor_tensor(ez2[:, :, :], ez[:, :, :], 0.2, ez[:, :, :], ALU.mult, ALU.max),
                                   vec.scalar_tensor_tensor(er2[:, :, :], er[:, :, :], 0.2, er[:, :, :], ALU.mult, ALU.max))
                        hot(h, 4)
                        steps.catch()
                        vec.tensor_tensor(ez[:, :, :], ez2[:, :, :], er2[:, :, :], ALU.subtract).then_inc(e_ready, 1)
                        steps.mark(vec.tensor_copy(estage[:, 1 - h, :], lohi[:, ds(i * 2 + (h + 1), 1), :, :].rearrange("p a b r -> p (a b r)")))
                        hot(h, 5)
                        hot(h, 6)
                        steps.catch()
                        v.wait_ge(w_ready, i * 2 + (h + 1))
                        steps.mark(vec.tensor_tensor(val[:, :, :].rearrange("p r (h e) -> p r h e", e=1 + NX), wexp[:, :, :].unsqueeze(3).to_broadcast([P, BC, HEADS, 1 + NX]),
                                                     rows[:, h, :, HEADS:ROWW].rearrange("p r (h e) -> p r h e", e=1 + NX), ALU.mult))
                        hot(h, 7).then_inc(lo_hot_ready, 1)
                        steps.catch()
                        v.sem_inc(rows_used, 1)
                        link(vec.tensor_copy(vh[:, :, 0, :], val[:, :, :]))
                        link(vec.tensor_tensor(vh[:, :, 1, :], val[:, :, :], vh[:, :, 0, :], ALU.subtract))
                        for part in range(2):
                            last = vec.tensor_tensor(M[:, h, :, part * HIV:(part + 1) * HIV].rearrange("p r (t f) -> p r t f", f=VAL),
                                                     vh[:, :, part, :].unsqueeze(2).to_broadcast([P, BC, NHI, VAL]),
                                                     Hm[:, :, :].rearrange("p r (t f) -> p r t f", f=VAL), ALU.mult)
                        last.then_inc(spread_ready, 1)
                link(vec.scalar_tensor_tensor(n4[:, :, :], n1[:, :, :], 0.2, n1[:, :, :], ALU.mult, ALU.max), ops(n2[:, :, :], AD[:, :, :], NTB[:, :, 0:HEADS], ALU.add))
                link(vec.scalar_tensor_tensor(n3[:, :, :], n2[:, :, :], 0.2, n2[:, :, :], ALU.mult, ALU.max))
                link(ops(n2[:, :, :], n3[:, :, :], n4[:, :, :], ALU.subtract))
                link(vec.tensor_copy(n1[:, :, :], n4[:, :, :]))
                v.sem_inc(self_e, 1)
                v.wait_ge(sums_ready, 1)
                link(*[vec.tensor_copy(L[:, :, :].rearrange("p (t j) f -> p j t f", j=NJ)[:, j, :, :], PS[:, j, 0:HIV].rearrange("p (t f) -> p t f", f=VAL)) for j in range(NJ)])
                v.wait_ge(self_w, 1)
                w5 = [P, NTP, HEADS, 1 + NX]
                tmp5 = tmp16[:, :, :].rearrange("p t (h e) -> p t h e", e=1 + NX)
                acc5 = acc[:, :, :].rearrange("p t (h e) -> p t h e", e=1 + NX)
                link(ops(tmp5, n3[:, :, :].unsqueeze(3).to_broadcast(w5), NT5, ALU.mult),
                     vec.tensor_scalar(n4[:, :, :], acc5[:, :, :, 0], 0.0, None, ALU.is_equal))
                link(ops(L[:, :, :], L[:, :, :], tmp16[:, :, :], ALU.add), ops(n2[:, :, :], n1[:, :, :], n4[:, :, :], ALU.mult),
                     vec.tensor_scalar(n3[:, :, :], n4[:, :, :], -1.0, 1.0, ALU.mult, ALU.add))
                link(ops(Rsh[:, :, :], Rsh[:, :, :], n3[:, :, :], ALU.mult))
                link(ops(Rsh[:, :, :], Rsh[:, :, :], n2[:, :, :], ALU.add))
                link(ops(n2[:, :, :], n1[:, :, :], Rsh[:, :, :], ALU.subtract))
                v.sem_inc(mg_ready, 1)
                v.wait_ge(mg_exp, 1)
                link(ops(tmp5, n4[:, :, :].unsqueeze(3).to_broadcast(w5), L[:, :, :].rearrange("p t (h e) -> p t h e", e=1 + NX), ALU.mult),
                     vec.tensor_copy(Gk[:, :], Gk1[:, :]))
                link(ops(acc[:, :, :], acc[:, :, :], tmp16[:, :, :], ALU.add))
                v.sem_inc(level_done, 3)
                v.sem_inc(level_end, 1)
                v.wait_ge(level_go, lv + 1)
                v.sem_inc(dve_go, 1)
            steps = Chain(v, gate_steps)
            link = steps.link
            link(vec.tensor_scalar(esc[:, 8:11], extr[:, 10:13], 1e-20, None, ALU.max))
            link(vec.reciprocal(esc[:, 6:8], esc[:, 8:10]), vec.scalar_tensor_tensor(esc[:, 11:12], esc[:, 8:9], float(D), esc[:, 10:11], ALU.mult, ALU.add),
                 vec.tensor_scalar(esc[:, 2:3], esc[:, 8:9], 1.0 / (FULL * XSCALE), None, ALU.mult))
            link(vec.tensor_scalar(esc[:, 0:2], esc[:, 6:8], FULL, None, ALU.mult), vec.reciprocal(esc[:, 5:6], esc[:, 11:12]),
                 vec.scalar_tensor_tensor(esc[:, 4:5], esc[:, 9:10], 1.0 / (FULL * FULL), esc[:, 11:12], ALU.mult, ALU.mult))
            link(vec.tensor_scalar(esc[:, 3:4], esc[:, 5:6], FULL, None, ALU.mult))
            v.sem_inc(exp_ready, 1)
            acc5 = acc[:, :, :].rearrange("p t (h e) -> p t h e", e=1 + NX)
            A4 = A16[:, :, :].rearrange("p t (h e) -> p t h e", e=NX)
            T1 = [P, NTP, HX]
            link(vec.tensor_scalar(rank[:, :, :], acc5[:, :, :, 0], 1.0 / DEN_SCALE, 1e-16, ALU.mult, ALU.add))
            link(vec.reciprocal(pick[:, :, :], rank[:, :, :]))
            link(vec.tensor_scalar(pick[:, :, :], pick[:, :, :], sc[:, 7:8], None, ALU.mult))
            link(ops(A4, acc5[:, :, :, 1:1 + NX], pick[:, :, :].unsqueeze(3).to_broadcast([P, NTP, HEADS, NX]), ALU.mult))
            link(ops(A16[:, :, :], A16[:, :, :], small[:, 2:3, :].to_broadcast(T1), ALU.add))
            link(vec.tensor_reduce(m1[:, :], A16[:, :, :], AX.X, ALU.add))
            link(vec.tensor_scalar(m1[:, :], m1[:, :], 1.0 / HX, None, ALU.mult))
            link(ops(A16[:, :, :], A16[:, :, :], m1[:, :].unsqueeze(2).to_broadcast(T1), ALU.subtract))
            link(ops(B16[:, :, :], A16[:, :, :], A16[:, :, :], ALU.mult))
            link(vec.tensor_reduce(m2[:, :], B16[:, :, :], AX.X, ALU.add))
            link(vec.tensor_scalar(m2[:, :], m2[:, :], 1.0 / HX, None, ALU.mult))
            v.sem_inc(gate_in, 1)
            v.wait_ge(gate_std_r, 1)
            link(vec.reciprocal(m1[:, :], m3[:, :]))
            link(ops(A16[:, :, :], A16[:, :, :], m1[:, :].unsqueeze(2).to_broadcast(T1), ALU.mult))
            link(ops(A16[:, :, :], A16[:, :, :], small[:, 3:4, :].to_broadcast(T1), ALU.mult))
            link(ops(A16[:, :, :], A16[:, :, :], small[:, 4:5, :].to_broadcast(T1), ALU.add))
            link(vec.tensor_reduce(scr4[:, :, :], A16[:, :, :].rearrange("p t (h e) -> p t e h", e=NX), AX.X, ALU.add))
            link(vec.tensor_scalar(scr4[:, :, :], scr4[:, :, :], 1.0 / HEADS, None, ALU.mult))
            link(vec.memset(rank[:, :, :], 0.0))
            for a in range(NX):
                for c in range(a + 1, NX):
                    link(ops(cmp[:, :], scr4[:, :, a], scr4[:, :, c], ALU.is_ge), ops(m3[:, :], scr4[:, :, a], scr4[:, :, c], ALU.is_lt))
                    link(ops(rank[:, :, c], rank[:, :, c], cmp[:, :], ALU.add), ops(rank[:, :, a], rank[:, :, a], m3[:, :], ALU.add))
            for place, to in ((0.0, s1), (1.0, s2)):
                link(vec.tensor_scalar(pick[:, :, :], rank[:, :, :], place, None, ALU.is_equal))
                link(ops(B16[:, :, 0:NX], pick[:, :, :], scr4[:, :, :], ALU.mult))
                link(vec.tensor_reduce(to[:, :], B16[:, :, 0:NX], AX.X, ALU.add))
            link(ops(cmp[:, :], s2[:, :], s1[:, :], ALU.subtract))
            v.sem_inc(gate_in, 1)
            v.wait_ge(gate_exp, 1)
            link(vec.tensor_scalar(m1[:, :], dexp[:, :], 1.0, None, ALU.add))
            link(vec.reciprocal(m2[:, :], m1[:, :]))
            link(ops(m3[:, :], m2[:, :], dexp[:, :], ALU.mult), vec.tensor_scalar(pick[:, :, :], rank[:, :, :], 0.0, None, ALU.is_equal),
                 vec.tensor_scalar(scr4[:, :, :], rank[:, :, :], 1.0, None, ALU.is_equal))
            link(ops(pick[:, :, :], pick[:, :, :], m2[:, :].unsqueeze(2).to_broadcast([P, NTP, NX]), ALU.mult),
                 ops(scr4[:, :, :], scr4[:, :, :], m3[:, :].unsqueeze(2).to_broadcast([P, NTP, NX]), ALU.mult))
            link(ops(gate[:, :].rearrange("p (t e) -> p t e", e=NX), pick[:, 0:NT, :], scr4[:, 0:NT, :], ALU.add))
            link(vec.tensor_scalar(gates[:, :], gate[:, :], esc[:, 4:5], None, ALU.mult))
            v.wait_ge(b1_turned, 1)
            link(vec.tensor_copy(b1T[:, :], PS[:, 7, 0:NE_X * HID // P]))
            for n, c in enumerate(CHUNKS):
                v.wait_ge(w_split, n + 1)
                hi, lo, st, a = w_chunk(c)
                last = vec.scalar_tensor_tensor(lo, st, esc[:, a:a + 1], hi, ALU.mult, ALU.subtract)
                if n == 1:
                    link(last)
                    v.sem_inc(exp_ready, 1)
            link(last)
            v.sem_inc(exp_ready, 1)
            v.sem_inc(o_used, 2)
            v.sem_inc(hid_ready, 4)

            def low_parts(e, base, w):
                for c in range(HID // P):
                    v.wait_ge(hi_hid, base * 16 + (e * 4 + c + 1))
                    vec.scalar_tensor_tensor(hh[:, e % 2, 1, c, 0:w], hh32[:, c, 0:w], esc[:, 3:4], hh[:, e % 2, 0, c, 0:w],
                                             ALU.mult, ALU.subtract).then_inc(hid_ready, 1)

            def gated(e, base, tile0, nt):
                ats = [X3[:, ds(tile0 + t, 1), :].rearrange("p a d -> p (a d)") for t in range(nt)]
                for t in range(nt):
                    last = vec.scalar_tensor_tensor(ats[t], b2_bc[:, e * D:(e + 1) * D], gate[:, ds((tile0 + t) * NX + e, 1)], ats[t], ALU.mult, ALU.add)
                last.then_inc(bias_added, 1)
                v.wait_ge(bias_added, base * 4 + (e + 1))
                v.wait_ge(o_mm, base * 4 + (e + 3))
                for t in range(nt):
                    last = vec.scalar_tensor_tensor(ats[t], PS[:, 4 + 2 * (e % 2) + t // 2, (t % 2) * D:(t % 2 + 1) * D],
                                                    gates[:, ds((tile0 + t) * NX + e, 1)], ats[t], ALU.mult, ALU.add)
                last.then_inc(o_used, 1)
                v.wait_ge(o_used, base * 4 + (e + 3))

            def add_experts(base, tile0, nt):
                low_parts(0, base, nt * P)
                for e in range(1, NE_X):
                    low_parts(e, base, nt * P)
                    gated(e - 1, base, tile0, nt)
                gated(NE_X - 1, base, tile0, nt)

            with v.Fori(0, NT // NJ) as i:
                add_experts(i, i * NJ, NJ)
            add_experts(NT // NJ, (NT // NJ) * NJ, 1)


_INS = ['x', 'src', 'dst', 'L0_gnn_W', 'L0_gnn_b', 'L0_ffn_W_gat', 'L0_ffn_att_src', 'L0_ffn_att_dst', 'L0_ffn_b_gat',
        'L0_ffn_ln_gamma', 'L0_ffn_ln_beta', 'L0_ffn_W1', 'L0_ffn_b1', 'L0_ffn_W2', 'L0_ffn_b2', 'L0_ffn_edge_index']
_OUTS = [((6250, 256), 'float32')]


def kernel(**inputs):
    import numpy as _np
    import concourse.bacc as _bacc
    from concourse import mybir as _mybir
    from concourse.bass_utils import run_bass_kernel_spmd as _run

    nc = _bacc.Bacc("TRN2", target_bir_lowering=False, num_devices=1)
    arrays, args = {}, []
    for name in _INS:
        a = _np.ascontiguousarray(inputs[name])
        arrays[f"in_{name}_dram"] = a
        args.append(nc.dram_tensor(f"in_{name}_dram", a.shape, _mybir.dt.from_np(a.dtype), kind="ExternalInput").ap())
    for i, (shape, dtype) in enumerate(_OUTS):
        dt = _mybir.dt.from_np(_np.dtype(dtype))
        args.append(nc.dram_tensor(f"out_{i}_dram", shape, dt, kind="ExternalOutput").ap())
    gnn_moe(nc, *args)
    r = _run(nc, [arrays], core_ids=[0])
    got = tuple(r.results[0][f"out_{i}_dram"] for i in range(len(_OUTS)))
    return got[0]
```
